# Optimizing a Trainium2 kernel written in Bass

```python
import numpy as np
import jax
import jax.numpy as jnp

def _softmax(x, axis=-1):
    return jax.nn.softmax(x, axis=axis)

def _gelu(x):
    return jax.nn.gelu(x, approximate=True)

def _silu(x):
    return jax.nn.silu(x)

def _sigmoid(x):
    return jax.nn.sigmoid(x)

def _layernorm(x, axis=-1, eps=1e-05):
    m = jnp.mean(x, axis=axis, keepdims=True)
    v = jnp.var(x, axis=axis, keepdims=True)
    return (x - m) / jnp.sqrt(v + eps)

def _scatter_add(tgt, idx, src, axis=0):
    return tgt.at[idx].add(src)

def _segment_sum(src, seg, n):
    return jax.ops.segment_sum(src, seg, n)
kernel_name = 'mk_decoder_postln_d1_seqx_r8_be0e35'

def setup_inputs(seed: int=0):
    np.random.seed(seed)
    _w = jnp.asarray

    def _rec_inputs():
        import jax
        import jax.numpy as jnp
        _rk = jax.random.key(seed)
        x = -0.0002928 + 1 * jax.random.normal(jax.random.fold_in(_rk, 1), (16, 256, 128), jnp.float32)
        _lenS = 256 - jax.random.randint(jax.random.fold_in(_rk, 7), (16,), 0, max(1, 256 // 4) + 1, jnp.int32)
        _lenS2 = 64 - jax.random.randint(jax.random.fold_in(_rk, 8), (16,), 0, max(1, 64 // 4) + 1, jnp.int32)
        _ctx_512P = jax.random.normal(jax.random.fold_in(_rk, 11), (16, 16, 64), jnp.float32)
        _ctx_512c = jax.random.dirichlet(jax.random.fold_in(_rk, 511), 0.3 * jnp.ones((16,), jnp.float32), (16, 64))
        _ctx_512t = jnp.einsum('bsk,bkd->bsd', _ctx_512c, _ctx_512P)
        _ctx_512t = _ctx_512t * jax.lax.rsqrt(jnp.mean(jnp.square(_ctx_512t)) + 1e-12) * 0.953939
        ctx_512 = 0.00222621 + 0.99962 * (_ctx_512t + 0.3 * jax.random.normal(jax.random.fold_in(_rk, 611), (16, 64, 64), jnp.float32))
        return (x, ctx_512)
    x, ctx_512 = _rec_inputs()

    def _L0_attn_setup():
        import jax, jax.numpy as jnp
        import numpy as np
        EMB = 128
        HEADS = 16
        HEAD_DIM = EMB // HEADS
        B, S = (2, 256)
        key = jax.random.key(seed)
        k1, k2, k3 = jax.random.split(key, 3)
        scale = 0.02
        return {'x': jax.random.normal(k1, (B, S, EMB), dtype=jnp.float32), 'W_qkv': jax.random.normal(k2, (3 * EMB, EMB), dtype=jnp.float32) * scale, 'b_qkv': jnp.zeros((3 * EMB,), dtype=jnp.float32), 'W_out': jax.random.normal(k3, (EMB, EMB), dtype=jnp.float32) * scale, 'b_out': jnp.zeros((EMB,), dtype=jnp.float32)}
    _L0_attn_all = _L0_attn_setup()
    _L0_attn_in = {k: v for k, v in _L0_attn_all.items() if k in ('W_qkv', 'b_qkv', 'W_out', 'b_out')}
    del _L0_attn_all

    def _L0_xattn_setup():
        import jax, jax.numpy as jnp
        import numpy as np
        B, T, TC, C, CC, H = (2, 256, 64, 128, 64, 16)
        D = C // H

        def _heads(t):
            b, l, _ = t.shape
            return t.reshape(b, l, H, D).transpose(0, 2, 1, 3)
        key = jax.random.key(seed)
        ks = jax.random.split(key, 18)
        w = lambda k, i, o: jax.random.normal(k, (i, o), jnp.float32) / np.sqrt(i).astype(np.float32)
        return {'x': jax.random.normal(ks[0], (B, T, C), jnp.float32), 'cross_input': jax.random.normal(ks[1], (B, TC, CC), jnp.float32), 'Wk': w(ks[2], C, C), 'bk': jnp.zeros((C,), jnp.float32), 'Wq': w(ks[3], C, C), 'bq': jnp.zeros((C,), jnp.float32), 'Wv': w(ks[4], C, C), 'bv': jnp.zeros((C,), jnp.float32), 'Wck': w(ks[5], CC, C), 'bck': jnp.zeros((C,), jnp.float32), 'Wcq': w(ks[6], C, C), 'bcq': jnp.zeros((C,), jnp.float32), 'Wcv': w(ks[7], CC, C), 'bcv': jnp.zeros((C,), jnp.float32), 'Wp': w(ks[8], C, C), 'bp': jnp.zeros((C,), jnp.float32)}
    _L0_xattn_all = _L0_xattn_setup()
    _L0_xattn_in = {k: v for k, v in _L0_xattn_all.items() if k in ('Wk', 'bk', 'Wq', 'bq', 'Wv', 'bv', 'Wck', 'bck', 'Wcq', 'bcq', 'Wcv', 'bcv', 'Wp', 'bp')}
    del _L0_xattn_all

    def _L0_ffn_setup():
        import jax, jax.numpy as jnp
        import numpy as np
        TOP_K = 2
        key = jax.random.key(seed)
        k1, k2, k3, k4 = jax.random.split(key, 4)
        B, S, H, F, E = (2, 256, 128, 352, 8)
        hidden_states = jax.random.normal(k1, (B, S, H), dtype=jnp.float32)
        wqkv = jax.random.normal(k2, (3 * E, H), dtype=jnp.float32) * 0.02
        w1 = jax.random.normal(k3, (E, 2 * F, H), dtype=jnp.float32) * 0.02
        w2 = jax.random.normal(k4, (E, H, F), dtype=jnp.float32) * 0.02
        return {'hidden_states': hidden_states, 'wqkv': wqkv, 'w1': w1, 'w2': w2}
    _L0_ffn_all = _L0_ffn_setup()
    _L0_ffn_in = {k: v for k, v in _L0_ffn_all.items() if k in ('wqkv', 'w1', 'w2')}
    del _L0_ffn_all
    return {'x': x, 'ctx_512': ctx_512, 'L0_attn_W_qkv': _L0_attn_in['W_qkv'], 'L0_attn_b_qkv': _L0_attn_in['b_qkv'], 'L0_attn_W_out': _L0_attn_in['W_out'], 'L0_attn_b_out': _L0_attn_in['b_out'], 'L0_xattn_Wk': _L0_xattn_in['Wk'], 'L0_xattn_bk': _L0_xattn_in['bk'], 'L0_xattn_Wq': _L0_xattn_in['Wq'], 'L0_xattn_bq': _L0_xattn_in['bq'], 'L0_xattn_Wv': _L0_xattn_in['Wv'], 'L0_xattn_bv': _L0_xattn_in['bv'], 'L0_xattn_Wck': _L0_xattn_in['Wck'], 'L0_xattn_bck': _L0_xattn_in['bck'], 'L0_xattn_Wcq': _L0_xattn_in['Wcq'], 'L0_xattn_bcq': _L0_xattn_in['bcq'], 'L0_xattn_Wcv': _L0_xattn_in['Wcv'], 'L0_xattn_bcv': _L0_xattn_in['bcv'], 'L0_xattn_Wp': _L0_xattn_in['Wp'], 'L0_xattn_bp': _L0_xattn_in['bp'], 'L0_ffn_wqkv': _L0_ffn_in['wqkv'], 'L0_ffn_w1': _L0_ffn_in['w1'], 'L0_ffn_w2': _L0_ffn_in['w2']}

def reference(x, ctx_512, L0_attn_W_qkv, L0_attn_b_qkv, L0_attn_W_out, L0_attn_b_out, L0_xattn_Wk, L0_xattn_bk, L0_xattn_Wq, L0_xattn_bq, L0_xattn_Wv, L0_xattn_bv, L0_xattn_Wck, L0_xattn_bck, L0_xattn_Wcq, L0_xattn_bcq, L0_xattn_Wcv, L0_xattn_bcv, L0_xattn_Wp, L0_xattn_bp, L0_ffn_wqkv, L0_ffn_w1, L0_ffn_w2):
    import jax
    import jax.numpy as jnp

    def _L0_attn_ref(x, W_qkv, b_qkv, W_out, b_out):
        import jax, jax.numpy as jnp
        import numpy as np
        EMB = 128
        HEADS = 16
        HEAD_DIM = EMB // HEADS
        B, S = (2, 256)
        b = x.shape[0]
        qkv = jnp.einsum('bse,fe->bsf', x, W_qkv) + b_qkv
        qkv = qkv.reshape(b, HEADS, -1, 3 * HEAD_DIM)
        q, k, v = jnp.split(qkv, 3, axis=-1)
        score = jnp.einsum('bhqd,bhkd->bhqk', q, k) / np.sqrt(HEAD_DIM).astype(np.float32)
        weights = jax.nn.softmax(score, axis=-1)
        context = jnp.einsum('bhqk,bhkd->bhqd', weights, v)
        context = jnp.transpose(context, (0, 2, 1, 3)).reshape(b, -1, EMB)
        out = jnp.einsum('bse,fe->bsf', context, W_out) + b_out
        return out

    def _L0_xattn_ref(x, cross_input, Wk, bk, Wq, bq, Wv, bv, Wck, bck, Wcq, bcq, Wcv, bcv, Wp, bp):
        import jax, jax.numpy as jnp
        import numpy as np
        B, T, TC, C, CC, H = (2, 256, 64, 128, 64, 16)
        D = C // H

        def _heads(t):
            b, l, _ = t.shape
            return t.reshape(b, l, H, D).transpose(0, 2, 1, 3)
        scale = np.float32(1.0 / np.sqrt(D))
        q = _heads(x @ Wq + bq)
        k = _heads(x @ Wk + bk)
        v = _heads(x @ Wv + bv)
        att = jnp.einsum('bhqd,bhkd->bhqk', q, k) * scale
        causal = jnp.tril(jnp.ones((T, T), bool))
        att = jnp.where(causal[None, None], att, -jnp.inf)
        y = jnp.einsum('bhqk,bhkd->bhqd', jax.nn.softmax(att, axis=-1), v)
        qc = _heads(x @ Wcq + bcq)
        kc = _heads(cross_input @ Wck + bck)
        vc = _heads(cross_input @ Wcv + bcv)
        attc = jnp.einsum('bhqd,bhkd->bhqk', qc, kc) * scale
        y = y + jnp.einsum('bhqk,bhkd->bhqd', jax.nn.softmax(attc, axis=-1), vc)
        y = y.transpose(0, 2, 1, 3).reshape(x.shape[0], T, C)
        return y @ Wp + bp

    def _L0_ffn_ref(hidden_states, wqkv, w1, w2):
        import jax, jax.numpy as jnp
        import numpy as np
        TOP_K = 2
        b, s, h = hidden_states.shape
        E = w1.shape[0]
        mixed = hidden_states @ wqkv.T
        q, k, v = jnp.split(mixed, 3, axis=-1)
        q = q.astype(jnp.float32)
        k = k.astype(jnp.float32)
        v = v.astype(jnp.float32)
        attn = jax.nn.softmax(q[..., :, None] * k[..., None, :], axis=-1)
        logits = jnp.einsum('bsej,bsj->bse', attn, v).reshape(-1, E)
        top_logits, idx = jax.lax.top_k(logits, TOP_K)
        scores = jax.nn.softmax(top_logits.astype(jnp.float32), axis=-1).astype(hidden_states.dtype)
        N = b * s
        x = hidden_states.reshape(N, h)
        token_ids = jnp.repeat(jnp.arange(N), TOP_K)
        expert_ids = idx.reshape(-1)
        x_rep = x[token_ids]
        out = jnp.zeros_like(x_rep)
        for e in range(E):
            h1 = x_rep @ w1[e].T
            a, g = jnp.split(h1, 2, axis=-1)
            he = jax.nn.silu(a) * g @ w2[e].T
            out = out + jnp.where((expert_ids == e)[:, None], he, jnp.zeros((), out.dtype))
        out = out * scores.reshape(-1, 1)
        combined = out.reshape(N, TOP_K, h).sum(axis=1)
        return combined.reshape(b, s, h)
    x = _layernorm(x + _L0_attn_ref(x, L0_attn_W_qkv, L0_attn_b_qkv, L0_attn_W_out, L0_attn_b_out), axis=-1)
    x = _layernorm(x + _L0_xattn_ref(x, ctx_512, L0_xattn_Wk, L0_xattn_bk, L0_xattn_Wq, L0_xattn_bq, L0_xattn_Wv, L0_xattn_bv, L0_xattn_Wck, L0_xattn_bck, L0_xattn_Wcq, L0_xattn_bcq, L0_xattn_Wcv, L0_xattn_bcv, L0_xattn_Wp, L0_xattn_bp), axis=-1)
    x = _layernorm(x + _L0_ffn_ref(x, L0_ffn_wqkv, L0_ffn_w1, L0_ffn_w2), axis=-1)
    return x

_drawn_inputs = setup_inputs


def setup_inputs(seed=0):
    import zlib

    import numpy as np

    out = dict(_drawn_inputs(seed))
    spreads = {'L0_attn_b_qkv': (0.0, 0.8),
     'L0_attn_b_out': (0.0, 0.1),
     'L0_xattn_bk': (0.0, 0.8),
     'L0_xattn_bq': (0.0, 0.476),
     'L0_xattn_bv': (0.0, 0.1),
     'L0_xattn_bck': (0.0, 0.8),
     'L0_xattn_bcq': (0.0, 0.378),
     'L0_xattn_bcv': (0.0, 0.1),
     'L0_xattn_bp': (0.0, 0.1)}
    factors = {'L0_attn_W_qkv': 8.0,
     'L0_attn_W_out': 8.0,
     'L0_ffn_wqkv': 8.0,
     'L0_ffn_w1': 8.0,
     'L0_ffn_w2': 8.0}
    for name, (base, spread) in spreads.items():
        noise = np.random.default_rng([zlib.crc32(name.encode()), seed]).standard_normal(out[name].shape)
        drawn = base * np.exp(spread * noise) if base else spread * noise
        out[name] = jnp.asarray(drawn.astype(out[name].dtype))
    for name, factor in factors.items():
        out[name] = (out[name] * factor).astype(out[name].dtype)
    return out
```

```python
from contextlib import ExitStack
import numpy as np
import concourse.bass as bass
from concourse import mybir

F32, BF16 = mybir.dt.float32, mybir.dt.bfloat16
ALU = mybir.AluOpType
ACT = mybir.ActivationFunctionType
AX = mybir.AxisListType



def decoder_layer(nc, x, ctx_in, aW, ab, aWo, abo, W, bias, rwqkv, w1, w2, out):
    B, T, C = x.shape
    H, D = 16, C // 16
    NT = T // 128
    SCALE = float(1.0 / np.sqrt(np.float32(D)))
    EPS = 1e-5
    KS, MROW = 96, 96
    NBUF = 3

    es = ExitStack()
    with es:
        def sb(name, shape, dt=F32):
            return es.enter_context(nc.sbuf_tensor(name, shape, dt))

        def sem(name):
            return es.enter_context(nc.semaphore(name))

        X = sb("X", [128, B * NT, C])
        ident = sb("ident", [128, 128])
        half = sb("half", [128, NT])
        WnatA = sb("WnatA", [128, 4, 128])
        WTA = sb("WTA", [128, 512])
        bqkA = sb("bqkA", [128, 2])
        bvA = sb("bvA", [128, C])
        boA = sb("boA", [128, C])
        Qs = [sb(f"Qs{i}", [128, H * T], BF16) for i in range(NBUF)]
        Ks = [sb(f"Ks{i}", [128, H * T], BF16) for i in range(NBUF)]
        Vp = [sb(f"Vp{i}", [128, 2, H, 32]) for i in range(NBUF)]
        xin = [sb(f"xin{i}", [128, NT, C]) for i in range(3)]
        xT = sb("xT", [128, T])
        qk32 = sb("qk32", [128, 2, T])
        res = sb("res", [128, 2, T])
        parts = sb("parts", [128, 6, T], BF16)
        vsb = sb("vsb", [128, NT, C])
        M = sb("M", [128, NT, H])
        Mb = sb("Mb", [128, 2, NT * H], BF16)
        WqkA = sb("WqkA", [128, 2, C])
        P = [sb(f"P{i}", [128, 2, 2, T]) for i in range(5)]
        TK = ctx_in.shape[1]
        CK = ctx_in.shape[2]
        Qcs = [sb(f"Qcs{i}", [128, H * T], BF16) for i in range(NBUF)]
        Kcs = [sb(f"Kcs{i}", [128, H * TK], BF16) for i in range(NBUF)]
        VCp = [sb(f"VCp{i}", [128, H // 2, 32]) for i in range(NBUF)]
        identb = sb("identb", [128, 128], BF16)
        maskq = sb("maskq", [128, 128], BF16)
        maskk = sb("maskk", [128, 128], BF16)
        Wx = sb("Wx", [128, 5, C])
        Wqkc = sb("Wqkc", [128, 3, C])
        Wckr = sb("Wckr", [CK, 2, C])
        Wckp = sb("Wckp", [CK, C])
        bx3 = sb("bx3", [128, 4])
        bvx = sb("bvx", [128, C])
        bcvx = sb("bcvx", [128, C])
        bpx = sb("bpx", [128, C])
        x2in = sb("x2in", [128, NT, C])
        qkc32 = sb("qkc32", [128, 3, T])
        res3 = sb("res3", [128, 3, T])
        parts3 = sb("parts3", [128, 9, T], BF16)
        M2 = sb("M2", [128, 4 * H])
        mT = sb("mT", [4 * H, 2, 128], BF16)
        OTx = sb("OTx", [128, 2, T])
        linx = sb("linx", [128, 4, 4, 2])
        ctx2 = sb("ctx2", [128, NT, C])
        cin = P[0][:].rearrange("p a b c -> p (a b c)")[:, 0:512].rearrange("p (n c) -> p n c", n=8)
        cT = P[1][:].rearrange("p a b c -> p (a b c)")[0:CK, :]
        kc32 = P[2][:].rearrange("p a b c -> p (a b c)")
        rc32 = P[3][:].rearrange("p a b c -> p (a b c)")
        vc32 = P[4][:].rearrange("p a b c -> p (a b c)")
        kcp = sb("kcp", [128, 3, B * TK], BF16)
        E_, F2 = w1.shape[0], w1.shape[1]
        FF = F2 // 2
        KF = (128, 128, FF - 256)
        NC = 8
        f32 = lambda t: t[:].bitcast(F32)
        w1r = [f32(Qs[i]).rearrange("p (n e) -> p n e", e=C) for i in range(3)]
        w2r = [f32(Qcs[i])[:, 0:4 * FF].rearrange("p (e f) -> p e f", f=FF) for i in range(2)]
        flatP = [P[i][:].rearrange("p a b c -> p (a b c)") for i in range(5)]
        w1T_t = [f32(Ks[0]), f32(Ks[1]), f32(Ks[2]), f32(Qcs[2])]
        w1T = [w1T_t[e // 2][:, F2 * (e % 2):F2 * (e % 2) + F2] for e in range(8)]
        w2T = [flatP[e // 2][:, 384 * (e % 2):384 * (e % 2) + 384].rearrange("p (k c) -> p k c", k=3) for e in range(8)]
        he = [[Vp[n // 2][:].rearrange("p a b c -> p (a b c)")[:, 512 * (n % 2):512 * (n % 2) + 512] for n in (3 * i, 3 * i + 1, 3 * i + 2)]
              for i in range(2)]
        sa = [flatP[4][:, 512 * i:512 * i + 512] for i in range(2)]
        wrr = sb("wrr", [24, C])
        wrT = sb("wrT", [C, 24])
        x3 = sb("x3", [128, 4, C])
        x3T = sb("x3T", [128, 512])
        mx = sb("mx", [128, 4, 24])
        A = sb("A", [128, 4, 8, 8])
        G = sb("G", [128, 4, 8, 8])
        EQ = sb("EQ", [128, 4, 8, 8])
        LT = sb("LT", [128, 8, 8])
        mr = sb("mr", [128, 4, 8])
        den = sb("den", [128, 4, 8])
        num = sb("num", [128, 4, 8])
        lg = sb("lg", [128, 4, 8])
        dl = sb("dl", [128, 4, 8])
        rank = sb("rank", [128, 4, 8])
        m0 = sb("m0", [128, 4, 1])
        cw = sb("cw", [128, 4, 8])
        acc = sb("acc", [128, 4, C])
        st4 = sb("st4", [128, 4, 6])
        mv4 = sb("mv4", [128, 4, 2])
        ve4 = sb("ve4", [128, 4])
        rs4 = sb("rs4", [128, 4])
        half4 = sb("half4", [128, 4])
        yo = sb("yo", [128, 4, C])
        scr_qkc = nc.dram_tensor("scr_qkc", (9, 128, T), BF16, kind="Internal").ap()
        scr_kc = nc.dram_tensor("scr_kc", (3, B, 128, TK), BF16, kind="Internal").ap()
        scr_vc = nc.dram_tensor("scr_vc", (B * TK, C), F32, kind="Internal").ap()
        OTs = sb("OTs", [128, 2, T])
        linv = sb("linv", [128, 4, 4, 2])
        ctx = sb("ctx", [128, NT, C])
        ctxT = sb("ctxT", [128, T])
        r = sb("r", [128, NT, C])
        xb = sb("xb", [128, NT, C])
        st = sb("st", [128, NT, 6])
        mv = sb("mv", [128, NT, 2])
        ve = sb("ve", [128, NT])
        rstd = sb("rstd", [128, NT])

        scr_qk = nc.dram_tensor("scr_qk", (6, 128, T), BF16, kind="Internal").ap()
        scr_v = nc.dram_tensor("scr_v", (16, T, D), F32, kind="Internal").ap()

        PS = es.enter_context(nc.psum_tensor("PS", [128, 8 * 512], F32))
        Sps = [PS[:, 512 * i:512 * (i + 1)] for i in range(2)]
        STps = [PS[:, 1024 * (i + 1):1024 * (i + 2)] for i in range(2)]
        OTps = PS[:, 512 * 6:512 * 7]
        AUX = PS[:, 512 * 7:512 * 8]

        turns = sem("turns")
        xin_in = sem("xin_in")
        wA_in = sem("wA_in")
        cA_in = sem("cA_in")
        ident_ok = sem("ident_ok")
        zero_ok = sem("zero_ok")
        wTA_ps = sem("wTA_ps")
        wTA_sb = sem("wTA_sb")
        xT_ps = sem("xT_ps")
        xT_sb = sem("xT_sb")
        qk_ps = sem("qk_ps")
        qk_sb = sem("qk_sb")
        v_ps = sem("v_ps")
        v_sb = sem("v_sb")
        split = sem("split")
        parts_out = sem("parts_out")
        v_out = sem("v_out")
        stacks_in = sem("stacks_in")
        v_in = sem("v_in")
        s_ps = sem("s_ps")
        max_sb = sem("max_sb")
        mb_sb = sem("mb_sb")
        m_in = sem("m_in")
        st_ps = sem("st_ps")
        p_sb = sem("p_sb")
        pv_ps = sem("pv_ps")
        ot_sb = sem("ot_sb")
        oT_ps = sem("oT_ps")
        linv_sb = sem("linv_sb")
        ctx_sb = sem("ctx_sb")
        ctxT_ps = sem("ctxT_ps")
        ctxT_sb = sem("ctxT_sb")
        y_ps = sem("y_ps")
        xb_sb = sem("xb_sb")
        r_sb = sem("r_sb")
        st_sb = sem("st_sb")
        mv_sb = sem("mv_sb")
        ve_sb = sem("ve_sb")
        rstd_sb = sem("rstd_sb")
        x1_sb = sem("x1_sb")
        dbg = sem("dbg")
        vp_ok = sem("vp_ok")
        mask_ok = sem("mask_ok")
        wx_in = sem("wx_in")
        cx_in = sem("cx_in")
        cin_in = sem("cin_in")
        wx_sb = sem("wx_sb")
        cT_ps = sem("cT_ps")
        cT_sb = sem("cT_sb")
        kc_ps = sem("kc_ps")
        kc_sb = sem("kc_sb")
        kc_split = sem("kc_split")
        vc_ps = sem("vc_ps")
        vc_sb = sem("vc_sb")
        kc_out = sem("kc_out")
        vc_out = sem("vc_out")
        c_x2in = sem("c_x2in")
        c_xT_ps = sem("c_xT_ps")
        c_xT_sb = sem("c_xT_sb")
        c_qk_ps = sem("c_qk_ps")
        c_qk_sb = sem("c_qk_sb")
        c_qv_ps = sem("c_qv_ps")
        c_qc_sb = sem("c_qc_sb")
        c_v_sb = sem("c_v_sb")
        c_split = sem("c_split")
        c_vp_sb = sem("c_vp_sb")
        c_parts_out = sem("c_parts_out")
        c_stacks_in = sem("c_stacks_in")
        c_s_ps = sem("c_s_ps")
        c_max_sb = sem("c_max_sb")
        c_mT_ps = sem("c_mT_ps")
        c_mT_sb = sem("c_mT_sb")
        c_m_in = sem("c_m_in")
        c_st_ps = sem("c_st_ps")
        c_p_sb = sem("c_p_sb")
        c_pv_ps = sem("c_pv_ps")
        c_ot_sb = sem("c_ot_sb")
        c_oTs_ps = sem("c_oTs_ps")
        c_oTx_ps = sem("c_oTx_ps")
        c_lin_sb = sem("c_lin_sb")
        c_ctx_sb = sem("c_ctx_sb")
        c_ctx2_sb = sem("c_ctx2_sb")
        c_ctxT_ps = sem("c_ctxT_ps")
        c_ctxT_sb = sem("c_ctxT_sb")
        c_y_ps = sem("c_y_ps")
        c_xb_sb = sem("c_xb_sb")
        c_r_sb = sem("c_r_sb")
        c_st_sb = sem("c_st_sb")
        c_mv_sb = sem("c_mv_sb")
        c_ve_sb = sem("c_ve_sb")
        c_rstd_sb = sem("c_rstd_sb")
        x2_sb = sem("x2_sb")
        f_w1_in = sem("f_w1_in")
        f_w2_in = sem("f_w2_in")
        f_wr_in = sem("f_wr_in")
        f_w_ps = sem("f_w_ps")
        f_w_sb = sem("f_w_sb")
        f_lt = sem("f_lt")
        f_x3 = sem("f_x3")
        f_xT_ps = sem("f_xT_ps")
        f_xT_sb = sem("f_xT_sb")
        f_rt_ps = sem("f_rt_ps")
        f_route = sem("f_route")
        f_exp = sem("f_exp")
        f_h_ps = sem("f_h_ps")
        f_sa = sem("f_sa")
        f_he = sem("f_he")
        f_y_ps = sem("f_y_ps")
        f_acc = sem("f_acc")
        f_st = sem("f_st")
        f_mv = sem("f_mv")
        f_ve = sem("f_ve")
        f_rs = sem("f_rs")
        f_yo = sem("f_yo")
        f_out = sem("f_out")
        x_in = [sem(f"x_in{i}") for i in range(4)]
        FFB = [PS[:, 512 * i:512 * i + 512] for i in range(7)]

        def count(value):
            return max(value, 0) if isinstance(value, int) else value

        def settle(eng):
            eng.sem_inc(turns, 1)

        ranges = [("P", 0), ("L", 1), ("SA", 1), ("SB", 2), ("T", 3), ("E", 4)]

        def run(eng, step):
            last = B + 4

            def act(t):
                return {k for k, lag in ranges if 0 <= t - lag < B}
            for t in range(5):
                step(t, t % 3, act(t))
            if eng is not None:
                with eng.Fori(5, B - 4, 3) as it:
                    for u in range(3):
                        step(it + u, (5 + u) % 3, {k for k, _ in ranges})
            for t in range(B - 2, last):
                step(t, t % 3, act(t))

        HA, HB = (0, 8), (8, 16)
        S_SLOTS = {4: ("SA", 0, 2), 5: ("SA", 2, 4), 6: ("SA", 4, 6), 7: ("SA", 6, 8),
                   0: ("SB", 8, 11), 1: ("SB", 11, 14), 2: ("SB", 14, 16)}
        LAG = dict(ranges)

        NR = 20
        block = es.enter_context(nc.Block())

        @block.tensor
        def _(pe):
            pe.wait_ge(ident_ok, 2)
            pe.wait_ge(wA_in, 32)
            for c in range(4):
                i = pe.transpose(AUX[:, 128 * c:128 * c + 128], WnatA[:, c, :], ident[:])
            i.then_inc(wTA_ps, 1)
            pe.wait_ge(wTA_sb, 3)
            WV = WTA[:, 0:384].rearrange("p (j x) -> p j x", x=24)[:, :, 16:24]
            pe.wait_ge(zero_ok, 4 * NBUF)
            pe.wait_ge(cin_in, 16)
            for n in range(8):
                i = pe.transpose(PS[0:CK, 1024 + 128 * n:1152 + 128 * n], cin[:, n, :], ident[:])
            i.then_inc(cT_ps, 1)
            pe.wait_ge(cT_sb, 1)
            pe.wait_ge(wx_sb, 4)
            for n in range(2):
                i = pe.matmul(PS[:, 2048 + 512 * n:2560 + 512 * n], Wckp[:], cT[:, 512 * n:512 * n + 512], start=True, stop=True)
            i.then_inc(kc_ps, 1)
            for n in range(8):
                i = pe.matmul(PS[:, 1024 + 128 * n:1152 + 128 * n], cT[:, 128 * n:128 * n + 128], Wckr[:, 1, :], start=True, stop=True)
            i.then_inc(vc_ps, 1)
            pe.wait_ge(vc_sb, 1)

            def step(t, u, on):
                def S(slot):
                    if slot not in S_SLOTS:
                        return
                    stage, h0, h1 = S_SLOTS[slot]
                    if stage not in on:
                        return
                    b = t - LAG[stage]
                    k = (u - LAG[stage]) % 3
                    if h0 == 0:
                        pe.wait_ge(stacks_in, count(b * 96 + 96))
                    Q4 = Qs[k][0:KS, :].rearrange("p (q h) -> p q h", h=H)
                    K4 = Ks[k][0:KS, :].rearrange("p (q h) -> p q h", h=H)
                    for h in range(h0, h1):
                        pe.wait_ge(max_sb, count(b * 16 + (h - 1)))
                        for q in range(2):
                            i = pe.matmul(Sps[h % 2][:, 256 * q:256 * q + 256], Q4[:, 128 * q:128 * q + 128, h], K4[:, :, h],
                                          start=True, stop=True)
                        i.then_inc(s_ps, 1)

                def ST(slot):
                    if "T" not in on:
                        return
                    b = t - 3
                    k = u % 3
                    if slot == 0:
                        pe.wait_ge(m_in, count(b * 64 + 64))
                    pe.wait_ge(p_sb, count(b * 8 + (slot - 1)))
                    Q4 = Qs[k][0:MROW + 2, :].rearrange("p (q h) -> p q h", h=H)
                    K4 = Ks[k][0:MROW + 2, :].rearrange("p (q h) -> p q h", h=H)
                    for n in range(2):
                        h = slot // 2 + 4 * (2 * (slot % 2) + n)
                        for kt in range(2):
                            o = 512 * n + 256 * kt
                            i = pe.matmul(STps[slot % 2][:, o:o + 256], K4[:, 128 * kt:128 * kt + 128, h], Q4[:, :, h],
                                          start=True, stop=True)
                    i.then_inc(st_ps, 1)

                def PV(g, b, k):
                    pe.wait_ge(p_sb, count(b * 8 + (2 * g + 2)))
                    if g == 0:
                        pe.wait_ge(ot_sb, count(b))
                        pe.wait_ge(v_in, count(b * 64 + 64))
                    hf, gg = g // 2, g % 2
                    for kt in range(2):
                        for c in range(4):
                            h = 4 * c + g
                            i = pe.matmul(OTps[32 * c:32 * c + 32, 256 * hf:256 * hf + 256], Vp[k][:, kt, h, :],
                                          P[(2 * g + c // 2) % 4][:, c % 2, kt, :],
                                          start=(gg == 0 and kt == 0), stop=(gg == 1 and kt == 1))
                    i.then_inc(pv_ps, 1)

                for slot in range(8):
                    if slot == 0 and "P" in on:
                        b = t
                        pe.wait_ge(v_sb, count(t))
                        pe.wait_ge(xin_in, count(t * 16 + 16))
                        pe.wait_ge(r_sb, count(t - 4))
                        for c in range(NT):
                            i = pe.transpose(AUX[:, 128 * c:128 * c + 128], xin[u][:, c, :], ident[:])
                        i.then_inc(xT_ps, 1)
                    if slot == 1 and "P" in on:
                        pe.wait_ge(xT_sb, count(t + 1))
                        for a in range(2):
                            i = pe.matmul(AUX[:, 256 * a:256 * a + 256], WqkA[:, a, :], xT[:], start=True, stop=True)
                        i.then_inc(qk_ps, 1)
                    if slot == 2 and "P" in on:
                        pe.wait_ge(qk_sb, count(t * 2 + 2))
                        for c in range(2):
                            i = pe.matmul(AUX[:, 128 * c:128 * c + 128], xT[:, 128 * c:128 * c + 128], WV, start=True, stop=True)
                        i.then_inc(v_ps, 1)
                    if slot == 4 and "E" in on:
                        b = t - 4
                        pe.wait_ge(ot_sb, count(b + 1))
                        if "P" in on:
                            pe.wait_ge(v_sb, count(t + 1))
                        else:
                            pe.wait_ge(r_sb, count(t - 4))
                        for c in range(2):
                            for hf in range(2):
                                o = 256 * c + 128 * hf
                                i = pe.transpose(AUX[:, o:o + 128], OTs[:, hf, 128 * c:128 * c + 128], ident[:])
                        i.then_inc(oT_ps, 1)
                    if slot == 5 and "E" in on:
                        pe.wait_ge(ctx_sb, count(t - 3))
                        for c in range(NT):
                            i = pe.transpose(AUX[:, 128 * c:128 * c + 128], ctx[:, c, :], ident[:])
                        i.then_inc(ctxT_ps, 1)
                    if slot == 6 and "E" in on:
                        pe.wait_ge(ctxT_sb, count(t - 3))
                        for c in range(NT):
                            i = pe.matmul(AUX[:, 128 * c:128 * c + 128], ctxT[:, 128 * c:128 * c + 128], WTA[:, 384:512], start=True, stop=True)
                        i.then_inc(y_ps, 1)
                    S(slot)
                    ST(slot)
                    if slot == 0 and "E" in on:
                        PV(3, t - 4, (u - 1) % 3)
                    if slot in (2, 4, 6) and "T" in on:
                        PV(slot // 2 - 1, t - 3, u % 3)
                if isinstance(t, int) and t == 3:
                    pe.wait_ge(v_sb, 4)
            run(pe, step)

            S2_SLOTS = {5: ("SA", 0, 2), 6: ("SA", 2, 4), 7: ("SA", 4, 6), 8: ("SA", 6, 8), 9: ("SA", 8, 10),
                        0: ("SB", 10, 13), 1: ("SB", 13, 16), 2: ("SB", 16, 18), 3: ("SB", 18, 20)}

            def step2(t, u, on):
                def S(slot):
                    if slot not in S2_SLOTS or S2_SLOTS[slot][0] not in on:
                        return
                    stage, n0, n1 = S2_SLOTS[slot]
                    b = t - LAG[stage]
                    k = (u - LAG[stage]) % 3
                    if n0 == 0:
                        pe.wait_ge(c_stacks_in, count(b * 224 + 224))
                    for n in range(n0, n1):
                        pe.wait_ge(c_max_sb, count(b * 20 + (n - 1)))
                        o = Sps[n % 2]
                        if n < 16:
                            q, kk = Qs[k][0:KS, T * n:T * n + T], Ks[k][0:KS, T * n:T * n + T]
                            pe.matmul(o[:, 0:128], q[:, 0:128], kk[:, 0:128], start=True, stop=False)
                            pe.matmul(o[:, 0:128], identb[:], maskq[:], start=False, stop=True)
                            pe.matmul(o[:, 128:384], q[:, 128:256], kk, start=True, stop=False)
                            i = pe.matmul(o[:, 256:384], identb[:], maskq[:], start=False, stop=True)
                        else:
                            for h in range(4 * (n - 16), 4 * (n - 15)):
                                for qt in range(2):
                                    c = (h % 4) * 128 + 64 * qt
                                    i = pe.matmul(o[:, c:c + 64], Qcs[k][0:KS, T * h + 128 * qt:T * h + 128 * qt + 128],
                                                  Kcs[k][0:KS, TK * h:TK * h + TK], start=True, stop=True)
                        i.then_inc(c_s_ps, 1)

                def ST(slot):
                    if "T" not in on:
                        return
                    b = t - 3
                    k = u % 3
                    if slot == 0:
                        pe.wait_ge(c_m_in, count(b * 64 + 64))
                    pe.wait_ge(c_p_sb, count(b * 10 + (slot - 1)))
                    o = STps[slot % 2]
                    if slot < 8:
                        for n in range(2):
                            h = slot // 2 + 4 * (2 * (slot % 2) + n)
                            q, kk = Qs[k][0:MROW + 2, T * h:T * h + T], Ks[k][0:MROW + 2, T * h:T * h + T]
                            c = 512 * n
                            pe.matmul(o[:, c:c + 256], kk[:, 0:128], q, start=True, stop=False)
                            pe.matmul(o[:, c:c + 128], identb[:], maskk[:], start=False, stop=True)
                            pe.matmul(o[:, c + 256:c + 384], kk[:, 128:256], q[:, 128:256], start=True, stop=False)
                            i = pe.matmul(o[:, c + 256:c + 384], identb[:], maskk[:], start=False, stop=True)
                    else:
                        for c in range(4):
                            for n in range(2):
                                h = 4 * c + 2 * (slot - 8) + n
                                i = pe.matmul(o[64 * n:64 * n + 64, 256 * c:256 * c + 256], Kcs[k][0:MROW + 2, TK * h:TK * h + TK],
                                              Qcs[k][0:MROW + 2, T * h:T * h + T], start=True, stop=True)
                    i.then_inc(c_st_ps, 1)

                def PV(g, b, k):
                    pe.wait_ge(c_p_sb, count(b * 10 + (2 * g + 2)))
                    if g == 0:
                        pe.wait_ge(c_ot_sb, count(b * 2))
                        pe.wait_ge(c_vp_sb, count(b * 2 + 2))
                    hf, gg = g // 2, g % 2
                    for kt in range(2):
                        for c in range(4):
                            h = 4 * c + g
                            tile = P[(2 * g + c // 2) % 5][:, c % 2].rearrange("p a b -> p (a b)")
                            i = pe.matmul(OTps[32 * c:32 * c + 32, 256 * hf + 128 * kt:256 * hf + 256], Vp[k][:, kt, h, :],
                                          tile[:, 256 * kt:256 + 128 * kt],
                                          start=(gg == 0 and kt == 0), stop=(gg == 1 and kt == 1))
                    i.then_inc(c_pv_ps, 1)

                def PVX(hf, b, k):
                    pe.wait_ge(c_p_sb, count(b * 10 + 9 + hf))
                    if hf == 0:
                        pe.wait_ge(c_ot_sb, count(b * 2 + 1))
                    tile = P[(8 + hf) % 5][:].rearrange("p a b c -> p (a b c)")
                    for c in range(4):
                        i = pe.matmul(OTps[32 * c:32 * c + 32, 256 * hf:256 * hf + 256], VCp[k][:, 2 * c + hf, :],
                                      tile[:, 256 * c:256 * c + 256], start=True, stop=True)
                    i.then_inc(c_pv_ps, 1)

                for slot in range(10):
                    if slot == 0 and "P" in on:
                        pe.wait_ge(c_v_sb, count(t))
                        pe.wait_ge(c_x2in, count(t + 1))
                        pe.wait_ge(c_r_sb, count(t - 4))
                        for c in range(NT):
                            i = pe.transpose(AUX[:, 128 * c:128 * c + 128], x2in[:, c, :], ident[:])
                        i.then_inc(c_xT_ps, 1)
                    if slot == 1 and "P" in on:
                        pe.wait_ge(c_xT_sb, count(t + 1))
                        for a in range(2):
                            i = pe.matmul(AUX[:, 256 * a:256 * a + 256], Wqkc[:, a, :], xT[:], start=True, stop=True)
                        i.then_inc(c_qk_ps, 1)
                    if slot == 2 and "P" in on:
                        pe.wait_ge(c_qk_sb, count(t * 2 + 2))
                        pe.matmul(AUX[:, 0:256], Wqkc[:, 2, :], xT[:], start=True, stop=True)
                        for c in range(2):
                            i = pe.matmul(AUX[:, 256 + 128 * c:384 + 128 * c], xT[:, 128 * c:128 * c + 128], Wx[:, 3, :], start=True, stop=True)
                        i.then_inc(c_qv_ps, 1)
                    if slot == 4 and "SB" in on:
                        b = t - 2
                        if "P" in on:
                            pe.wait_ge(c_qc_sb, count(t + 1))
                            pe.wait_ge(c_v_sb, count(t + 1))
                        else:
                            pe.wait_ge(c_r_sb, count(t - 4))
                        pe.wait_ge(c_max_sb, count(b * 20 + 20))
                        settle(pe)
                        pe.transpose(AUX[0:4 * H, 0:128], M2[:], ident[:]).then_inc(c_mT_ps, 1)
                    if slot == 5 and "E" in on:
                        if "SB" in on:
                            pe.wait_ge(c_mT_sb, count(t * 2 - 2))
                        else:
                            pe.wait_ge(c_r_sb, count(t - 4))
                        for c in range(2):
                            for hf in range(2):
                                o = 256 * c + 128 * hf
                                i = pe.transpose(AUX[:, o:o + 128], OTs[:, hf, 128 * c:128 * c + 128], ident[:])
                        i.then_inc(c_oTs_ps, 1)
                    if slot == 6 and "E" in on:
                        pe.wait_ge(c_ot_sb, count(t * 2 - 6))
                        pe.wait_ge(c_ctx_sb, count(t - 3))
                        for c in range(2):
                            for hf in range(2):
                                o = 256 * c + 128 * hf
                                i = pe.transpose(AUX[:, o:o + 128], OTx[:, hf, 128 * c:128 * c + 128], ident[:])
                        i.then_inc(c_oTx_ps, 1)
                    if slot == 7 and "E" in on:
                        pe.wait_ge(c_ctx2_sb, count(t * 2 - 6))
                        for c in range(NT):
                            i = pe.transpose(AUX[:, 128 * c:128 * c + 128], ctx[:, c, :], ident[:])
                        i.then_inc(c_ctxT_ps, 1)
                    if slot == 8 and "E" in on:
                        pe.wait_ge(c_ctxT_sb, count(t - 3))
                        for c in range(NT):
                            i = pe.matmul(AUX[:, 128 * c:128 * c + 128], ctxT[:, 128 * c:128 * c + 128], Wx[:, 4, :], start=True, stop=True)
                        i.then_inc(c_y_ps, 1)
                    S(slot)
                    ST(slot)
                    if slot == 0 and "E" in on:
                        PVX(1, t - 4, (u - 1) % 3)
                    if slot in (2, 4, 6, 8) and "T" in on:
                        PV(slot // 2 - 1, t - 3, u % 3)
                    if slot == 9 and "T" in on:
                        PVX(0, t - 3, u % 3)
                if isinstance(t, int) and t == 3:
                    pe.wait_ge(c_mT_sb, 4)
                    pe.wait_ge(c_qc_sb, 4)
                    pe.wait_ge(c_v_sb, 4)
            pe.wait_ge(r_sb, B)
            pe.wait_ge(mask_ok, 6)
            pe.wait_ge(zero_ok, 6 * NBUF)
            run(pe, step2)
            pe.wait_ge(c_r_sb, B)
            pe.wait_ge(f_wr_in, 16)
            pe.transpose(AUX[:, 0:24], wrr[:], ident[0:24, 0:24]).then_inc(f_w_ps, 1)
            pe.wait_ge(f_w1_in, 96 * E_)
            pe.wait_ge(c_ot_sb, 2 * B)
            pe.wait_ge(c_max_sb, 20 * B)
            for e in range(E_):
                for g in range(2):
                    n = 3 * e + g
                    if n >= 2:
                        pe.wait_ge(f_w_sb, count(3 * e + g - 1))
                    for k in range(3):
                        src = 6 * e + 3 * g + k
                        i = pe.transpose(FFB[(3 * e + g) % 4][:, 128 * k:128 * k + KF[k]], w1r[src // 16][0:KF[k], src % 16, :],
                                         ident[0:KF[k], 0:KF[k]])
                    i.then_inc(f_w_ps, 1)
                if e == 0:
                    pe.wait_ge(f_w2_in, 32)
                pe.wait_ge(f_w_sb, count(3 * e + 1))
                for k in range(3):
                    i = pe.transpose(FFB[(3 * e + 2) % 4][0:KF[k], 128 * k:128 * k + 128], w2r[e // 4][:, e % 4, 128 * k:128 * k + KF[k]], ident[:])
                i.then_inc(f_w_ps, 1)
            pe.wait_ge(f_w_sb, 3 * E_ + 1)

            def chunk(c):
                pe.wait_ge(f_x3, count(c + 1))
                pe.wait_ge(f_route, count(c * NR + 0))
                for k in range(4):
                    i = pe.transpose(AUX[:, 128 * k:128 * k + 128], x3[:, k, :], ident[:])
                i.then_inc(f_xT_ps, 1)
                pe.wait_ge(f_xT_sb, count(c + 1))
                for k in range(4):
                    i = pe.matmul(FFB[6][:, 24 * k:24 * k + 24], x3T[:, 128 * k:128 * k + 128], wrT[:], start=True, stop=True)
                i.then_inc(f_rt_ps, 1)
                for e in range(E_ + 1):
                    if e < E_:
                        for k in range(3):
                            n = 3 * e + k
                            pe.wait_ge(f_he, count(c * 24 + max(n - 1, 0)))
                            for g in range(2):
                                i = pe.matmul(FFB[2 * g + n % 2][0:KF[k], :], w1T[e][:, FF * g + 128 * k:FF * g + 128 * k + KF[k]], x3T[:],
                                              start=True, stop=True)
                            i.then_inc(f_h_ps, 1)
                    if e > 0:
                        pe.wait_ge(f_he, count(c * 24 + 3 * e))
                        pe.wait_ge(f_acc, count(c * 8 + max(e - 2, 0)))
                        for t in range(4):
                            for k in range(3):
                                i = pe.matmul(FFB[4 + (e - 1) % 2][:, 128 * t:128 * t + 128], he[(e - 1) % 2][k][0:KF[k], 128 * t:128 * t + 128],
                                              w2T[e - 1][0:KF[k], k, :], start=(k == 0), stop=(k == 2))
                        i.then_inc(f_y_ps, 1)
            chunk(0)
            with pe.Fori(1, NC, 1) as c:
                chunk(c)

        @block.scalar
        def _(act):
            def step(t, u, on):
                for slot in range(8):
                    if slot == 1 and "P" in on:
                        act.wait_ge(qk_ps, count(t + 1))
                        act.wait_ge(split, count(t * 4))
                        for a in range(2):
                            act.activation(qk32[:, a, :], AUX[:, 256 * a:256 * a + 256], ACT.Identity, bias=bqkA[:, a:a + 1]).then_inc(qk_sb, 1)
                    if slot == 5 and "E" in on:
                        act.wait_ge(ctxT_ps, count(t - 3))
                        act.wait_ge(y_ps, count(t - 4))
                        act.activation(ctxT[:], AUX[:, 0:256], ACT.Copy).then_inc(ctxT_sb, 1)
                    if "T" in on:
                        b = t - 3
                        act.wait_ge(st_ps, count(b * 8 + (slot + 1)))
                        act.wait_ge(pv_ps, count(b * 4 + (slot // 2 - 1)))
                        act.activation(P[slot % 4][:].rearrange("p a b c -> p (a b c)"), STps[slot % 2], ACT.Exp, scale=SCALE).then_inc(p_sb, 1)
                    if slot == 0 and "E" in on:
                        act.wait_ge(pv_ps, count(t * 4 - 12))
                        act.wait_ge(oT_ps, count(t - 4))
                        act.activation(OTs[:].rearrange("p f (i j) -> p f j i", j=16), OTps.rearrange("p (f j i) -> p f j i", f=2, i=16), ACT.Copy).then_inc(ot_sb, 1)
            act.wait_ge(cA_in, 64)
            run(act, step)

            def step2(t, u, on):
                for slot in range(10):
                    if slot == 1 and "P" in on:
                        act.wait_ge(c_qk_ps, count(t + 1))
                        act.wait_ge(c_split, count(t * 4))
                        for a in range(2):
                            act.activation(qkc32[:, a, :], AUX[:, 256 * a:256 * a + 256], ACT.Identity, bias=bx3[:, a:a + 1]).then_inc(c_qk_sb, 1)
                    if slot == 2 and "P" in on:
                        act.wait_ge(c_qv_ps, count(t + 1))
                        act.activation(qkc32[:, 2, :], AUX[:, 0:256], ACT.Identity, bias=bx3[:, 2:3]).then_inc(c_qc_sb, 1)
                    if slot == 7 and "E" in on:
                        act.wait_ge(c_ctxT_ps, count(t - 3))
                        act.wait_ge(c_y_ps, count(t - 4))
                        act.activation(ctxT[:], AUX[:, 0:256], ACT.Copy).then_inc(c_ctxT_sb, 1)
                    if "T" in on:
                        b = t - 3
                        act.wait_ge(c_st_ps, count(b * 10 + (slot + 1)))
                        if slot < 5:
                            if not (isinstance(b, int) and b == 0):
                                act.wait_ge(c_pv_ps, count(b * 6 - 6 + (3, 4, 4, 5, 6)[slot]))
                        else:
                            act.wait_ge(c_pv_ps, count(b * 6 + ((slot - 5) // 2 + 1)))
                        src, dst = STps[slot % 2], P[slot % 5][:].rearrange("p a b c -> p (a b c)")
                        if slot < 8:
                            src = src.rearrange("p (n k) -> p n k", n=2)[:, :, 0:384]
                            dst = dst.rearrange("p (n k) -> p n k", n=2)[:, :, 0:384]
                        act.activation(dst, src, ACT.Exp, scale=SCALE).then_inc(c_p_sb, 1)
                    if slot == 8 and "T" in on:
                        b = t - 3
                        act.wait_ge(c_pv_ps, count(b * 6 + 4))
                        act.wait_ge(c_oTs_ps, count(b))
                        act.activation(OTs[:].rearrange("p a b -> p (a b)"), OTps, ACT.Copy).then_inc(c_ot_sb, 1)
                    if slot == 0 and "E" in on:
                        b = t - 4
                        act.wait_ge(c_pv_ps, count(b * 6 + 6))
                        act.wait_ge(c_oTx_ps, count(b))
                        act.activation(OTx[:].rearrange("p a b -> p (a b)"), OTps, ACT.Copy).then_inc(c_ot_sb, 1)
            act.wait_ge(cx_in, 144)
            run(act, step2)
            def chunk(c):
                act.wait_ge(f_route, count(c * NR + 4))
                act.activation(A[:], A[:], ACT.Exp).then_inc(f_exp, 1)
                act.wait_ge(f_route, count(c * NR + 16))
                act.activation(dl[:], dl[:], ACT.Exp).then_inc(f_exp, 1)
                for n in range(24):
                    act.wait_ge(f_h_ps, count(c * 24 + (n + 1)))
                    act.wait_ge(f_he, count(c * 24 + max(n - 1, 0)))
                    act.activation(sa[n % 2][0:KF[n % 3], :], FFB[n % 2][0:KF[n % 3], :], ACT.Silu).then_inc(f_sa, 1)
            chunk(0)
            with act.Fori(1, NC, 1) as c:
                chunk(c)

        @block.vector
        def _(dve):
            dve.wait_ge(wTA_ps, 1)
            dve.tensor_copy(WTA[:], AUX).then_inc(wTA_sb, 1)
            for a in range(2):
                dve.tensor_copy(WqkA[:, a, :].rearrange("p (d j) -> p d j", j=16),
                                AUX[:, 0:384].rearrange("p (j x) -> p x j", x=24)[:, 8 * a:8 * a + 8, :]).then_inc(wTA_sb, 1)
            for k in range(NBUF):
                dve.memset(Qs[k][0:96, :].bitcast(F32), 0.0).then_inc(zero_ok, 1)
                dve.memset(Ks[k][64:96, :].bitcast(F32), 0.0).then_inc(zero_ok, 1)
                dve.memset(Ks[k][32:64, :], 1.0).then_inc(zero_ok, 1)
                dve.memset(Ks[k][96:98, :], 1.0).then_inc(zero_ok, 1)
            for k in range(NBUF):
                dve.memset(Qcs[k][0:96, :].bitcast(F32), 0.0).then_inc(zero_ok, 1)
                dve.memset(Kcs[k][96:98, :], 1.0).then_inc(zero_ok, 1)
            dve.wait_ge(vp_ok, 2 * NBUF)
            for k in range(NBUF):
                dve.memset(VCp[k][0:64, :, 16:17], 1.0).then_inc(vp_ok, 1)
                dve.memset(VCp[k][64:128, :, 17:18], 1.0).then_inc(vp_ok, 1)
            dve.wait_ge(wx_in, 80)
            for a in range(3):
                dve.tensor_copy(Wqkc[:, a, :].rearrange("p (d h) -> p d h", d=D), Wx[:, a, :].rearrange("p (h d) -> p d h", d=D)).then_inc(wx_sb, 1)
            dve.wait_ge(cx_in, 144)
            dve.tensor_copy(Wckp[:].rearrange("p (d h) -> p d h", d=D), Wckr[:, 0, :].rearrange("p (h d) -> p d h", d=D)).then_inc(wx_sb, 1)
            dve.wait_ge(cT_ps, 1)
            dve.tensor_copy(cT, PS[0:CK, 1024:2048]).then_inc(cT_sb, 1)
            dve.wait_ge(kc_ps, 1)
            dve.tensor_scalar(kc32, PS[:, 2048:3072], bx3[:, 3:4], None, ALU.add).then_inc(kc_split, 1)
            dve.wait_ge(kc_split, 1)
            kv = kcp[:]
            dve.tensor_copy(kv[:, 0, :], kc32).then_inc(kc_split, 1)
            dve.wait_ge(kc_split, 2)
            dve.tensor_tensor(rc32, kc32, kv[:, 0, :], ALU.subtract).then_inc(kc_split, 1)
            dve.wait_ge(kc_split, 3)
            dve.tensor_copy(kv[:, 1, :], rc32).then_inc(kc_split, 1)
            dve.wait_ge(kc_split, 4)
            dve.tensor_tensor(kv[:, 2, :], rc32, kv[:, 1, :], ALU.subtract).then_inc(kc_split, 1)
            dve.wait_ge(vc_ps, 1)
            dve.tensor_tensor(vc32.rearrange("p (n c) -> p n c", c=C), PS[:, 1024:2048].rearrange("p (n c) -> p n c", c=C),
                              bcvx[:].unsqueeze(1).to_broadcast((128, 8, C)), ALU.add).then_inc(vc_sb, 1)
            dve.wait_ge(cA_in, 64)

            def step(t, u, on):
                for slot in range(8):
                    if slot == 0 and "P" in on:
                        dve.wait_ge(xT_ps, count(t + 1))
                        dve.wait_ge(v_ps, count(t))
                        dve.tensor_copy(xT[:].rearrange("p (i h) -> p h i", h=H), AUX[:, 0:256].rearrange("p (h i) -> p h i", i=16)).then_inc(xT_sb, 1)
                    if slot == 2 and "P" in on:
                        dve.wait_ge(v_ps, count(t + 1))
                        dve.wait_ge(v_out, count(t * 32))
                        dve.tensor_tensor(vsb[:], AUX[:, 0:256].rearrange("p (c f) -> p c f", c=2),
                                          bvA[:].unsqueeze(1).to_broadcast((128, 2, C)), ALU.add).then_inc(v_sb, 1)
                    if slot == 3 and "SB" in on:
                        b = t - 2
                        dve.wait_ge(m_in, count(b * 64))
                        dve.wait_ge(max_sb, count(b * 16 + 16))
                        dve.tensor_scalar(Mb[:, 0, :], M[:].rearrange("p q h -> p (q h)"), -1.0, None, ALU.mult).then_inc(mb_sb, 1)
                        dve.wait_ge(mb_sb, count(b * 2 + 1))
                        dve.scalar_tensor_tensor(out=Mb[:, 1, :], in0=M[:].rearrange("p q h -> p (q h)"), scalar=-1.0, in1=Mb[:, 0, :],
                                                 op0=ALU.mult, op1=ALU.subtract).then_inc(mb_sb, 1)
                    if slot == 4 and "E" in on:
                        b = t - 4
                        dve.wait_ge(oT_ps, count(b + 1))
                        o5 = AUX.rearrange("p (t c x) -> p t c x", t=4, c=4)
                        dve.wait_ge(ctx_sb, count(b))
                        dve.reciprocal(linv[:], o5[:, :, :, 16:18]).then_inc(linv_sb, 1)
                        dve.wait_ge(linv_sb, count(b + 1))
                        dve.wait_ge(ctxT_ps, count(b))
                        for c in range(2):
                            for hf in range(2):
                                th = 2 * c + hf
                                i = dve.tensor_tensor(ctx[:, c, :].rearrange("p (q f g d) -> p q f g d", q=4, f=2, g=2)[:, :, hf],
                                                      o5[:, th, :, 0:16].rearrange("p q (g d) -> p q g d", g=2),
                                                      linv[:, th, :, :].unsqueeze(3).to_broadcast((128, 4, 2, D)), ALU.mult)
                        i.then_inc(ctx_sb, 1)
                    if slot == 6 and "E" in on:
                        b = t - 4
                        dve.wait_ge(y_ps, count(b + 1))
                        dve.wait_ge(xb_sb, count(b + 1))
                        dve.wait_ge(x1_sb, count(b * 2))
                        dve.tensor_tensor(r[:], AUX[:, 0:256].rearrange("p (c f) -> p c f", c=2), xb[:], ALU.add).then_inc(r_sb, 1)
                        dve.wait_ge(r_sb, count(b + 1))
                        dve.wait_ge(mv_sb, count(b * 2))
                        for c in range(2):
                            dve.bn_stats(st[:, c, :], r[:, c, :]).then_inc(st_sb, 1)
                        dve.wait_ge(st_sb, count(b * 2 + 2))
                        settle(dve)
                        for c in range(2):
                            dve.bn_aggr(mv[:, c, :], st[:, c, :]).then_inc(mv_sb, 1)
                    if slot == 7 and "E" in on:
                        b = t - 4
                        dve.wait_ge(rstd_sb, count(b + 1))
                        for c in range(2):
                            dve.tensor_scalar(X[:, b * 2 + c, :], r[:, c, :], mv[:, c, 0:1], rstd[:, c:c + 1],
                                              ALU.subtract, ALU.mult).then_inc(x1_sb, 1)
                    if slot in S_SLOTS and S_SLOTS[slot][0] in on:
                        stage, h0, h1 = S_SLOTS[slot]
                        b = t - LAG[stage]
                        if h0 == 0:
                            dve.wait_ge(mb_sb, count(b * 2))
                        for h in range(h0, h1):
                            dve.wait_ge(s_ps, count(b * 16 + (h + 1)))
                            dve.tensor_reduce(out=M[:, :, h], in_=Sps[h % 2].rearrange("p (q k) -> p q k", q=2), op=ALU.max,
                                              axis=AX.X).then_inc(max_sb, 1)
            run(dve, step)

            S2_SLOTS = {5: ("SA", 0, 2), 6: ("SA", 2, 4), 7: ("SA", 4, 6), 8: ("SA", 6, 8), 9: ("SA", 8, 10),
                        0: ("SB", 10, 13), 1: ("SB", 13, 16), 2: ("SB", 16, 18), 3: ("SB", 18, 20)}

            def step2(t, u, on):
                def normalise(lin, dst):
                    o5 = AUX.rearrange("p (t c x) -> p t c x", t=4, c=4)
                    for c in range(2):
                        for hf in range(2):
                            th = 2 * c + hf
                            i = dve.tensor_tensor(dst[:, c, :].rearrange("p (q f g d) -> p q f g d", q=4, f=2, g=2)[:, :, hf],
                                                  o5[:, th, :, 0:16].rearrange("p q (g d) -> p q g d", g=2),
                                                  lin[:, th, :, :].unsqueeze(3).to_broadcast((128, 4, 2, D)), ALU.mult)
                    return i
                for slot in range(10):
                    if slot == 0 and "P" in on:
                        dve.wait_ge(c_xT_ps, count(t + 1))
                        dve.wait_ge(c_qv_ps, count(t))
                        dve.tensor_copy(xT[:], AUX[:, 0:256]).then_inc(c_xT_sb, 1)
                    if slot == 2 and "P" in on:
                        dve.wait_ge(c_qv_ps, count(t + 1))
                        dve.wait_ge(c_vp_sb, count(t * 2))
                        dve.wait_ge(c_qc_sb, count(t + 1))
                        dve.tensor_tensor(vsb[:], AUX[:, 256:512].rearrange("p (c f) -> p c f", c=2),
                                          bvx[:].unsqueeze(1).to_broadcast((128, 2, C)), ALU.add).then_inc(c_v_sb, 1)
                    if slot == 4 and "SB" in on:
                        b = t - 2
                        dve.wait_ge(c_mT_ps, count(b + 1))
                        dve.wait_ge(c_m_in, count(b * 64))
                        dve.tensor_scalar(mT[:, 0, :], AUX[0:4 * H, 0:128], -1.0, None, ALU.mult).then_inc(c_mT_sb, 1)
                        dve.wait_ge(c_mT_sb, count(b * 2 + 1))
                        dve.scalar_tensor_tensor(out=mT[:, 1, :], in0=AUX[0:4 * H, 0:128], scalar=-1.0, in1=mT[:, 0, :],
                                                 op0=ALU.mult, op1=ALU.subtract).then_inc(c_mT_sb, 1)
                    if slot == 5 and "E" in on:
                        b = t - 4
                        dve.wait_ge(c_oTs_ps, count(b + 1))
                        dve.reciprocal(linv[:], AUX.rearrange("p (t c x) -> p t c x", t=4, c=4)[:, :, :, 16:18]).then_inc(c_lin_sb, 1)
                        dve.wait_ge(c_lin_sb, count(b * 2 + 1))
                        dve.wait_ge(c_ctxT_ps, count(b))
                        normalise(linv, ctx).then_inc(c_ctx_sb, 1)
                    if slot == 6 and "E" in on:
                        b = t - 4
                        dve.wait_ge(c_oTx_ps, count(b + 1))
                        dve.reciprocal(linx[:], AUX.rearrange("p (t c x) -> p t c x", t=4, c=4)[:, :, :, 16:18]).then_inc(c_lin_sb, 1)
                        dve.wait_ge(c_lin_sb, count(b * 2 + 2))
                        normalise(linx, ctx2).then_inc(c_ctx2_sb, 1)
                        dve.wait_ge(c_ctx2_sb, count(b * 2 + 1))
                        dve.tensor_tensor(ctx[:], ctx[:], ctx2[:], ALU.add).then_inc(c_ctx2_sb, 1)
                    if slot == 8 and "E" in on:
                        b = t - 4
                        dve.wait_ge(c_y_ps, count(b + 1))
                        dve.wait_ge(c_xb_sb, count(b + 1))
                        dve.wait_ge(x2_sb, count(b * 2))
                        dve.tensor_tensor(r[:], AUX[:, 0:256].rearrange("p (c f) -> p c f", c=2), xb[:], ALU.add).then_inc(c_r_sb, 1)
                        dve.wait_ge(c_r_sb, count(b + 1))
                        dve.wait_ge(c_mv_sb, count(b * 2))
                        for c in range(2):
                            dve.bn_stats(st[:, c, :], r[:, c, :]).then_inc(c_st_sb, 1)
                        dve.wait_ge(c_st_sb, count(b * 2 + 2))
                        settle(dve)
                        for c in range(2):
                            dve.bn_aggr(mv[:, c, :], st[:, c, :]).then_inc(c_mv_sb, 1)
                    if slot == 9 and "E" in on:
                        b = t - 4
                        dve.wait_ge(c_rstd_sb, count(b + 1))
                        for c in range(2):
                            dve.tensor_scalar(X[:, b * 2 + c, :], r[:, c, :], mv[:, c, 0:1], rstd[:, c:c + 1],
                                              ALU.subtract, ALU.mult).then_inc(x2_sb, 1)
                    if slot in S2_SLOTS and S2_SLOTS[slot][0] in on:
                        stage, n0, n1 = S2_SLOTS[slot]
                        b = t - LAG[stage]
                        if n0 == 0:
                            dve.wait_ge(c_mT_ps, count(b))
                        for n in range(n0, n1):
                            dve.wait_ge(c_s_ps, count(b * 20 + (n + 1)))
                            if n < 16:
                                dve.tensor_reduce(out=M2[:, 2 * n:2 * n + 1], in_=Sps[n % 2][:, 0:128], op=ALU.max, axis=AX.X)
                                i = dve.tensor_reduce(out=M2[:, 2 * n + 1:2 * n + 2], in_=Sps[n % 2][:, 128:384], op=ALU.max, axis=AX.X)
                            else:
                                c = 32 + 8 * (n - 16)
                                i = dve.tensor_reduce(out=M2[:, c:c + 8], in_=Sps[n % 2].rearrange("p (g k) -> p g k", k=TK), op=ALU.max, axis=AX.X)
                            i.then_inc(c_max_sb, 1)
            run(dve, step2)
            dve.wait_ge(f_w_ps, 1)
            dve.tensor_copy(wrT[:], AUX[:, 0:24]).then_inc(f_w_sb, 1)
            for e in range(E_):
                for g in range(2):
                    dve.wait_ge(f_w_ps, count(3 * e + g + 2))
                    dve.tensor_copy(w1T[e][:, FF * g:FF * g + FF], FFB[(3 * e + g) % 4][:, 0:FF]).then_inc(f_w_sb, 1)
                dve.wait_ge(f_w_ps, count(3 * e + 4))
                dve.tensor_copy(w2T[e][:, 0:2, :].rearrange("p k c -> p (k c)"), FFB[(3 * e + 2) % 4][:, 0:256])
                dve.tensor_copy(w2T[e][0:KF[2], 2, :], FFB[(3 * e + 2) % 4][0:KF[2], 256:384]).then_inc(f_w_sb, 1)

            dve.wait_ge(f_lt, 3)
            def chunk(c):
                def link(k, ins):
                    ins.then_inc(f_route, 1)
                    dve.wait_ge(f_route, count(c * NR + k))
                bj = lambda t: t.unsqueeze(2).to_broadcast((128, 4, 8, 8))
                be = lambda t: t.unsqueeze(3).to_broadcast((128, 4, 8, 8))
                dve.wait_ge(f_acc, count(c * 8))
                dve.wait_ge(f_rt_ps, count(c))
                dve.tensor_copy(x3[:], X[:, 0:4, :] if isinstance(c, int) else X[:, bass.ds(c * 4, 4), :]).then_inc(f_x3, 1)
                dve.wait_ge(f_xT_ps, count(c + 1))
                dve.tensor_copy(x3T[:], AUX).then_inc(f_xT_sb, 1)
                dve.wait_ge(f_rt_ps, count(c + 1))
                link(1, dve.tensor_copy(mx[:].rearrange("p a b -> p (a b)"), FFB[6][:, 0:96]))
                link(2, dve.tensor_tensor(A[:], be(mx[:, :, 0:8]), bj(mx[:, :, 8:16]), ALU.mult))
                link(3, dve.tensor_reduce(out=mr[:], in_=A[:], op=ALU.max, axis=AX.X))
                link(4, dve.tensor_tensor(A[:], A[:], be(mr[:]), ALU.subtract))
                dve.wait_ge(f_exp, count(c * 2 + 1))
                link(5, dve.tensor_reduce(out=den[:], in_=A[:], op=ALU.add, axis=AX.X))
                link(6, dve.tensor_tensor(A[:], A[:], bj(mx[:, :, 16:24]), ALU.mult))
                link(7, dve.tensor_reduce(out=num[:], in_=A[:], op=ALU.add, axis=AX.X))
                link(8, dve.reciprocal(den[:], den[:]))
                link(9, dve.tensor_tensor(lg[:], num[:], den[:], ALU.mult))
                link(10, dve.tensor_tensor(G[:], bj(lg[:]), be(lg[:]), ALU.is_gt))
                link(11, dve.tensor_tensor(EQ[:], bj(lg[:]), be(lg[:]), ALU.is_equal))
                link(12, dve.tensor_tensor(EQ[:], EQ[:], LT[:].unsqueeze(1).to_broadcast((128, 4, 8, 8)), ALU.mult))
                link(13, dve.tensor_tensor(G[:], G[:], EQ[:], ALU.add))
                link(14, dve.tensor_reduce(out=rank[:], in_=G[:], op=ALU.add, axis=AX.X))
                link(15, dve.tensor_reduce(out=m0[:, :, 0], in_=lg[:], op=ALU.max, axis=AX.X))
                link(16, dve.tensor_tensor(dl[:], lg[:], m0[:].to_broadcast((128, 4, 8)), ALU.subtract))
                dve.wait_ge(f_exp, count(c * 2 + 2))
                link(17, dve.scalar_tensor_tensor(out=cw[:], in0=rank[:], scalar=1.5, in1=dl[:], op0=ALU.is_lt, op1=ALU.mult))
                link(18, dve.tensor_reduce(out=m0[:, :, 0], in_=cw[:], op=ALU.add, axis=AX.X))
                link(19, dve.reciprocal(m0[:], m0[:]))
                link(20, dve.tensor_tensor(cw[:], cw[:], m0[:].to_broadcast((128, 4, 8)), ALU.mult))
                for e in range(E_ + 1):
                    if e < E_:
                        for k in range(3):
                            n = 3 * e + k
                            dve.wait_ge(f_sa, count(c * 24 + (n + 1)))
                            if k == 0:
                                dve.wait_ge(f_y_ps, count(c * 8 + max(e - 1, 0)))
                            dve.tensor_tensor(he[e % 2][k][0:KF[k], :], sa[n % 2][0:KF[k], :], FFB[2 + n % 2][0:KF[k], :], ALU.mult).then_inc(f_he, 1)
                    if e > 0:
                        dve.wait_ge(f_y_ps, count(c * 8 + e))
                        dve.wait_ge(f_acc, count(c * 8 + max(e - 1, 0)))
                        if e == 1:
                            dve.wait_ge(f_yo, count(c * 4))
                        for t in range(4):
                            yb = FFB[4 + (e - 1) % 2][:, 128 * t:128 * t + 128]
                            i = dve.scalar_tensor_tensor(out=acc[:, t, :], in0=yb, scalar=cw[:, t, e - 1:e],
                                                         in1=(x3 if e == 1 else acc)[:, t, :], op0=ALU.mult, op1=ALU.add)
                        i.then_inc(f_acc, 1)
                dve.wait_ge(f_acc, count(c * 8 + 8))
                for t in range(4):
                    dve.bn_stats(st4[:, t, :], acc[:, t, :]).then_inc(f_st, 1)
                dve.wait_ge(f_st, count(c * 4 + 4))
                settle(dve)
                for t in range(4):
                    dve.bn_aggr(mv4[:, t, :], st4[:, t, :]).then_inc(f_mv, 1)
                dve.wait_ge(f_rs, count(c + 1))
                dve.wait_ge(f_out, count(c * 16))
                for t in range(4):
                    dve.tensor_scalar(yo[:, t, :], acc[:, t, :], mv4[:, t, 0:1], rs4[:, t:t + 1], ALU.subtract, ALU.mult).then_inc(f_yo, 1)
            chunk(0)
            with dve.Fori(1, NC, 1) as c:
                chunk(c)

        @block.gpsimd
        def _(pool):
            pool.memset(ident[:], 0.0).then_inc(ident_ok, 1)
            pool.wait_ge(ident_ok, 1)
            pool.affine_select(out=ident[:], in_=ident[:], compare_op=ALU.not_equal, fill=1.0, base=0, pattern=[[-1, 128]],
                               channel_multiplier=1).then_inc(ident_ok, 1)
            pool.wait_ge(ident_ok, 2)
            pool.memset(maskq[:], 0.0).then_inc(mask_ok, 1)
            pool.memset(maskk[:], 0.0).then_inc(mask_ok, 1)
            pool.wait_ge(mask_ok, 2)
            for m, sign in ((maskq, 1), (maskk, -1)):
                pool.affine_select(out=m[:], in_=m[:], compare_op=ALU.is_ge, fill=-1e38, base=0, pattern=[[-sign, 128]],
                                   channel_multiplier=sign).then_inc(mask_ok, 1)
            pool.tensor_copy(identb[:], ident[:]).then_inc(mask_ok, 1)
            pool.memset(half[:], -0.5).then_inc(mask_ok, 1)
            pool.wait_ge(cA_in, 64)
            for i in range(4):
                pool.wait_ge(x_in[i], 16)

            def step(t, u, on):
                if "E" in on:
                    b = t - 4
                    pool.wait_ge(r_sb, count(b))
                    pool.tensor_tensor(xb[:], X[:, bass.ds(b * 2, 2), :] if not isinstance(b, int) else X[:, 2 * b:2 * b + 2, :],
                                       boA[:].unsqueeze(1).to_broadcast((128, 2, C)), ALU.add).then_inc(xb_sb, 1)
                if "P" in on:
                    pool.wait_ge(qk_sb, count(t * 2 + 2))
                    pool.wait_ge(parts_out, count(t * 16))
                    settle(pool)
                    pool.tensor_copy(parts[:, 0:6:3, :], qk32[:]).then_inc(split, 1)
                    pool.wait_ge(split, count(t * 4 + 1))
                    pool.tensor_tensor(res[:], qk32[:], parts[:, 0:6:3, :], ALU.subtract).then_inc(split, 1)
                    pool.wait_ge(split, count(t * 4 + 2))
                    settle(pool)
                    pool.tensor_copy(parts[:, 1:6:3, :], res[:]).then_inc(split, 1)
                    pool.wait_ge(split, count(t * 4 + 3))
                    pool.tensor_tensor(parts[:, 2:6:3, :], res[:], parts[:, 1:6:3, :], ALU.subtract).then_inc(split, 1)
                if "E" in on:
                    b = t - 4
                    pool.wait_ge(mv_sb, count(b * 2 + 2))
                    pool.wait_ge(rstd_sb, count(b))
                    settle(pool)
                    pool.tensor_scalar(ve[:], mv[:, :, 1], EPS, None, ALU.add).then_inc(ve_sb, 1)
                    pool.wait_ge(ve_sb, count(b + 1))
                    pool.wait_ge(x1_sb, count(b * 2))
                    pool.tensor_tensor(rstd[:], ve[:], half[:], ALU.pow).then_inc(rstd_sb, 1)
            for k in range(NBUF):
                pool.memset(Vp[k][:], 0.0).then_inc(vp_ok, 1)
                pool.memset(VCp[k][:], 0.0).then_inc(vp_ok, 1)
            pool.wait_ge(vp_ok, 2 * NBUF)
            for k in range(NBUF):
                v = Vp[k][:].rearrange("p t (m g) x -> p (t m) g x", g=2)
                for g in range(2):
                    pool.memset(v[:, :, g, 16 + g:17 + g], 1.0).then_inc(vp_ok, 1)
                pool.memset(Kcs[k][0:96, :], 0.0).then_inc(vp_ok, 1)
            run(pool, step)

            def step2(t, u, on):
                if "P" in on:
                    pool.wait_ge(x1_sb, count(t * 2 + 2)) if isinstance(t, int) else None
                    pool.wait_ge(c_xT_ps, count(t))
                    settle(pool)
                    src = X[:, 2 * t:2 * t + 2, :] if isinstance(t, int) else X[:, bass.ds(t * 2, 2), :]
                    pool.tensor_copy(x2in[:], src).then_inc(c_x2in, 1)
                if "E" in on:
                    b = t - 4
                    pool.wait_ge(c_r_sb, count(b))
                    pool.tensor_tensor(xb[:], X[:, bass.ds(b * 2, 2), :] if not isinstance(b, int) else X[:, 2 * b:2 * b + 2, :],
                                       bpx[:].unsqueeze(1).to_broadcast((128, 2, C)), ALU.add).then_inc(c_xb_sb, 1)
                if "L" in on:
                    b = t - 1
                    pool.wait_ge(c_v_sb, count(b + 1))
                    pool.wait_ge(c_pv_ps, count(b * 6 - 12))
                    settle(pool)
                    vd = Vp[(u - 1) % 3][:].rearrange("p t (m g) x -> p (t m) g x", g=2)
                    vs = vsb[:].rearrange("p t (m g d) -> p (t m) g d", g=2, d=D)
                    for g in range(2):
                        pool.tensor_copy(vd[:, :, g, 8 * g:8 * g + 8], vs[:, :, g, :]).then_inc(c_vp_sb, 1)
                if "P" in on:
                    p3 = parts3[:].rearrange("p (g a) t -> p g a t", a=3)
                    pool.wait_ge(c_qk_sb, count(t * 2 + 2))
                    pool.wait_ge(c_qc_sb, count(t + 1))
                    pool.wait_ge(c_parts_out, count(t * 16))
                    settle(pool)
                    pool.tensor_copy(p3[:, :, 0, :], qkc32[:]).then_inc(c_split, 1)
                    pool.wait_ge(c_split, count(t * 4 + 1))
                    pool.tensor_tensor(res3[:], qkc32[:], p3[:, :, 0, :], ALU.subtract).then_inc(c_split, 1)
                    pool.wait_ge(c_split, count(t * 4 + 2))
                    settle(pool)
                    pool.tensor_copy(p3[:, :, 1, :], res3[:]).then_inc(c_split, 1)
                    pool.wait_ge(c_split, count(t * 4 + 3))
                    pool.tensor_tensor(p3[:, :, 2, :], res3[:], p3[:, :, 1, :], ALU.subtract).then_inc(c_split, 1)
                if "E" in on:
                    b = t - 4
                    pool.wait_ge(c_mv_sb, count(b * 2 + 2))
                    pool.wait_ge(c_rstd_sb, count(b))
                    settle(pool)
                    pool.tensor_scalar(ve[:], mv[:, :, 1], EPS, None, ALU.add).then_inc(c_ve_sb, 1)
                    pool.wait_ge(c_ve_sb, count(b + 1))
                    pool.wait_ge(x2_sb, count(b * 2))
                    pool.tensor_tensor(rstd[:], ve[:], half[:], ALU.pow).then_inc(c_rstd_sb, 1)
            pool.wait_ge(x1_sb, 2 * B)
            pool.wait_ge(cx_in, 144)
            pool.wait_ge(v_out, 32 * B)
            run(pool, step2)
            pool.memset(half4[:], -0.5).then_inc(f_lt, 1)
            pool.memset(LT[:], 1.0).then_inc(f_lt, 1)
            pool.wait_ge(f_lt, 2)
            pool.affine_select(out=LT[:], in_=LT[:], compare_op=ALU.is_ge, fill=0.0, base=-1, pattern=[[1, 8], [-1, 8]],
                               channel_multiplier=0).then_inc(f_lt, 1)
            pool.wait_ge(f_lt, 3)
            def chunk(c):
                pool.wait_ge(f_mv, count(c * 4 + 4))
                settle(pool)
                pool.tensor_scalar(ve4[:], mv4[:, :, 1], EPS, None, ALU.add).then_inc(f_ve, 1)
                pool.wait_ge(f_ve, count(c + 1))
                pool.wait_ge(f_yo, count(c * 4))
                pool.tensor_tensor(rs4[:], ve4[:], half4[:], ALU.pow).then_inc(f_rs, 1)
            chunk(0)
            with pool.Fori(1, NC, 1) as c:
                chunk(c)

        @block.sync
        def _(sp):
            xv = x.rearrange("b (c p) f -> p (b c) f", p=128)
            sp.dma_start(WnatA[:, 0:3, :], aW.rearrange("(c p) e -> p c e", p=128)).then_inc(wA_in, 16)
            sp.dma_start(WnatA[:, 3, :], aWo).then_inc(wA_in, 16)
            for i in range(4):
                n = B * NT // 4
                sp.dma_start(X[:, n * i:n * i + n, :], xv[:, n * i:n * i + n, :]).then_inc(x_in[i], 16)
            bx = ab.rearrange("(j x) -> x j", x=24)
            for a in range(2):
                sp.dma_start(bqkA[:, a:a + 1], bx[8 * a:8 * a + 8, :], allow_slow_non_contiguous=True).then_inc(cA_in, 16)
            sp.dma_start(bvA[:].rearrange("p (j d) -> p j d", d=8), ab.rearrange("(j x) -> j x", x=24)[:, 16:24].unsqueeze(0).to_broadcast((128, 16, 8))).then_inc(cA_in, 16)
            sp.dma_start(boA[:], abo.unsqueeze(0).to_broadcast((128, C))).then_inc(cA_in, 16)
            for n, name in enumerate(("Wq", "Wk", "Wcq", "Wv", "Wp")):
                sp.dma_start(Wx[:, n, :], W[name]).then_inc(wx_in, 16)
            sp.dma_start(cin, ctx_in.rearrange("(n u) t c -> (u t) n c", u=2)).then_inc(cin_in, 16)
            sp.dma_start(Wckr[:, 0, :], W["Wck"]).then_inc(cx_in, 16)
            sp.dma_start(Wckr[:, 1, :], W["Wcv"]).then_inc(cx_in, 16)
            for n, name in enumerate(("bq", "bk", "bcq", "bck")):
                sp.dma_start(bx3[:, n:n + 1], W[name].rearrange("(h d) -> d h", d=D), allow_slow_non_contiguous=True).then_inc(cx_in, 16)
            for tile, name in ((bvx, "bv"), (bcvx, "bcv"), (bpx, "bp")):
                sp.dma_start(tile[:], W[name].unsqueeze(0).to_broadcast((128, C))).then_inc(cx_in, 16)
            sp.wait_ge(kc_split, 5)
            for a in range(3):
                sp.dma_start(scr_kc[a].rearrange("b p t -> p b t"), kcp[:, a, :].rearrange("p (b t) -> p b t", t=TK)).then_inc(kc_out, 16)
            sp.wait_ge(vc_sb, 1)
            sp.dma_start(scr_vc.rearrange("(n p) c -> p n c", p=128), vc32.rearrange("p (n c) -> p n c", c=C)).then_inc(vc_out, 16)
            sp.wait_ge(zero_ok, 6 * NBUF)
            sp.wait_ge(vp_ok, 5 * NBUF + 2 * NBUF)
            sp.wait_ge(ident_ok, 2)
            rows = scr_qk.rearrange("a (d j) t -> (a d) (j t)", d=8)

            def step(t, u, on):
                if "P" in on:
                    sp.wait_ge(xT_ps, count(t - 2))
                    settle(sp)
                    sp.wait_ge(xin_in, count(t * 16))
                    settle(sp)
                    settle(sp)
                    sp.dma_start(xin[u][:], (x[t] if isinstance(t, int) else x[bass.ds(t, 1)].rearrange("o n f -> (o n) f")).rearrange("(c p) f -> p c f", p=128)).then_inc(xin_in, 16)
                if "L" in on:
                    b = t - 1
                    k = (u - 1) % 3
                    sp.wait_ge(parts_out, count(b * 16 + 16))
                    settle(sp)
                    sp.wait_ge(v_out, count(b * 32 + 32))
                    settle(sp)
                    sp.wait_ge(stacks_in, count(b * 96))
                    settle(sp)
                    sp.wait_ge(v_in, count(b * 64))
                    settle(sp)
                    sp.wait_ge(st_ps, count(b * 8 - 16))
                    settle(sp)
                    for n, o in ((3, 0), (2, 24), (1, 40)):
                        sp.dma_start(Qs[k][o:o + 8 * n, :], rows[0:8 * n, :]).then_inc(stacks_in, 16)
                        a = (3 - n) * 8 + 24
                        sp.dma_start(Ks[k][o:o + 8 * n, :], rows[a:a + 8, :].unsqueeze(0).to_broadcast((n, 8, H * T))).then_inc(stacks_in, 16)
                    sp.wait_ge(pv_ps, count(b * 4 - 8))
                    settle(sp)
                    vr = scr_v.rearrange("(kt j) (i m g) d -> kt g (j i) m d", kt=2, i=16, g=2)
                    for kt in range(2):
                        for g in range(2):
                            dst = Vp[k][:, kt, :, :].rearrange("p (m g) x -> p m g x", g=2)[:, :, g, 8 * g:8 * g + 8]
                            sp.dma_start(dst, vr[kt, g]).then_inc(v_in, 16)
                if "P" in on:
                    sp.wait_ge(v_sb, count(t + 1))
                    settle(sp)
                    sp.wait_ge(v_in, count(t * 64))
                    settle(sp)
                    for c in range(2):
                        sp.dma_start(scr_v[:, 128 * c:128 * c + 128, :].rearrange("j p d -> p j d"),
                                     vsb[:, c, :].rearrange("p (j d) -> p j d", d=8)).then_inc(v_out, 16)
                if "SB" in on:
                    b = t - 2
                    k = (u - 2) % 3
                    sp.wait_ge(mb_sb, count(b * 2 + 2))
                    settle(sp)
                    sp.wait_ge(m_in, count(b * 64))
                    settle(sp)
                    for c in range(2):
                        for f in range(2):
                            sp.dma_start(Qs[k][MROW + c:MROW + c + 1, 2048 * f:2048 * f + 2048].rearrange("o (q h) -> o q h", h=H),
                                         Mb[:, c, 16 * f:16 * f + 16]).then_inc(m_in, 16)
                if "P" in on:
                    sp.wait_ge(split, count(t * 4 + 4))
                    settle(sp)
                    sp.wait_ge(stacks_in, count(t * 96))
                    settle(sp)
                    sp.dma_start(scr_qk.rearrange("a p t -> p a t"), parts[:]).then_inc(parts_out, 16)
            run(sp, step)
            sp.wait_ge(kc_out, 48)
            sp.wait_ge(vc_out, 16)
            rows2 = scr_qkc.rearrange("a (d h) t -> (a d) (h t)", d=D)

            def step2(t, u, on):
                if "L" in on:
                    b = t - 1
                    k = (u - 1) % 3
                    sp.wait_ge(c_parts_out, count(b * 16 + 16))
                    settle(sp)
                    sp.wait_ge(c_stacks_in, count(b * 224))
                    settle(sp)
                    sp.wait_ge(c_st_ps, count(b * 10 - 20))
                    settle(sp)
                    for n, o in ((3, 0), (2, 24), (1, 40)):
                        sp.dma_start(Qs[k][o:o + 8 * n, :], rows2[0:8 * n, :]).then_inc(c_stacks_in, 16)
                        sp.dma_start(Qcs[k][o:o + 8 * n, :], rows2[48:48 + 8 * n, :]).then_inc(c_stacks_in, 16)
                        a = (3 - n) * 8 + 24
                        sp.dma_start(Ks[k][o:o + 8 * n, :], rows2[a:a + 8, :].unsqueeze(0).to_broadcast((n, 8, H * T))).then_inc(c_stacks_in, 16)
                        kb = (scr_kc[3 - n][b] if isinstance(b, int) else scr_kc[3 - n][bass.ds(b, 1)].rearrange("o p t -> (o p) t")).rearrange("(d h) t -> d (h t)", d=D)
                        sp.dma_start(Kcs[k][o:o + 8 * n, :], kb.unsqueeze(0).to_broadcast((n, 8, H * TK))).then_inc(c_stacks_in, 16)
                    sp.wait_ge(c_pv_ps, count(b * 6 - 12))
                    settle(sp)
                    vb = scr_vc[bass.ds(b * TK, TK)] if not isinstance(b, int) else scr_vc[b * TK:b * TK + TK]
                    vb = vb.rearrange("t (m g d) -> g t m d", g=2, d=D)
                    for g in range(2):
                        sp.dma_start(VCp[k][64 * g:64 * g + 64, :, 8 * g:8 * g + 8], vb[g]).then_inc(c_stacks_in, 16)
                if "SB" in on:
                    b = t - 2
                    k = (u - 2) % 3
                    sp.wait_ge(c_mT_sb, count(b * 2 + 2))
                    settle(sp)
                    sp.wait_ge(c_m_in, count(b * 64))
                    settle(sp)
                    for c in range(2):
                        for stack, o in ((Qs, 0), (Qcs, 2 * H)):
                            sp.dma_start(stack[k][MROW + c:MROW + c + 1, :].rearrange("o (r q) -> o r q", q=128),
                                         mT[o:o + 2 * H, c, :]).then_inc(c_m_in, 16)
                if "P" in on:
                    sp.wait_ge(c_split, count(t * 4 + 4))
                    settle(sp)
                    sp.wait_ge(c_stacks_in, count(t * 224))
                    settle(sp)
                    sp.dma_start(scr_qkc.rearrange("a p t -> p a t"), parts3[:]).then_inc(c_parts_out, 16)
            sp.wait_ge(st_ps, 8 * B)
            sp.wait_ge(pv_ps, 4 * B)
            run(sp, step2)
            sp.dma_start(wrr[:], rwqkv).then_inc(f_wr_in, 16)
            sp.wait_ge(c_st_ps, 10 * B)
            for e in range(E_):
                for g in range(2):
                    for k in range(3):
                        src = 6 * e + 3 * g + k
                        r0 = FF * g + 128 * k
                        sp.dma_start(w1r[src // 16][0:KF[k], src % 16, :], w1[e, r0:r0 + KF[k], :]).then_inc(f_w1_in, 16)
            for i in range(2):
                sp.dma_start(w2r[i], w2[4 * i:4 * i + 4].rearrange("e c f -> c e f")).then_inc(f_w2_in, 16)
            outv = out.rearrange("b (c p) f -> p (b c) f", p=128)
            def chunk(c):
                sp.wait_ge(f_yo, count(c * 4 + 4))
                settle(sp)
                sp.dma_start(outv[:, 0:4, :] if isinstance(c, int) else outv[:, bass.ds(c * 4, 4), :], yo[:]).then_inc(f_out, 16)
            chunk(0)
            with sp.Fori(1, NC, 1) as c:
                chunk(c)

            sp.wait_ge(f_out, 16 * NC)


def kernel(**inputs):
    import concourse.bacc as bacc
    from concourse.bass_utils import run_bass_kernel_spmd
    nc = bacc.Bacc("TRN2", target_bir_lowering=False, num_devices=1)
    arrays, a = {}, {}
    for name, value in inputs.items():
        arrays[name] = np.ascontiguousarray(value)
        a[name] = nc.dram_tensor(name, arrays[name].shape, mybir.dt.from_np(arrays[name].dtype), kind="ExternalInput").ap()
    out = nc.dram_tensor("out", arrays["x"].shape, F32, kind="ExternalOutput").ap()
    cross = {k.removeprefix("L0_xattn_"): v for k, v in a.items() if k.startswith("L0_xattn_")}
    decoder_layer(nc, a["x"], a["ctx_512"], a["L0_attn_W_qkv"], a["L0_attn_b_qkv"], a["L0_attn_W_out"], a["L0_attn_b_out"],
                  cross, None, a["L0_ffn_wqkv"], a["L0_ffn_w1"], a["L0_ffn_w2"], out)
    return run_bass_kernel_spmd(nc, [arrays], core_ids=[0]).results[0]["out"]
```

```python
from contextlib import ExitStack
import numpy as np
import concourse.bass as bass
from concourse import mybir

F32, BF16, I32, U32 = mybir.dt.float32, mybir.dt.bfloat16, mybir.dt.int32, mybir.dt.uint32
ALU = mybir.AluOpType
ACT = mybir.ActivationFunctionType
AX = mybir.AxisListType


def decoder_layer(nc, x, ctx_in, aW, ab, aWo, abo, W, bias, rwqkv, w1, w2, out):
    B, T, C = x.shape
    H, D = 16, C // 16
    NT = T // 128
    SCALE = float(1.0 / np.sqrt(np.float32(D)))
    EPS = 1e-5
    KS, MROW = 96, 96
    NBUF = 3

    es = ExitStack()
    with es:
        def sb(name, shape, dt=F32):
            return es.enter_context(nc.sbuf_tensor(name, shape, dt))

        def sem(name):
            return es.enter_context(nc.semaphore(name))

        X = sb("X", [128, B * NT, C])
        ident = sb("ident", [128, 128])
        half = sb("half", [128, NT])
        arena1 = sb("arena1", [128, 4160])
        taken = [0]

        def part(arena, cols, dt=F32, size=None):
            a = arena[:, taken[0]:taken[0] + cols]
            taken[0] += cols
            assert taken[0] <= arena.shape[1], (taken[0], arena.shape)
            return a if dt == F32 else a.bitcast(dt)
        WnatA = part(arena1, 512).rearrange("p (a b) -> p a b", b=128)
        WTA = part(arena1, 512)
        bvA = part(arena1, C)
        boA = part(arena1, C)
        WqkA = part(arena1, 2 * C).rearrange("p (a b) -> p a b", b=C)
        xin = [part(arena1, NT * C).rearrange("p (a b) -> p a b", b=C) for i in range(3)]
        qk32 = part(arena1, 2 * T).rearrange("p (a b) -> p a b", b=T)
        res = part(arena1, 2 * T).rearrange("p (a b) -> p a b", b=T)
        parts = part(arena1, 3 * T, BF16).rearrange("p (a b) -> p a b", b=T)
        M = part(arena1, NT * H).rearrange("p (a b) -> p a b", b=H)
        Mb = part(arena1, NT * H, BF16).rearrange("p (a b) -> p a b", b=NT * H)
        bqkA = sb("bqkA", [128, 2])
        stackQ = sb("stackQ", [128, NBUF * H * T], BF16)
        stackK = sb("stackK", [128, NBUF * H * T], BF16)
        Qs = [stackQ[:, H * T * i:H * T * (i + 1)] for i in range(NBUF)]
        Ks = [stackK[:, H * T * i:H * T * (i + 1)] for i in range(NBUF)]
        Vp = [sb(f"Vp{i}", [128, 2, H, 32]) for i in range(NBUF)]
        xT = sb("xT", [128, T])
        vsb = sb("vsb", [128, NT, C])
        arenaP = sb("arenaP", [128, 5 * 4 * T])
        P = [arenaP[:, 4 * T * i:4 * T * (i + 1)].rearrange("p (a b c) -> p a b c", a=2, b=2) for i in range(5)]
        TK = ctx_in.shape[1]
        CK = ctx_in.shape[2]
        stackQc = sb("stackQc", [128, NBUF * H * T], BF16)
        stackKc = sb("stackKc", [128, NBUF * H * TK], BF16)
        Qcs = [stackQc[:, H * T * i:H * T * (i + 1)] for i in range(NBUF)]
        Kcs = [stackKc[:, H * TK * i:H * TK * (i + 1)] for i in range(NBUF)]
        VCp = [sb(f"VCp{i}", [128, H // 2, 32]) for i in range(NBUF)]
        identb = sb("identb", [128, 128], BF16)
        maskq = sb("maskq", [128, 128], BF16)
        maskk = sb("maskk", [128, 128], BF16)
        Wx = sb("Wx", [128, 5, C])
        Wqkc = sb("Wqkc", [128, 3, C])
        Wckr = sb("Wckr", [CK, 2, C])
        Wckp = sb("Wckp", [CK, C])
        bx3 = sb("bx3", [128, 4])
        bvx = sb("bvx", [128, C])
        bcvx = sb("bcvx", [128, C])
        bpx = sb("bpx", [128, C])
        arena2 = sb("arena2", [128, 8 * 3 * C])
        taken[0] = 0
        x2in = part(arena2, NT * C).rearrange("p (a b) -> p a b", b=C)
        qkc32 = part(arena2, 3 * T).rearrange("p (a b) -> p a b", b=T)
        res3 = part(arena2, 3 * T).rearrange("p (a b) -> p a b", b=T)
        parts3 = part(arena2, 9 * T // 2, BF16).rearrange("p (a b) -> p a b", b=T)
        M2 = sb("M2", [128, 4 * H])
        mT = sb("mT", [4 * H, 2, 128], BF16)
        OTx = sb("OTx", [128, 2, T])
        linx = sb("linx", [128, 4, 4, 2])
        ctx2 = sb("ctx2", [128, NT, C])
        cin = P[0][:].rearrange("p a b c -> p (a b c)")[:, 0:512].rearrange("p (n c) -> p n c", n=8)
        cT = P[1][:].rearrange("p a b c -> p (a b c)")[0:CK, :]
        kc32 = P[2][:].rearrange("p a b c -> p (a b c)")
        rc32 = P[3][:].rearrange("p a b c -> p (a b c)")
        vc32 = P[4][:].rearrange("p a b c -> p (a b c)")
        kcp = sb("kcp", [128, 3, B * TK], BF16)
        E_, F2 = w1.shape[0], w1.shape[1]
        FF = F2 // 2
        KF = (128, 128, FF - 256)
        NC = 8
        WAVES = (20, 12)
        TOP = 2
        G4 = 4
        BLOCKS = [-(-(TOP * n + E_ - 1) // G4) * G4 for n in WAVES]
        NTT = B * NT
        NBK = sum(BLOCKS)
        NG, GW0 = NBK // G4, BLOCKS[0] // G4
        T0 = (0, WAVES[0])
        B0 = (0, BLOCKS[0])
        NW = max(WAVES)
        NRG = 3
        NCH = 24
        f32 = lambda t: t.bitcast(F32)
        W1R = {3: (stackQ, 2048), 4: (stackQ, 3072), 5: (stackQc, 2048), 6: (stackQc, 3072),
               7: (stackQ, 4096), 2: (stackQ, 5120), 0: (stackQc, 4096), 1: (stackQc, 5120)}
        W1ROWS = F2 // 8
        w1r = {e: f32(t[:])[0:W1ROWS, o:o + 8 * C].rearrange("p (k c) -> p k c", c=C) for e, (t, o) in W1R.items()}
        w1T = f32(stackK[:])[:, 0:E_ * F2].rearrange("p (e f) -> p e f", e=E_)
        w2T = arena2[:].rearrange("p (e f) -> p e f", e=E_)
        w2r = sb("w2r", [128, E_, FF])
        taken[0] = 0
        A = part(arena1, NW * 64).rearrange("p (t a b) -> p t a b", a=8, b=8)
        G = part(arena1, NW * 32, BF16).rearrange("p (t a b) -> p t a b", a=8, b=8)
        EQ = part(arena1, NW * 32, BF16).rearrange("p (t a b) -> p t a b", a=8, b=8)
        mx = part(arena1, NTT * 24).rearrange("p (t c) -> p t c", c=24)
        rxin = part(arena1, NT * C).rearrange("p (a b) -> p a b", b=C)
        rxT = part(arena1, NT * C)
        taken[0] = 0
        xblk = [part(arenaP, 512).rearrange("p (a b) -> p a b", b=C) for i in range(2)]
        xbT = [part(arenaP, 512).rearrange("p (a b) -> p a b", b=C) for i in range(2)]
        ysb = [part(arenaP, 512).rearrange("p (a b) -> p a b", b=C) for i in range(2)]
        sa = [part(arenaP, FF) for i in range(2)]
        he = [part(arenaP, FF) for i in range(2)]
        heT = [f32(stackKc[:])[:, 384 * i:384 * i + 384].rearrange("p (a b) -> p a b", b=128) for i in range(2)]
        gat = [f32(stackQ[:])[:, 1024 * i:1024 * i + 1024].rearrange("p (a b c) -> p a b c", a=2, b=4) for i in range(NRG)]
        acc = f32(stackQ[:])[:, 3072:3584].rearrange("p (a b) -> p a b", b=C)
        yo = f32(stackQ[:])[:, 3584:4096].rearrange("p (a b) -> p a b", b=C)
        wrr = sb("wrr", [24, C])
        wrT = sb("wrT", [C, 24])
        LT = sb("LT", [128, 8, 8])
        mr = sb("mr", [128, NW, 8])
        den = sb("den", [128, NW, 8])
        num = sb("num", [128, NW, 8])
        lg = sb("lg", [128, NW, 8])
        rank = sb("rank", [128, NW, 8])
        m0 = sb("m0", [128, NW])
        pick = sb("pick", [128, 2, NTT, 8])
        both = sb("both", [128, NTT, 8], BF16)
        cw = sb("cw", [128, 2, NTT])
        iota_i = sb("iota_i", [128, 64], I32)
        iota = sb("iota", [128, 64])
        iota128 = sb("iota128", [128, 32])
        trib = sb("trib", [128, 128], BF16)
        onesb = sb("onesb", [128, 128], BF16)
        nb3 = sb("nb3", [128, 8, NW])
        nblk = sb("nblk", [128, 8])
        ex3 = sb("ex3", [128, 8, 8])
        exb = sb("exb", [128, 8])
        eb3 = sb("eb3", [128, 64, 7], BF16)
        ebf = sb("ebf", [128, 64])
        eid = sb("eid", [128, NBK], I32)
        place = sb("place", [128, NW, 8])
        sl3 = sb("sl3", [128, NW, 8])
        slf = sb("slf", [128, NW])
        slot_u = sb("slot_u", [128, 2, NTT], U32)
        zrow = sb("zrow", [128, C])
        st4 = sb("st4", [128, 4, 6])
        mv4 = sb("mv4", [128, 4, 2])
        ve4 = sb("ve4", [128, 4])
        rs4 = sb("rs4", [128, 4])
        half4 = sb("half4", [128, 4])
        xs = [nc.dram_tensor(f"xs{w}", (128 * BLOCKS[w], C), F32, kind="Internal").ap() for w in range(2)]
        ys = [nc.dram_tensor(f"ys{w}", (128 * BLOCKS[w], C), F32, kind="Internal").ap() for w in range(2)]
        scr_qkc = nc.dram_tensor("scr_qkc", (9, 128, T), BF16, kind="Internal").ap()
        scr_kc = nc.dram_tensor("scr_kc", (3, B, 128, TK), BF16, kind="Internal").ap()
        scr_vc = nc.dram_tensor("scr_vc", (B * TK, C), F32, kind="Internal").ap()
        OTs = sb("OTs", [128, 2, T])
        linv = sb("linv", [128, 4, 4, 2])
        ctx = sb("ctx", [128, NT, C])
        ctxT = sb("ctxT", [128, T])
        r = sb("r", [128, NT, C])
        xb = sb("xb", [128, NT, C])
        st = sb("st", [128, NT, 6])
        mv = sb("mv", [128, NT, 2])
        ve = sb("ve", [128, NT])
        rstd = sb("rstd", [128, NT])

        scr_qk = nc.dram_tensor("scr_qk", (6, 128, T), BF16, kind="Internal").ap()
        scr_v = nc.dram_tensor("scr_v", (16, T, D), F32, kind="Internal").ap()

        PS = es.enter_context(nc.psum_tensor("PS", [128, 8 * 512], F32))
        Sps = [PS[:, 512 * i:512 * (i + 1)] for i in range(2)]
        STps = [PS[:, 1024 * (i + 1):1024 * (i + 2)] for i in range(2)]
        OTps = PS[:, 512 * 6:512 * 7]
        AUX = PS[:, 512 * 7:512 * 8]
        BK = [PS[:, 512 * i:512 * i + 512] for i in range(8)]

        turns = sem("turns")
        xin_in = sem("xin_in")
        wA_in = sem("wA_in")
        cA_in = sem("cA_in")
        ident_ok = sem("ident_ok")
        zero_ok = sem("zero_ok")
        wTA_ps = sem("wTA_ps")
        wTA_sb = sem("wTA_sb")
        xT_ps = sem("xT_ps")
        xT_sb = sem("xT_sb")
        qk_ps = sem("qk_ps")
        qk_sb = sem("qk_sb")
        v_ps = sem("v_ps")
        v_sb = sem("v_sb")
        split = sem("split")
        parts_out = sem("parts_out")
        v_out = sem("v_out")
        stacks_in = sem("stacks_in")
        v_in = sem("v_in")
        s_ps = sem("s_ps")
        max_sb = sem("max_sb")
        mb_sb = sem("mb_sb")
        m_in = sem("m_in")
        st_ps = sem("st_ps")
        p_sb = sem("p_sb")
        pv_ps = sem("pv_ps")
        ot_sb = sem("ot_sb")
        oT_ps = sem("oT_ps")
        linv_sb = sem("linv_sb")
        ctx_sb = sem("ctx_sb")
        ctxT_ps = sem("ctxT_ps")
        ctxT_sb = sem("ctxT_sb")
        y_ps = sem("y_ps")
        xb_sb = sem("xb_sb")
        r_sb = sem("r_sb")
        st_sb = sem("st_sb")
        mv_sb = sem("mv_sb")
        ve_sb = sem("ve_sb")
        rstd_sb = sem("rstd_sb")
        x1_sb = sem("x1_sb")
        vp_ok = sem("vp_ok")
        mask_ok = sem("mask_ok")
        wx_in = sem("wx_in")
        cx_in = sem("cx_in")
        cin_in = sem("cin_in")
        wx_sb = sem("wx_sb")
        cT_ps = sem("cT_ps")
        cT_sb = sem("cT_sb")
        kc_ps = sem("kc_ps")
        kc_sb = sem("kc_sb")
        kc_split = sem("kc_split")
        vc_ps = sem("vc_ps")
        vc_sb = sem("vc_sb")
        kc_out = sem("kc_out")
        vc_out = sem("vc_out")
        c_x2in = sem("c_x2in")
        c_xT_ps = sem("c_xT_ps")
        c_xT_sb = sem("c_xT_sb")
        c_qk_ps = sem("c_qk_ps")
        c_qk_sb = sem("c_qk_sb")
        c_qv_ps = sem("c_qv_ps")
        c_qc_sb = sem("c_qc_sb")
        c_v_sb = sem("c_v_sb")
        c_split = sem("c_split")
        c_vp_sb = sem("c_vp_sb")
        c_parts_out = sem("c_parts_out")
        c_stacks_in = sem("c_stacks_in")
        c_s_ps = sem("c_s_ps")
        c_max_sb = sem("c_max_sb")
        c_mT_ps = sem("c_mT_ps")
        c_mT_sb = sem("c_mT_sb")
        c_m_in = sem("c_m_in")
        c_st_ps = sem("c_st_ps")
        c_p_sb = sem("c_p_sb")
        c_pv_ps = sem("c_pv_ps")
        c_ot_sb = sem("c_ot_sb")
        c_oTs_ps = sem("c_oTs_ps")
        c_oTx_ps = sem("c_oTx_ps")
        c_lin_sb = sem("c_lin_sb")
        c_ctx_sb = sem("c_ctx_sb")
        c_ctx2_sb = sem("c_ctx2_sb")
        c_ctxT_ps = sem("c_ctxT_ps")
        c_ctxT_sb = sem("c_ctxT_sb")
        c_y_ps = sem("c_y_ps")
        c_xb_sb = sem("c_xb_sb")
        c_r_sb = sem("c_r_sb")
        c_st_sb = sem("c_st_sb")
        c_mv_sb = sem("c_mv_sb")
        c_ve_sb = sem("c_ve_sb")
        c_rstd_sb = sem("c_rstd_sb")
        x2_sb = sem("x2_sb")
        f_w1_in = [sem(f"f_w1_in{i}") for i in range(5)]
        f_w2_in = sem("f_w2_in")
        f_wr_in = sem("f_wr_in")
        f_w_ps = sem("f_w_ps")
        f_w_sb = sem("f_w_sb")
        f_const = sem("f_const")
        f_zero = sem("f_zero")
        r_chain = sem("r_chain")
        r_exp = sem("r_exp")
        r_place_ps = sem("r_place_ps")
        r_slots = sem("r_slots")
        x_sent = [sem(f"x_sent{w}") for w in range(2)]
        s_chain = sem("s_chain")
        g_half = sem("g_half")
        zeroed = sem("zeroed")
        b_x_in = [sem(f"b_x_in{i}") for i in range(2)]
        b_xT_ps = sem("b_xT_ps")
        b_xT_sb = sem("b_xT_sb")
        b_h_ps = sem("b_h_ps")
        b_sa = sem("b_sa")
        b_he = sem("b_he")
        b_heT_ps = sem("b_heT_ps")
        b_heT_sb = sem("b_heT_sb")
        b_y_ps = sem("b_y_ps")
        b_y_sb = sem("b_y_sb")
        b_y_out = [sem(f"b_y_out{i}") for i in range(2)]
        g_in = [sem(f"g_in{i}") for i in range(NRG)]
        g_acc = sem("g_acc")
        g_st = sem("g_st")
        g_mv = sem("g_mv")
        g_ve = sem("g_ve")
        g_rs = sem("g_rs")
        g_yo = sem("g_yo")
        g_out = sem("g_out")
        rx_sb = sem("rx_sb")
        rxT_ps = sem("rxT_ps")
        rxT_sb = sem("rxT_sb")
        mx_ps = sem("mx_ps")
        mx_sb = sem("mx_sb")
        wr_ps = sem("wr_ps")
        wr_sb = sem("wr_sb")
        x_in = [sem(f"x_in{i}") for i in range(4)]

        def count(value):
            return max(value, 0) if isinstance(value, int) else value

        def settle(eng):
            eng.sem_inc(turns, 1)

        def span(eng, lo, hi, step):
            if (hi - lo) % 2:
                step(lo, lo // 2, lo % 2)
                lo += 1
            if hi > lo:
                with eng.Fori(0, (hi - lo) // 2, 1) as i:
                    for u in (lo, lo + 1):
                        step(i * 2 + u, i + u // 2, u % 2)
        ranges = [("P", 0), ("L", 1), ("SA", 1), ("SB", 2), ("T", 3), ("E", 4), ("R", 5)]

        def run(eng, step, last):

            def act(t):
                return {k for k, lag in ranges if 0 <= t - lag < B}
            for t in range(5):
                step(t, t % 3, act(t))
            if eng is not None:
                with eng.Fori(5, B - 4, 3) as it:
                    for u in range(3):
                        step(it + u, (5 + u) % 3, {k for k, _ in ranges})
            for t in range(B - 2, last):
                step(t, t % 3, act(t))

        HA, HB = (0, 8), (8, 16)
        S_SLOTS = {4: ("SA", 0, 2), 5: ("SA", 2, 4), 6: ("SA", 4, 6), 7: ("SA", 6, 8),
                   0: ("SB", 8, 11), 1: ("SB", 11, 14), 2: ("SB", 14, 16)}
        S2_SLOTS = {5: ("SA", 0, 2), 6: ("SA", 2, 4), 7: ("SA", 4, 6), 8: ("SA", 6, 8), 9: ("SA", 8, 10),
                    0: ("SB", 10, 13), 1: ("SB", 13, 16), 2: ("SB", 16, 18), 3: ("SB", 18, 20)}
        LAG = dict(ranges)
        UNITS = ([((17, 4 + e // 2 + e // 4), "w2", e, 0) for e in range(8)]
                 + [((18, i), "w1", 3 + i // 2, i % 2) for i in range(10)]
                 + [((19, i), "w1", i // 2, i % 2) for i in range(6)])
        ROUTE = (((15, 4), 0, 0), ((15, 8), 0, 1), ((16, 2), 0, 2), ((16, 5), 0, 3), ((16, 7), 0, 4))
        W1LOAD = {3: 1, 4: 1, 5: 2, 6: 2, 7: 3, 2: 4, 0: 5, 1: 5}

        block = es.enter_context(nc.Block())

        @block.tensor
        def _(pe):
            pe.wait_ge(ident_ok, 2)
            pe.wait_ge(wA_in, 32)
            for c in range(4):
                i = pe.transpose(AUX[:, 128 * c:128 * c + 128], WnatA[:, c, :], ident[:])
            i.then_inc(wTA_ps, 1)
            pe.wait_ge(wTA_sb, 3)
            WV = WTA[:, 0:384].rearrange("p (j x) -> p j x", x=24)[:, :, 16:24]
            pe.wait_ge(zero_ok, 4 * NBUF)
            pe.wait_ge(cin_in, 16)
            for n in range(8):
                i = pe.transpose(PS[0:CK, 1024 + 128 * n:1152 + 128 * n], cin[:, n, :], ident[:])
            i.then_inc(cT_ps, 1)
            pe.wait_ge(cT_sb, 1)
            pe.wait_ge(wx_sb, 4)
            for n in range(2):
                i = pe.matmul(PS[:, 2048 + 512 * n:2560 + 512 * n], Wckp[:], cT[:, 512 * n:512 * n + 512], start=True, stop=True)
            i.then_inc(kc_ps, 1)
            for n in range(8):
                i = pe.matmul(PS[:, 1024 + 128 * n:1152 + 128 * n], cT[:, 128 * n:128 * n + 128], Wckr[:, 1, :], start=True, stop=True)
            i.then_inc(vc_ps, 1)
            pe.wait_ge(vc_sb, 1)

            def step(t, u, on):
                def S(slot):
                    if slot not in S_SLOTS:
                        return
                    stage, h0, h1 = S_SLOTS[slot]
                    if stage not in on:
                        return
                    b = t - LAG[stage]
                    k = (u - LAG[stage]) % 3
                    if h0 == 0:
                        pe.wait_ge(stacks_in, count(b * 96 + 96))
                    Q4 = Qs[k][0:KS, :].rearrange("p (q h) -> p q h", h=H)
                    K4 = Ks[k][0:KS, :].rearrange("p (q h) -> p q h", h=H)
                    for h in range(h0, h1):
                        pe.wait_ge(max_sb, count(b * 16 + (h - 1)))
                        for q in range(2):
                            i = pe.matmul(Sps[h % 2][:, 256 * q:256 * q + 256], Q4[:, 128 * q:128 * q + 128, h], K4[:, :, h],
                                          start=True, stop=True)
                        i.then_inc(s_ps, 1)

                def ST(slot):
                    if "T" not in on:
                        return
                    b = t - 3
                    k = u % 3
                    if slot == 0:
                        pe.wait_ge(m_in, count(b * 64 + 64))
                    pe.wait_ge(p_sb, count(b * 8 + (slot - 1)))
                    Q4 = Qs[k][0:MROW + 2, :].rearrange("p (q h) -> p q h", h=H)
                    K4 = Ks[k][0:MROW + 2, :].rearrange("p (q h) -> p q h", h=H)
                    for n in range(2):
                        h = slot // 2 + 4 * (2 * (slot % 2) + n)
                        for kt in range(2):
                            o = 512 * n + 256 * kt
                            i = pe.matmul(STps[slot % 2][:, o:o + 256], K4[:, 128 * kt:128 * kt + 128, h], Q4[:, :, h],
                                          start=True, stop=True)
                    i.then_inc(st_ps, 1)

                def PV(g, b, k):
                    pe.wait_ge(p_sb, count(b * 8 + (2 * g + 2)))
                    if g == 0:
                        pe.wait_ge(ot_sb, count(b))
                        pe.wait_ge(v_in, count(b * 64 + 64))
                    hf, gg = g // 2, g % 2
                    for kt in range(2):
                        for c in range(4):
                            h = 4 * c + g
                            i = pe.matmul(OTps[32 * c:32 * c + 32, 256 * hf:256 * hf + 256], Vp[k][:, kt, h, :],
                                          P[(2 * g + c // 2) % 4][:, c % 2, kt, :],
                                          start=(gg == 0 and kt == 0), stop=(gg == 1 and kt == 1))
                    i.then_inc(pv_ps, 1)

                for slot in range(8):
                    if slot == 0 and "P" in on:
                        b = t
                        pe.wait_ge(v_sb, count(t))
                        pe.wait_ge(xin_in, count(t * 16 + 16))
                        pe.wait_ge(r_sb, count(t - 4))
                        for c in range(NT):
                            i = pe.transpose(AUX[:, 128 * c:128 * c + 128], xin[u][:, c, :], ident[:])
                        i.then_inc(xT_ps, 1)
                    if slot == 1 and "P" in on:
                        pe.wait_ge(xT_sb, count(t + 1))
                        for a in range(2):
                            i = pe.matmul(AUX[:, 256 * a:256 * a + 256], WqkA[:, a, :], xT[:], start=True, stop=True)
                        i.then_inc(qk_ps, 1)
                    if slot == 2 and "P" in on:
                        pe.wait_ge(qk_sb, count(t * 2 + 2))
                        for c in range(2):
                            i = pe.matmul(AUX[:, 128 * c:128 * c + 128], xT[:, 128 * c:128 * c + 128], WV, start=True, stop=True)
                        i.then_inc(v_ps, 1)
                    if slot == 4 and "E" in on:
                        b = t - 4
                        pe.wait_ge(ot_sb, count(b + 1))
                        if "P" in on:
                            pe.wait_ge(v_sb, count(t + 1))
                        else:
                            pe.wait_ge(r_sb, count(t - 4))
                        for c in range(2):
                            for hf in range(2):
                                o = 256 * c + 128 * hf
                                i = pe.transpose(AUX[:, o:o + 128], OTs[:, hf, 128 * c:128 * c + 128], ident[:])
                        i.then_inc(oT_ps, 1)
                    if slot == 5 and "E" in on:
                        pe.wait_ge(ctx_sb, count(t - 3))
                        for c in range(NT):
                            i = pe.transpose(AUX[:, 128 * c:128 * c + 128], ctx[:, c, :], ident[:])
                        i.then_inc(ctxT_ps, 1)
                    if slot == 6 and "E" in on:
                        pe.wait_ge(ctxT_sb, count(t - 3))
                        for c in range(NT):
                            i = pe.matmul(AUX[:, 128 * c:128 * c + 128], ctxT[:, 128 * c:128 * c + 128], WTA[:, 384:512], start=True, stop=True)
                        i.then_inc(y_ps, 1)
                    S(slot)
                    ST(slot)
                    if slot == 0 and "E" in on:
                        PV(3, t - 4, (u - 1) % 3)
                    if slot in (2, 4, 6) and "T" in on:
                        PV(slot // 2 - 1, t - 3, u % 3)
                if isinstance(t, int) and t == 3:
                    pe.wait_ge(v_sb, 4)
            run(pe, step, B + 4)


            def placement(w, bank):
                n = WAVES[w]
                pe.wait_ge(r_chain, NCH * w + 15)
                m = both[:, T0[w]:T0[w] + n, :]
                pe.matmul(bank[:, 0:8 * n], trib[:], m, start=True, stop=False)
                for i in range(n - 1):
                    pe.matmul(bank[:, 8 * i + 8:8 * n], onesb[:], m[:, i:i + 1, :].to_broadcast((128, n - 1 - i, 8)), start=False, stop=(i == n - 2))
                for i in range(n):
                    j = pe.matmul(bank[:, 8 * n:8 * n + 8], onesb[:], m[:, i, :], start=(i == 0), stop=(i == n - 1))
                j.then_inc(r_place_ps, 1)

            def turn_weights(n, kind, e, half_):
                bank = BK[n % 2]
                if n >= 2:
                    pe.wait_ge(f_w_sb, n - 1)
                else:
                    pe.wait_ge(c_max_sb, 20 * B)
                if kind == "w2":
                    pe.wait_ge(f_w2_in, 32)
                    for k in range(3):
                        i = pe.transpose(bank[0:KF[k], 128 * k:128 * k + 128], w2r[:, e, 128 * k:128 * k + KF[k]], ident[:])
                else:
                    pe.wait_ge(f_w1_in[W1LOAD[e] - 1], 16)
                    for k in range(4):
                        i = pe.transpose(bank[:, W1ROWS * k:W1ROWS * k + W1ROWS], w1r[e][:, 4 * half_ + k, :], ident[0:W1ROWS, 0:W1ROWS])
                i.then_inc(f_w_ps, 1)

            def step2(t, u, on):
                def S(slot):
                    if slot not in S2_SLOTS or S2_SLOTS[slot][0] not in on:
                        return
                    stage, n0, n1 = S2_SLOTS[slot]
                    b = t - LAG[stage]
                    k = (u - LAG[stage]) % 3
                    if n0 == 0:
                        pe.wait_ge(c_stacks_in, count(b * 224 + 224))
                    for n in range(n0, n1):
                        pe.wait_ge(c_max_sb, count(b * 20 + (n - 1)))
                        o = Sps[n % 2]
                        if n < 16:
                            q, kk = Qs[k][0:KS, T * n:T * n + T], Ks[k][0:KS, T * n:T * n + T]
                            pe.matmul(o[:, 0:128], q[:, 0:128], kk[:, 0:128], start=True, stop=False)
                            pe.matmul(o[:, 0:128], identb[:], maskq[:], start=False, stop=True)
                            pe.matmul(o[:, 128:384], q[:, 128:256], kk, start=True, stop=False)
                            i = pe.matmul(o[:, 256:384], identb[:], maskq[:], start=False, stop=True)
                        else:
                            for h in range(4 * (n - 16), 4 * (n - 15)):
                                for qt in range(2):
                                    c = (h % 4) * 128 + 64 * qt
                                    i = pe.matmul(o[:, c:c + 64], Qcs[k][0:KS, T * h + 128 * qt:T * h + 128 * qt + 128],
                                                  Kcs[k][0:KS, TK * h:TK * h + TK], start=True, stop=True)
                        i.then_inc(c_s_ps, 1)

                def ST(slot):
                    if "T" not in on:
                        return
                    b = t - 3
                    k = u % 3
                    if slot == 0:
                        pe.wait_ge(c_m_in, count(b * 64 + 64))
                    pe.wait_ge(c_p_sb, count(b * 10 + (slot - 1)))
                    o = STps[slot % 2]
                    if slot < 8:
                        for n in range(2):
                            h = slot // 2 + 4 * (2 * (slot % 2) + n)
                            q, kk = Qs[k][0:MROW + 2, T * h:T * h + T], Ks[k][0:MROW + 2, T * h:T * h + T]
                            c = 512 * n
                            pe.matmul(o[:, c:c + 256], kk[:, 0:128], q, start=True, stop=False)
                            pe.matmul(o[:, c:c + 128], identb[:], maskk[:], start=False, stop=True)
                            pe.matmul(o[:, c + 256:c + 384], kk[:, 128:256], q[:, 128:256], start=True, stop=False)
                            i = pe.matmul(o[:, c + 256:c + 384], identb[:], maskk[:], start=False, stop=True)
                    else:
                        for c in range(4):
                            for n in range(2):
                                h = 4 * c + 2 * (slot - 8) + n
                                i = pe.matmul(o[64 * n:64 * n + 64, 256 * c:256 * c + 256], Kcs[k][0:MROW + 2, TK * h:TK * h + TK],
                                              Qcs[k][0:MROW + 2, T * h:T * h + T], start=True, stop=True)
                    i.then_inc(c_st_ps, 1)

                def PV(g, b, k):
                    pe.wait_ge(c_p_sb, count(b * 10 + (2 * g + 2)))
                    if g == 0:
                        pe.wait_ge(c_ot_sb, count(b * 2))
                        pe.wait_ge(c_vp_sb, count(b * 2 + 2))
                    hf, gg = g // 2, g % 2
                    for kt in range(2):
                        for c in range(4):
                            h = 4 * c + g
                            tile = P[(2 * g + c // 2) % 5][:, c % 2].rearrange("p a b -> p (a b)")
                            i = pe.matmul(OTps[32 * c:32 * c + 32, 256 * hf + 128 * kt:256 * hf + 256], Vp[k][:, kt, h, :],
                                          tile[:, 256 * kt:256 + 128 * kt],
                                          start=(gg == 0 and kt == 0), stop=(gg == 1 and kt == 1))
                    i.then_inc(c_pv_ps, 1)

                def PVX(hf, b, k):
                    pe.wait_ge(c_p_sb, count(b * 10 + 9 + hf))
                    if hf == 0:
                        pe.wait_ge(c_ot_sb, count(b * 2 + 1))
                    tile = P[(8 + hf) % 5][:].rearrange("p a b c -> p (a b c)")
                    for c in range(4):
                        i = pe.matmul(OTps[32 * c:32 * c + 32, 256 * hf:256 * hf + 256], VCp[k][:, 2 * c + hf, :],
                                      tile[:, 256 * c:256 * c + 256], start=True, stop=True)
                    i.then_inc(c_pv_ps, 1)

                for slot in range(10):
                    if slot == 0 and "P" in on:
                        pe.wait_ge(c_v_sb, count(t))
                        pe.wait_ge(mx_sb, count(t - 5))
                        pe.wait_ge(c_x2in, count(t + 1))
                        pe.wait_ge(c_r_sb, count(t - 4))
                        for c in range(NT):
                            i = pe.transpose(AUX[:, 128 * c:128 * c + 128], x2in[:, c, :], ident[:])
                        i.then_inc(c_xT_ps, 1)
                    if slot == 1 and "P" in on:
                        pe.wait_ge(c_xT_sb, count(t + 1))
                        for a in range(2):
                            i = pe.matmul(AUX[:, 256 * a:256 * a + 256], Wqkc[:, a, :], xT[:], start=True, stop=True)
                        i.then_inc(c_qk_ps, 1)
                    if slot == 2 and "P" in on:
                        pe.wait_ge(c_qk_sb, count(t * 2 + 2))
                        pe.matmul(AUX[:, 0:256], Wqkc[:, 2, :], xT[:], start=True, stop=True)
                        for c in range(2):
                            i = pe.matmul(AUX[:, 256 + 128 * c:384 + 128 * c], xT[:, 128 * c:128 * c + 128], Wx[:, 3, :], start=True, stop=True)
                        i.then_inc(c_qv_ps, 1)
                    if slot == 4 and "SB" in on:
                        b = t - 2
                        if "P" in on:
                            pe.wait_ge(c_qc_sb, count(t + 1))
                            pe.wait_ge(c_v_sb, count(t + 1))
                        else:
                            pe.wait_ge(c_r_sb, count(t - 4))
                            pe.wait_ge(mx_sb, count(t - 5))
                        if isinstance(t, int) and t == 17:
                            pe.wait_ge(r_slots, 1)
                        pe.wait_ge(c_max_sb, count(b * 20 + 20))
                        settle(pe)
                        pe.transpose(AUX[0:4 * H, 0:128], M2[:], ident[:]).then_inc(c_mT_ps, 1)
                    if slot == 5 and "E" in on:
                        if "SB" in on:
                            pe.wait_ge(c_mT_sb, count(t * 2 - 2))
                        else:
                            pe.wait_ge(c_r_sb, count(t - 4))
                            pe.wait_ge(mx_sb, count(t - 5))
                        for c in range(2):
                            for hf in range(2):
                                o = 256 * c + 128 * hf
                                i = pe.transpose(AUX[:, o:o + 128], OTs[:, hf, 128 * c:128 * c + 128], ident[:])
                        i.then_inc(c_oTs_ps, 1)
                    if slot == 6 and "E" in on:
                        pe.wait_ge(c_ot_sb, count(t * 2 - 6))
                        pe.wait_ge(c_ctx_sb, count(t - 3))
                        for c in range(2):
                            for hf in range(2):
                                o = 256 * c + 128 * hf
                                i = pe.transpose(AUX[:, o:o + 128], OTx[:, hf, 128 * c:128 * c + 128], ident[:])
                        i.then_inc(c_oTx_ps, 1)
                    if slot == 7 and "E" in on:
                        pe.wait_ge(c_ctx2_sb, count(t * 2 - 6))
                        for c in range(NT):
                            i = pe.transpose(AUX[:, 128 * c:128 * c + 128], ctx[:, c, :], ident[:])
                        i.then_inc(c_ctxT_ps, 1)
                    if slot == 8 and "E" in on:
                        pe.wait_ge(c_ctxT_sb, count(t - 3))
                        for c in range(NT):
                            i = pe.matmul(AUX[:, 128 * c:128 * c + 128], ctxT[:, 128 * c:128 * c + 128], Wx[:, 4, :], start=True, stop=True)
                        i.then_inc(c_y_ps, 1)
                    if slot == 9 and "R" in on:
                        pe.wait_ge(rx_sb, count(t - 4))
                        if "E" in on:
                            pe.wait_ge(c_r_sb, count(t - 3))
                        else:
                            pe.wait_ge(mx_sb, count(t - 5))
                        for c in range(NT):
                            i = pe.transpose(AUX[:, 128 * c:128 * c + 128], rxin[:, c, :], ident[:])
                        i.then_inc(rxT_ps, 1)
                    S(slot)
                    ST(slot)
                    if slot == 0 and "E" in on:
                        PVX(1, t - 4, (u - 1) % 3)
                    if slot in (2, 4, 6, 8) and "T" in on:
                        PV(slot // 2 - 1, t - 3, u % 3)
                    if slot == 9 and "T" in on:
                        PVX(0, t - 3, u % 3)
                    if slot == 9 and "R" in on:
                        pe.wait_ge(rxT_sb, count(t - 4))
                        for c in range(NT):
                            i = pe.matmul(AUX[:, 24 * c:24 * c + 24], rxT[:, 128 * c:128 * c + 128], wrT[:], start=True, stop=True)
                        i.then_inc(mx_ps, 1)
                    if isinstance(t, int):
                        if t == 17 and slot == 0:
                            pe.wait_ge(mx_sb, t - 5)
                            placement(0, BK[7])
                        for n, unit in enumerate(UNITS):
                            if unit[0] == (t, slot):
                                turn_weights(n, *unit[1:])
                if isinstance(t, int) and t == 3:
                    pe.wait_ge(c_mT_sb, 4)
                    pe.wait_ge(c_qc_sb, 4)
                    pe.wait_ge(c_v_sb, 4)
            pe.wait_ge(f_wr_in, 16)
            pe.wait_ge(r_sb, B)
            pe.transpose(AUX[:, 0:24], wrr[:], ident[0:24, 0:24]).then_inc(wr_ps, 1)
            pe.wait_ge(wr_sb, 1)
            pe.wait_ge(mask_ok, 6)
            pe.wait_ge(zero_ok, 6 * NBUF)
            run(pe, step2, B + 5)
            pe.wait_ge(c_ot_sb, 2 * B)
            placement(1, BK[6])
            pe.wait_ge(f_w_sb, len(UNITS))
            pe.wait_ge(c_p_sb, 10 * B)
            pe.wait_ge(mx_sb, B)

            def turn_x(g, h, p):
                pe.wait_ge(b_x_in[p], h * 16 + 16)
                pe.wait_ge(b_xT_sb, count(g))
                for i in range(4):
                    j = pe.transpose(BK[7][:, 128 * i:128 * i + 128], xblk[p][:, i, :], ident[:])
                j.then_inc(b_xT_ps, 1)

            def expert(j):
                return pe.value_load(eid[0:1, j:j + 1] if isinstance(j, int) else eid[0:1, bass.ds(j, 1)], min_val=0, max_val=E_ - 1)

            def hidden(j, u, p):
                e = expert(j)
                pe.wait_ge(b_he, count(j - 1))
                for f in range(2):
                    i = pe.matmul(BK[2 * f + u % 2][:, 0:FF], xbT[p][:, u, :], w1T[:, bass.ds(e, 1), FF * f:FF * f + FF].rearrange("p a b -> p (a b)"), start=True, stop=True)
                i.then_inc(b_h_ps, 1)

            def turn_hidden(j, u):
                pe.wait_ge(b_he, count(j + 1))
                pe.wait_ge(b_heT_sb, count(j - 1))
                for k in range(3):
                    i = pe.transpose(BK[4 + u % 2][0:KF[k], 128 * k:128 * k + 128], he[u % 2][:, 128 * k:128 * k + KF[k]], ident[:])
                i.then_inc(b_heT_ps, 1)

            def result(j, u):
                if isinstance(j, int) and j == 0:
                    pe.wait_ge(r_slots, 2)
                e = expert(j)
                pe.wait_ge(b_heT_sb, count(j + 1))
                pe.wait_ge(b_y_sb, count(j))
                for k in range(3):
                    i = pe.matmul(BK[6][:, 0:128], heT[u % 2][0:KF[k], k, :], w2T[0:KF[k], bass.ds(e, 1), 128 * k:128 * k + 128].rearrange("p a b -> p (a b)"), start=(k == 0), stop=(k == 2))
                i.then_inc(b_y_ps, 1)

            def step(g, h, p, more=True):
                for u in range(4):
                    j = g * 4 + u
                    if u == 0:
                        pe.wait_ge(b_xT_sb, count(g + 1))
                    hidden(j, u, p)
                    if not (isinstance(j, int) and j < 1):
                        turn_hidden(j - 1, u + 1)
                    if not (isinstance(j, int) and j < 2):
                        result(j - 2, u)
                    if u == 1 and more:
                        turn_x(g + 1, h + p, 1 - p)
            turn_x(0, 0, 0)
            for g in range(2):
                step(g, g // 2, g % 2)
            span(pe, 2, NG - 2, step)
            step(NG - 2, NG // 2 - 1, 0)
            step(NG - 1, NG // 2 - 1, 1, more=False)
            turn_hidden(NBK - 1, 1)
            result(NBK - 2, 0)
            result(NBK - 1, 1)

        @block.scalar
        def _(act):
            def step(t, u, on):
                for slot in range(8):
                    if slot == 1 and "P" in on:
                        act.wait_ge(qk_ps, count(t + 1))
                        act.wait_ge(split, count(t * 4))
                        for a in range(2):
                            act.activation(qk32[:, a, :], AUX[:, 256 * a:256 * a + 256], ACT.Identity, bias=bqkA[:, a:a + 1]).then_inc(qk_sb, 1)
                    if slot == 5 and "E" in on:
                        act.wait_ge(ctxT_ps, count(t - 3))
                        act.wait_ge(y_ps, count(t - 4))
                        act.activation(ctxT[:], AUX[:, 0:256], ACT.Copy).then_inc(ctxT_sb, 1)
                    if "T" in on:
                        b = t - 3
                        act.wait_ge(st_ps, count(b * 8 + (slot + 1)))
                        act.wait_ge(pv_ps, count(b * 4 + (slot // 2 - 1)))
                        act.activation(P[slot % 4][:].rearrange("p a b c -> p (a b c)"), STps[slot % 2], ACT.Exp, scale=SCALE).then_inc(p_sb, 1)
                    if slot == 0 and "E" in on:
                        act.wait_ge(pv_ps, count(t * 4 - 12))
                        act.wait_ge(oT_ps, count(t - 4))
                        act.activation(OTs[:].rearrange("p f (i j) -> p f j i", j=16), OTps.rearrange("p (f j i) -> p f j i", f=2, i=16), ACT.Copy).then_inc(ot_sb, 1)
            act.wait_ge(cA_in, 64)
            run(act, step, B + 4)

            def step2(t, u, on):
                for slot in range(10):
                    if slot == 1 and "P" in on:
                        act.wait_ge(c_qk_ps, count(t + 1))
                        act.wait_ge(c_split, count(t * 4))
                        for a in range(2):
                            act.activation(qkc32[:, a, :], AUX[:, 256 * a:256 * a + 256], ACT.Identity, bias=bx3[:, a:a + 1]).then_inc(c_qk_sb, 1)
                    if slot == 2 and "P" in on:
                        act.wait_ge(c_qv_ps, count(t + 1))
                        act.activation(qkc32[:, 2, :], AUX[:, 0:256], ACT.Identity, bias=bx3[:, 2:3]).then_inc(c_qc_sb, 1)
                    if slot == 7 and "E" in on:
                        act.wait_ge(c_ctxT_ps, count(t - 3))
                        act.wait_ge(c_y_ps, count(t - 4))
                        act.activation(ctxT[:], AUX[:, 0:256], ACT.Copy).then_inc(c_ctxT_sb, 1)
                    if slot == 9 and "R" in on:
                        act.wait_ge(rxT_ps, count(t - 4))
                        act.wait_ge(mx_ps, count(t - 5))
                        act.activation(rxT, AUX[:, 0:256], ACT.Copy).then_inc(rxT_sb, 1)
                    if "T" in on:
                        b = t - 3
                        act.wait_ge(c_st_ps, count(b * 10 + (slot + 1)))
                        if slot < 5:
                            if not (isinstance(b, int) and b == 0):
                                act.wait_ge(c_pv_ps, count(b * 6 - 6 + (3, 4, 4, 5, 6)[slot]))
                        else:
                            act.wait_ge(c_pv_ps, count(b * 6 + ((slot - 5) // 2 + 1)))
                        src, dst = STps[slot % 2], P[slot % 5][:].rearrange("p a b c -> p (a b c)")
                        if slot < 8:
                            src = src.rearrange("p (n k) -> p n k", n=2)[:, :, 0:384]
                            dst = dst.rearrange("p (n k) -> p n k", n=2)[:, :, 0:384]
                        act.activation(dst, src, ACT.Exp, scale=SCALE).then_inc(c_p_sb, 1)
                    if slot == 8 and "T" in on:
                        b = t - 3
                        act.wait_ge(c_pv_ps, count(b * 6 + 4))
                        act.wait_ge(c_oTs_ps, count(b))
                        act.activation(OTs[:].rearrange("p a b -> p (a b)"), OTps, ACT.Copy).then_inc(c_ot_sb, 1)
                    if slot == 5 and "R" in on:
                        b = t - 5
                        act.wait_ge(x2_sb, count(b * 2 + 2))
                        act.wait_ge(rxT_ps, count(b))
                        act.activation(rxin, X[:, 2 * b:2 * b + 2, :] if isinstance(b, int) else X[:, bass.ds(b * 2, 2), :], ACT.Copy).then_inc(rx_sb, 1)
                    if slot == 9 and "R" in on:
                        act.wait_ge(mx_ps, count(t - 4))
                        b = t - 5
                        act.activation(mx[:, 2 * b:2 * b + 2, :] if isinstance(b, int) else mx[:, bass.ds(b * 2, 2), :],
                                       AUX[:, 0:48].rearrange("p (a b) -> p a b", b=24), ACT.Copy).then_inc(mx_sb, 1)
                    if isinstance(t, int) and (t, slot) == (15, 6):
                        act.wait_ge(r_chain, 3)
                        act.activation(A[:, 0:WAVES[0]], A[:, 0:WAVES[0]], ACT.Exp).then_inc(r_exp, 1)
                    if isinstance(t, int) and (t, slot) == (16, 8):
                        act.wait_ge(r_chain, 21)
                        act.activation(m0[:, 0:WAVES[0]], m0[:, 0:WAVES[0]], ACT.Exp).then_inc(r_exp, 1)
                    if slot == 0 and "E" in on:
                        b = t - 4
                        act.wait_ge(c_pv_ps, count(b * 6 + 6))
                        act.wait_ge(c_oTx_ps, count(b))
                        act.activation(OTx[:].rearrange("p a b -> p (a b)"), OTps, ACT.Copy).then_inc(c_ot_sb, 1)
            act.wait_ge(cx_in, 144)
            run(act, step2, B + 5)
            act.wait_ge(r_chain, NCH + 3)
            act.activation(A[:, 0:WAVES[1]], A[:, 0:WAVES[1]], ACT.Exp).then_inc(r_exp, 1)
            act.wait_ge(r_chain, NCH + 21)
            act.activation(m0[:, 0:WAVES[1]], m0[:, 0:WAVES[1]], ACT.Exp).then_inc(r_exp, 1)

            def step(g, h, p):
                for u in range(4):
                    j = g * 4 + u
                    act.wait_ge(b_h_ps, count(j + 1))
                    act.wait_ge(b_he, count(j - 1))
                    act.activation(sa[u % 2][:], BK[u % 2][:, 0:FF], ACT.Silu).then_inc(b_sa, 1)
                    if not (isinstance(j, int) and j < 1):
                        copy_heT(j - 1, u + 1)

            def copy_heT(j, u):
                act.wait_ge(b_heT_ps, count(j + 1))
                act.wait_ge(b_y_ps, count(j - 1))
                act.activation(heT[u % 2][:, 0:2, :].rearrange("p a b -> p (a b)"), BK[4 + u % 2][:, 0:256], ACT.Copy)
                act.activation(heT[u % 2][0:KF[2], 2, :], BK[4 + u % 2][0:KF[2], 256:384], ACT.Copy).then_inc(b_heT_sb, 1)
            for g in range(2):
                step(g, g // 2, g % 2)
            span(act, 2, NG, step)
            copy_heT(NBK - 1, 1)

        @block.vector
        def _(dve):
            dve.memset(zrow[:], 0.0).then_inc(f_zero, 1)
            dve.wait_ge(wTA_ps, 1)
            dve.tensor_copy(WTA[:], AUX).then_inc(wTA_sb, 1)
            for a in range(2):
                dve.tensor_copy(WqkA[:, a, :].rearrange("p (d j) -> p d j", j=16),
                                AUX[:, 0:384].rearrange("p (j x) -> p x j", x=24)[:, 8 * a:8 * a + 8, :]).then_inc(wTA_sb, 1)
            for k in range(NBUF):
                dve.memset(Qs[k][0:96, :].bitcast(F32), 0.0).then_inc(zero_ok, 1)
                dve.memset(Ks[k][64:96, :].bitcast(F32), 0.0).then_inc(zero_ok, 1)
                dve.memset(Ks[k][32:64, :], 1.0).then_inc(zero_ok, 1)
                dve.memset(Ks[k][96:98, :], 1.0).then_inc(zero_ok, 1)
            for k in range(NBUF):
                dve.memset(Qcs[k][0:96, :].bitcast(F32), 0.0).then_inc(zero_ok, 1)
                dve.memset(Kcs[k][96:98, :], 1.0).then_inc(zero_ok, 1)
            dve.wait_ge(vp_ok, 2 * NBUF)
            for k in range(NBUF):
                dve.memset(VCp[k][0:64, :, 16:17], 1.0).then_inc(vp_ok, 1)
                dve.memset(VCp[k][64:128, :, 17:18], 1.0).then_inc(vp_ok, 1)
            dve.wait_ge(wx_in, 80)
            for a in range(3):
                dve.tensor_copy(Wqkc[:, a, :].rearrange("p (d h) -> p d h", d=D), Wx[:, a, :].rearrange("p (h d) -> p d h", d=D)).then_inc(wx_sb, 1)
            dve.wait_ge(cx_in, 144)
            dve.tensor_copy(Wckp[:].rearrange("p (d h) -> p d h", d=D), Wckr[:, 0, :].rearrange("p (h d) -> p d h", d=D)).then_inc(wx_sb, 1)
            dve.wait_ge(cT_ps, 1)
            dve.tensor_copy(cT, PS[0:CK, 1024:2048]).then_inc(cT_sb, 1)
            dve.wait_ge(kc_ps, 1)
            dve.tensor_scalar(kc32, PS[:, 2048:3072], bx3[:, 3:4], None, ALU.add).then_inc(kc_split, 1)
            dve.wait_ge(kc_split, 1)
            kv = kcp[:]
            dve.tensor_copy(kv[:, 0, :], kc32).then_inc(kc_split, 1)
            dve.wait_ge(kc_split, 2)
            dve.tensor_tensor(rc32, kc32, kv[:, 0, :], ALU.subtract).then_inc(kc_split, 1)
            dve.wait_ge(kc_split, 3)
            dve.tensor_copy(kv[:, 1, :], rc32).then_inc(kc_split, 1)
            dve.wait_ge(kc_split, 4)
            dve.tensor_tensor(kv[:, 2, :], rc32, kv[:, 1, :], ALU.subtract).then_inc(kc_split, 1)
            dve.wait_ge(vc_ps, 1)
            dve.tensor_tensor(vc32.rearrange("p (n c) -> p n c", c=C), PS[:, 1024:2048].rearrange("p (n c) -> p n c", c=C),
                              bcvx[:].unsqueeze(1).to_broadcast((128, 8, C)), ALU.add).then_inc(vc_sb, 1)
            dve.wait_ge(cA_in, 64)

            def step(t, u, on):
                for slot in range(8):
                    if slot == 0 and "P" in on:
                        dve.wait_ge(xT_ps, count(t + 1))
                        dve.wait_ge(v_ps, count(t))
                        dve.tensor_copy(xT[:].rearrange("p (i h) -> p h i", h=H), AUX[:, 0:256].rearrange("p (h i) -> p h i", i=16)).then_inc(xT_sb, 1)
                    if slot == 2 and "P" in on:
                        dve.wait_ge(v_ps, count(t + 1))
                        dve.wait_ge(v_out, count(t * 32))
                        dve.tensor_tensor(vsb[:], AUX[:, 0:256].rearrange("p (c f) -> p c f", c=2),
                                          bvA[:].unsqueeze(1).to_broadcast((128, 2, C)), ALU.add).then_inc(v_sb, 1)
                    if slot == 3 and "SB" in on:
                        b = t - 2
                        dve.wait_ge(m_in, count(b * 64))
                        dve.wait_ge(max_sb, count(b * 16 + 16))
                        dve.tensor_scalar(Mb[:, 0, :], M[:].rearrange("p q h -> p (q h)"), -1.0, None, ALU.mult).then_inc(mb_sb, 1)
                        dve.wait_ge(mb_sb, count(b * 2 + 1))
                        dve.scalar_tensor_tensor(out=Mb[:, 1, :], in0=M[:].rearrange("p q h -> p (q h)"), scalar=-1.0, in1=Mb[:, 0, :],
                                                 op0=ALU.mult, op1=ALU.subtract).then_inc(mb_sb, 1)
                    if slot == 4 and "E" in on:
                        b = t - 4
                        dve.wait_ge(oT_ps, count(b + 1))
                        o5 = AUX.rearrange("p (t c x) -> p t c x", t=4, c=4)
                        dve.wait_ge(ctx_sb, count(b))
                        dve.reciprocal(linv[:], o5[:, :, :, 16:18]).then_inc(linv_sb, 1)
                        dve.wait_ge(linv_sb, count(b + 1))
                        dve.wait_ge(ctxT_ps, count(b))
                        for c in range(2):
                            for hf in range(2):
                                th = 2 * c + hf
                                i = dve.tensor_tensor(ctx[:, c, :].rearrange("p (q f g d) -> p q f g d", q=4, f=2, g=2)[:, :, hf],
                                                      o5[:, th, :, 0:16].rearrange("p q (g d) -> p q g d", g=2),
                                                      linv[:, th, :, :].unsqueeze(3).to_broadcast((128, 4, 2, D)), ALU.mult)
                        i.then_inc(ctx_sb, 1)
                    if slot == 6 and "E" in on:
                        b = t - 4
                        dve.wait_ge(y_ps, count(b + 1))
                        dve.wait_ge(xb_sb, count(b + 1))
                        dve.wait_ge(x1_sb, count(b * 2))
                        dve.tensor_tensor(r[:], AUX[:, 0:256].rearrange("p (c f) -> p c f", c=2), xb[:], ALU.add).then_inc(r_sb, 1)
                        dve.wait_ge(r_sb, count(b + 1))
                        dve.wait_ge(mv_sb, count(b * 2))
                        for c in range(2):
                            dve.bn_stats(st[:, c, :], r[:, c, :]).then_inc(st_sb, 1)
                        dve.wait_ge(st_sb, count(b * 2 + 2))
                        settle(dve)
                        for c in range(2):
                            dve.bn_aggr(mv[:, c, :], st[:, c, :]).then_inc(mv_sb, 1)
                    if slot == 7 and "E" in on:
                        b = t - 4
                        dve.wait_ge(rstd_sb, count(b + 1))
                        for c in range(2):
                            dve.tensor_scalar(X[:, b * 2 + c, :], r[:, c, :], mv[:, c, 0:1], rstd[:, c:c + 1],
                                              ALU.subtract, ALU.mult).then_inc(x1_sb, 1)
                    if slot in S_SLOTS and S_SLOTS[slot][0] in on:
                        stage, h0, h1 = S_SLOTS[slot]
                        b = t - LAG[stage]
                        if h0 == 0:
                            dve.wait_ge(mb_sb, count(b * 2))
                        for h in range(h0, h1):
                            dve.wait_ge(s_ps, count(b * 16 + (h + 1)))
                            dve.tensor_reduce(out=M[:, :, h], in_=Sps[h % 2].rearrange("p (q k) -> p q k", q=2), op=ALU.max,
                                              axis=AX.X).then_inc(max_sb, 1)
            run(dve, step, B + 4)
            dve.wait_ge(wr_ps, 1)
            dve.tensor_copy(wrT[:], AUX[:, 0:24]).then_inc(wr_sb, 1)
            dve.wait_ge(f_const, 9)


            turn, slots = [0], [0]

            def link(ins):
                turn[0] += 1
                ins.then_inc(r_chain, 1)
                dve.wait_ge(r_chain, turn[0])

            def hop(ins):
                slots[0] += 1
                ins.then_inc(s_chain, 1)
                dve.wait_ge(s_chain, slots[0])

            def route(w, piece):
                n, t0 = WAVES[w], T0[w]
                a, g, eq = A[:, 0:n], G[:, 0:n], EQ[:, 0:n]
                m, r_, d_, n_, l_, k_ = mx[:, t0:t0 + n], mr[:, 0:n], den[:, 0:n], num[:, 0:n], lg[:, 0:n], rank[:, 0:n]
                p0, p1 = pick[:, 0, t0:t0 + n], pick[:, 1, t0:t0 + n]
                c0, c1 = cw[:, 0, t0:t0 + n], cw[:, 1, t0:t0 + n]
                bj = lambda t: t.unsqueeze(2).to_broadcast((128, n, 8, 8))
                be = lambda t: t.unsqueeze(3).to_broadcast((128, n, 8, 8))
                if piece == 0:
                    dve.wait_ge(mx_sb, (t0 + n) // 2)
                    link(dve.tensor_tensor(a, be(m[:, :, 0:8]), bj(m[:, :, 8:16]), ALU.mult))
                    link(dve.tensor_reduce(out=r_, in_=a, op=ALU.max, axis=AX.X))
                    link(dve.tensor_tensor(a, a, be(r_), ALU.subtract))
                if piece == 1:
                    dve.wait_ge(r_exp, 2 * w + 1)
                    link(dve.tensor_reduce(out=d_, in_=a, op=ALU.add, axis=AX.X))
                    link(dve.tensor_tensor(a, a, bj(m[:, :, 16:24]), ALU.mult))
                    link(dve.tensor_reduce(out=n_, in_=a, op=ALU.add, axis=AX.X))
                    link(dve.reciprocal(d_, d_))
                    link(dve.tensor_tensor(l_, n_, d_, ALU.mult))
                if piece == 2:
                    link(dve.tensor_tensor(g, bj(l_), be(l_), ALU.is_gt))
                    link(dve.tensor_tensor(eq, bj(l_), be(l_), ALU.is_equal))
                if piece == 3:
                    link(dve.tensor_tensor(eq, eq, LT[:].unsqueeze(1).to_broadcast((128, n, 8, 8)), ALU.mult))
                    link(dve.tensor_tensor(g, g, eq, ALU.add))
                if piece == 4:
                    link(dve.tensor_reduce(out=k_, in_=g, op=ALU.add, axis=AX.X))
                    link(dve.tensor_scalar(p0, k_, 0.5, None, ALU.is_lt))
                    link(dve.tensor_scalar(both[:, t0:t0 + n, :], k_, 1.5, None, ALU.is_lt))
                    link(dve.tensor_scalar(p1, k_, 1.0, None, ALU.is_equal))
                    link(dve.tensor_tensor(n_, p0, l_, ALU.mult))
                    link(dve.tensor_tensor(d_, p1, l_, ALU.mult))
                    link(dve.tensor_reduce(out=c0, in_=n_, op=ALU.add, axis=AX.X))
                    link(dve.tensor_reduce(out=c1, in_=d_, op=ALU.add, axis=AX.X))
                    if w:
                        dve.wait_ge(r_exp, 2)
                    link(dve.tensor_tensor(m0[:, 0:n], c1, c0, ALU.subtract))
                    dve.wait_ge(r_exp, 2 * w + 2)
                    link(dve.tensor_scalar(c0, m0[:, 0:n], 1.0, None, ALU.add))
                    link(dve.reciprocal(c0, c0))
                    link(dve.tensor_tensor(c1, m0[:, 0:n], c0, ALU.mult))
                    assert turn[0] == NCH * (w + 1)

            def place_rows(w):
                n, t0, b0, nb = WAVES[w], T0[w], B0[w], BLOCKS[w]
                dve.wait_ge(r_place_ps, w + 1)
                bank = BK[7 - w]
                tot = bank[:, 8 * n:8 * n + 8]
                hop(dve.tensor_tensor(nb3[:, :, 0:n], tot.unsqueeze(2).to_broadcast((128, 8, n)),
                                      iota128[:, 0:n].unsqueeze(1).to_broadcast((128, 8, n)), ALU.is_gt))
                hop(dve.tensor_reduce(out=nblk[:], in_=nb3[:, :, 0:n], op=ALU.add, axis=AX.X))
                hop(dve.tensor_tensor(ex3[:], LT[:], nblk[:].unsqueeze(1).to_broadcast((128, 8, 8)), ALU.mult))
                hop(dve.tensor_reduce(out=exb[:], in_=ex3[:], op=ALU.add, axis=AX.X))
                hop(dve.tensor_tensor(eb3[:, 0:nb, :], iota[:, 0:nb].unsqueeze(2).to_broadcast((128, nb, 7)),
                                      exb[:, 1:8].unsqueeze(1).to_broadcast((128, nb, 7)), ALU.is_ge))
                hop(dve.tensor_reduce(out=ebf[:, 0:nb], in_=eb3[:, 0:nb, :], op=ALU.add, axis=AX.X))
                hop(dve.tensor_copy(eid[:, b0:b0 + nb], ebf[:, 0:nb]))
                hop(dve.scalar_tensor_tensor(out=place[:, 0:n], in0=exb[:].unsqueeze(1).to_broadcast((128, n, 8)), scalar=128.0,
                                             in1=bank[:, 0:8 * n].rearrange("p (t e) -> p t e", e=8), op0=ALU.mult, op1=ALU.add))
                for k in range(TOP):
                    hop(dve.tensor_tensor(sl3[:, 0:n], place[:, 0:n], pick[:, k, t0:t0 + n], ALU.mult))
                    hop(dve.tensor_reduce(out=slf[:, 0:n], in_=sl3[:, 0:n], op=ALU.add, axis=AX.X))
                    i = dve.tensor_copy(slot_u[:, k, t0:t0 + n], slf[:, 0:n])
                    if k == 0:
                        hop(i)
                i.then_inc(r_slots, 1)

            def take_weights(n, kind, e, half_):
                dve.wait_ge(f_w_ps, n + 1)
                bank = BK[n % 2]
                if kind == "w2":
                    dve.tensor_copy(w2T[:, e, 0:256], bank[:, 0:256])
                    dve.tensor_copy(w2T[0:KF[2], e, 256:384], bank[0:KF[2], 256:384]).then_inc(f_w_sb, 1)
                else:
                    dve.tensor_copy(w1T[:, e, :].rearrange("p (q k) -> p k q", k=8)[:, 4 * half_:4 * half_ + 4, :],
                                    bank[:, 0:4 * W1ROWS].rearrange("p (k q) -> p k q", k=4)).then_inc(f_w_sb, 1)

            def step2(t, u, on):
                def normalise(lin, dst):
                    o5 = AUX.rearrange("p (t c x) -> p t c x", t=4, c=4)
                    for c in range(2):
                        for hf in range(2):
                            th = 2 * c + hf
                            i = dve.tensor_tensor(dst[:, c, :].rearrange("p (q f g d) -> p q f g d", q=4, f=2, g=2)[:, :, hf],
                                                  o5[:, th, :, 0:16].rearrange("p q (g d) -> p q g d", g=2),
                                                  lin[:, th, :, :].unsqueeze(3).to_broadcast((128, 4, 2, D)), ALU.mult)
                    return i
                for slot in range(10):
                    if slot == 0 and "P" in on:
                        dve.wait_ge(c_xT_ps, count(t + 1))
                        dve.wait_ge(c_qv_ps, count(t))
                        dve.tensor_copy(xT[:], AUX[:, 0:256]).then_inc(c_xT_sb, 1)
                    if slot == 2 and "P" in on:
                        dve.wait_ge(c_qv_ps, count(t + 1))
                        dve.wait_ge(c_vp_sb, count(t * 2))
                        dve.wait_ge(c_qc_sb, count(t + 1))
                        dve.tensor_tensor(vsb[:], AUX[:, 256:512].rearrange("p (c f) -> p c f", c=2),
                                          bvx[:].unsqueeze(1).to_broadcast((128, 2, C)), ALU.add).then_inc(c_v_sb, 1)
                    if slot == 4 and "SB" in on:
                        b = t - 2
                        dve.wait_ge(c_mT_ps, count(b + 1))
                        dve.wait_ge(c_m_in, count(b * 64))
                        dve.tensor_scalar(mT[:, 0, :], AUX[0:4 * H, 0:128], -1.0, None, ALU.mult).then_inc(c_mT_sb, 1)
                        dve.wait_ge(c_mT_sb, count(b * 2 + 1))
                        dve.scalar_tensor_tensor(out=mT[:, 1, :], in0=AUX[0:4 * H, 0:128], scalar=-1.0, in1=mT[:, 0, :],
                                                 op0=ALU.mult, op1=ALU.subtract).then_inc(c_mT_sb, 1)
                    if slot == 5 and "E" in on:
                        b = t - 4
                        dve.wait_ge(c_oTs_ps, count(b + 1))
                        dve.reciprocal(linv[:], AUX.rearrange("p (t c x) -> p t c x", t=4, c=4)[:, :, :, 16:18]).then_inc(c_lin_sb, 1)
                        dve.wait_ge(c_lin_sb, count(b * 2 + 1))
                        dve.wait_ge(c_ctxT_ps, count(b))
                        normalise(linv, ctx).then_inc(c_ctx_sb, 1)
                    if slot == 6 and "E" in on:
                        b = t - 4
                        dve.wait_ge(c_oTx_ps, count(b + 1))
                        dve.reciprocal(linx[:], AUX.rearrange("p (t c x) -> p t c x", t=4, c=4)[:, :, :, 16:18]).then_inc(c_lin_sb, 1)
                        dve.wait_ge(c_lin_sb, count(b * 2 + 2))
                        normalise(linx, ctx2).then_inc(c_ctx2_sb, 1)
                        dve.wait_ge(c_ctx2_sb, count(b * 2 + 1))
                        dve.tensor_tensor(ctx[:], ctx[:], ctx2[:], ALU.add).then_inc(c_ctx2_sb, 1)
                    if slot == 8 and "E" in on:
                        b = t - 4
                        dve.wait_ge(c_y_ps, count(b + 1))
                        dve.wait_ge(c_xb_sb, count(b + 1))
                        dve.wait_ge(x2_sb, count(b * 2))
                        dve.tensor_tensor(r[:], AUX[:, 0:256].rearrange("p (c f) -> p c f", c=2), xb[:], ALU.add).then_inc(c_r_sb, 1)
                        dve.wait_ge(c_r_sb, count(b + 1))
                        dve.wait_ge(c_mv_sb, count(b * 2))
                        for c in range(2):
                            dve.bn_stats(st[:, c, :], r[:, c, :]).then_inc(c_st_sb, 1)
                        dve.wait_ge(c_st_sb, count(b * 2 + 2))
                        settle(dve)
                        for c in range(2):
                            dve.bn_aggr(mv[:, c, :], st[:, c, :]).then_inc(c_mv_sb, 1)
                    if slot == 9 and "E" in on:
                        b = t - 4
                        dve.wait_ge(c_rstd_sb, count(b + 1))
                        for c in range(2):
                            dve.tensor_scalar(X[:, b * 2 + c, :], r[:, c, :], mv[:, c, 0:1], rstd[:, c:c + 1],
                                              ALU.subtract, ALU.mult).then_inc(x2_sb, 1)
                    if slot in S2_SLOTS and S2_SLOTS[slot][0] in on:
                        stage, n0, n1 = S2_SLOTS[slot]
                        b = t - LAG[stage]
                        if n0 == 0:
                            dve.wait_ge(c_mT_ps, count(b))
                        for n in range(n0, n1):
                            dve.wait_ge(c_s_ps, count(b * 20 + (n + 1)))
                            if n < 16:
                                dve.tensor_reduce(out=M2[:, 2 * n:2 * n + 1], in_=Sps[n % 2][:, 0:128], op=ALU.max, axis=AX.X)
                                i = dve.tensor_reduce(out=M2[:, 2 * n + 1:2 * n + 2], in_=Sps[n % 2][:, 128:384], op=ALU.max, axis=AX.X)
                            else:
                                c = 32 + 8 * (n - 16)
                                i = dve.tensor_reduce(out=M2[:, c:c + 8], in_=Sps[n % 2].rearrange("p (g k) -> p g k", k=TK), op=ALU.max, axis=AX.X)
                            i.then_inc(c_max_sb, 1)
                    if isinstance(t, int):
                        for when, w, piece in ROUTE:
                            if when == (t, slot):
                                route(w, piece)
                        if (t, slot) == (17, 1):
                            place_rows(0)
                        for n, unit in enumerate(UNITS):
                            if unit[0] == (t, slot):
                                if n == 0:
                                    dve.wait_ge(c_parts_out, 16 * B)
                                    dve.wait_ge(c_split, 4 * B)
                                if n == 8:
                                    dve.wait_ge(c_st_ps, 10 * (B - 1))
                                if n == 18:
                                    dve.wait_ge(c_st_ps, 10 * B)
                                take_weights(n, *unit[1:])
            run(dve, step2, B + 5)
            dve.wait_ge(r_slots, 1)
            for piece in range(5):
                route(1, piece)
            place_rows(1)

            def copy_xT(g, p):
                dve.wait_ge(b_xT_ps, count(g + 1))
                dve.wait_ge(b_h_ps, count(g * 4 - 4))
                dve.tensor_copy(xbT[p][:].rearrange("p a b -> p (a b)"), BK[7]).then_inc(b_xT_sb, 1)

            def copy_y(j, u, h, p):
                dve.wait_ge(b_y_ps, count(j + 1))
                if u == 0:
                    dve.wait_ge(b_y_out[p], count(h * 16))
                dve.tensor_copy(ysb[p][:, u, :], BK[6][:, 0:128]).then_inc(b_y_sb, 1)

            def step(g, h, p, more=True):
                for u in range(4):
                    j = g * 4 + u
                    dve.wait_ge(b_sa, count(j + 1))
                    dve.wait_ge(b_heT_ps, count(j - 1))
                    dve.tensor_tensor(he[u % 2][:], sa[u % 2][:], BK[2 + u % 2][:, 0:FF], ALU.mult).then_inc(b_he, 1)
                    if u >= 2:
                        copy_y(j - 2, u - 2, h, p)
                    elif not (isinstance(j, int) and j < 2):
                        copy_y(j - 2, u + 2, h, 1 - p)
                    if u == 1 and more:
                        copy_xT(g + 1, 1 - p)
            copy_xT(0, 0)
            for g in range(2):
                step(g, g // 2, g % 2)
            span(dve, 2, NG - 2, step)
            step(NG - 2, NG // 2 - 1, 0)
            step(NG - 1, NG // 2 - 1, 1, more=False)
            copy_y(NBK - 2, 2, 0, 1)
            copy_y(NBK - 1, 3, 0, 1)

            for k in range(NTT // 4):
                q = k % NRG
                dve.wait_ge(g_in[q], (k // NRG + 1) * 128)
                if k:
                    dve.wait_ge(g_yo, 4 * k)
                    dve.wait_ge(g_mv, 4 * k)
                for r_ in range(TOP):
                    for t in range(4):
                        i = dve.scalar_tensor_tensor(out=acc[:, t, :], in0=gat[q][:, r_, t, :], scalar=cw[:, r_, 4 * k + t:4 * k + t + 1],
                                                     in1=(X[:, 4 * k + t, :] if r_ == 0 else acc[:, t, :]), op0=ALU.mult, op1=ALU.add)
                        if r_ == 0:
                            i.then_inc(g_half, 1)
                    if r_ == 0:
                        dve.wait_ge(g_half, 4 * k + 4)
                i.then_inc(g_acc, 1)
                dve.wait_ge(g_acc, k + 1)
                for t in range(4):
                    dve.bn_stats(st4[:, t, :], acc[:, t, :]).then_inc(g_st, 1)
                dve.wait_ge(g_st, 4 * k + 4)
                for t in range(4):
                    dve.bn_aggr(mv4[:, t, :], st4[:, t, :]).then_inc(g_mv, 1)
                dve.wait_ge(g_rs, k + 1)
                if k:
                    dve.wait_ge(g_out, 16 * k)
                for t in range(4):
                    dve.tensor_scalar(yo[:, t, :], acc[:, t, :], mv4[:, t, 0:1], rs4[:, t:t + 1], ALU.subtract, ALU.mult).then_inc(g_yo, 1)

        @block.gpsimd
        def _(pool):
            pool.memset(ident[:], 0.0).then_inc(ident_ok, 1)
            pool.wait_ge(ident_ok, 1)
            pool.affine_select(out=ident[:], in_=ident[:], compare_op=ALU.not_equal, fill=1.0, base=0, pattern=[[-1, 128]],
                               channel_multiplier=1).then_inc(ident_ok, 1)
            pool.wait_ge(ident_ok, 2)
            pool.memset(maskq[:], 0.0).then_inc(mask_ok, 1)
            pool.memset(maskk[:], 0.0).then_inc(mask_ok, 1)
            pool.wait_ge(mask_ok, 2)
            for m, sign in ((maskq, 1), (maskk, -1)):
                pool.affine_select(out=m[:], in_=m[:], compare_op=ALU.is_ge, fill=-1e38, base=0, pattern=[[-sign, 128]],
                                   channel_multiplier=sign).then_inc(mask_ok, 1)
            pool.tensor_copy(identb[:], ident[:]).then_inc(mask_ok, 1)
            pool.memset(half[:], -0.5).then_inc(mask_ok, 1)
            pool.wait_ge(cA_in, 64)
            for i in range(4):
                pool.wait_ge(x_in[i], 16)

            def step(t, u, on):
                if "E" in on:
                    b = t - 4
                    pool.wait_ge(r_sb, count(b))
                    pool.tensor_tensor(xb[:], X[:, bass.ds(b * 2, 2), :] if not isinstance(b, int) else X[:, 2 * b:2 * b + 2, :],
                                       boA[:].unsqueeze(1).to_broadcast((128, 2, C)), ALU.add).then_inc(xb_sb, 1)
                if "P" in on:
                    pool.wait_ge(qk_sb, count(t * 2 + 2))
                    pool.wait_ge(parts_out, count(t * 16))
                    settle(pool)
                    pool.tensor_copy(parts[:, 0:6:3, :], qk32[:]).then_inc(split, 1)
                    pool.wait_ge(split, count(t * 4 + 1))
                    pool.tensor_tensor(res[:], qk32[:], parts[:, 0:6:3, :], ALU.subtract).then_inc(split, 1)
                    pool.wait_ge(split, count(t * 4 + 2))
                    settle(pool)
                    pool.tensor_copy(parts[:, 1:6:3, :], res[:]).then_inc(split, 1)
                    pool.wait_ge(split, count(t * 4 + 3))
                    pool.tensor_tensor(parts[:, 2:6:3, :], res[:], parts[:, 1:6:3, :], ALU.subtract).then_inc(split, 1)
                if "E" in on:
                    b = t - 4
                    pool.wait_ge(mv_sb, count(b * 2 + 2))
                    pool.wait_ge(rstd_sb, count(b))
                    settle(pool)
                    pool.tensor_scalar(ve[:], mv[:, :, 1], EPS, None, ALU.add).then_inc(ve_sb, 1)
                    pool.wait_ge(ve_sb, count(b + 1))
                    pool.wait_ge(x1_sb, count(b * 2))
                    pool.tensor_tensor(rstd[:], ve[:], half[:], ALU.pow).then_inc(rstd_sb, 1)
            for k in range(NBUF):
                pool.memset(Vp[k][:], 0.0).then_inc(vp_ok, 1)
                pool.memset(VCp[k][:], 0.0).then_inc(vp_ok, 1)
            pool.wait_ge(vp_ok, 2 * NBUF)
            for k in range(NBUF):
                v = Vp[k][:].rearrange("p t (m g) x -> p (t m) g x", g=2)
                for g in range(2):
                    pool.memset(v[:, :, g, 16 + g:17 + g], 1.0).then_inc(vp_ok, 1)
                pool.memset(Kcs[k][0:96, :], 0.0).then_inc(vp_ok, 1)
            pool.memset(onesb[:], 1.0).then_inc(f_const, 1)
            pool.memset(trib[:], 1.0).then_inc(f_const, 1)
            pool.memset(LT[:], 1.0).then_inc(f_const, 1)
            pool.iota(iota_i[:], [[1, 64]], base=0, channel_multiplier=0).then_inc(f_const, 1)
            pool.wait_ge(f_const, 4)
            pool.affine_select(out=trib[:], in_=trib[:], compare_op=ALU.is_ge, fill=0.0, base=-1, pattern=[[1, 128]],
                               channel_multiplier=-1).then_inc(f_const, 1)
            pool.affine_select(out=LT[:], in_=LT[:], compare_op=ALU.is_ge, fill=0.0, base=-1, pattern=[[1, 8], [-1, 8]],
                               channel_multiplier=0).then_inc(f_const, 1)
            pool.tensor_copy(iota[:], iota_i[:]).then_inc(f_const, 1)
            pool.wait_ge(f_const, 7)
            pool.tensor_scalar(iota128[:], iota[:, 0:32], 128.0, None, ALU.mult).then_inc(f_const, 1)
            pool.memset(half4[:], -0.5).then_inc(f_const, 1)
            run(pool, step, B + 4)

            SENT0 = (0, 8, 14, 20, 26)

            def send(w, lo, hi):
                for n in range(lo, hi):
                    t, k = T0[w] + n // TOP, n % TOP
                    pool.indirect_dma_start(xs[w], bass.IndirectOffsetOnAxis(ap=slot_u[:, k, t:t + 1], axis=0), X[:, t, :], None).then_inc(x_sent[w], 16)

            def step2(t, u, on):
                if "P" in on:
                    pool.wait_ge(x1_sb, count(t * 2 + 2)) if isinstance(t, int) else None
                    pool.wait_ge(c_xT_ps, count(t))
                    settle(pool)
                    src = X[:, 2 * t:2 * t + 2, :] if isinstance(t, int) else X[:, bass.ds(t * 2, 2), :]
                    pool.tensor_copy(x2in[:], src).then_inc(c_x2in, 1)
                if "E" in on:
                    b = t - 4
                    pool.wait_ge(c_r_sb, count(b))
                    pool.tensor_tensor(xb[:], X[:, bass.ds(b * 2, 2), :] if not isinstance(b, int) else X[:, 2 * b:2 * b + 2, :],
                                       bpx[:].unsqueeze(1).to_broadcast((128, 2, C)), ALU.add).then_inc(c_xb_sb, 1)
                if "L" in on:
                    b = t - 1
                    pool.wait_ge(c_v_sb, count(b + 1))
                    pool.wait_ge(c_pv_ps, count(b * 6 - 12))
                    settle(pool)
                    vd = Vp[(u - 1) % 3][:].rearrange("p t (m g) x -> p (t m) g x", g=2)
                    vs = vsb[:].rearrange("p t (m g d) -> p (t m) g d", g=2, d=D)
                    for g in range(2):
                        pool.tensor_copy(vd[:, :, g, 8 * g:8 * g + 8], vs[:, :, g, :]).then_inc(c_vp_sb, 1)
                if "P" in on:
                    p3 = parts3[:].rearrange("p (g a) t -> p g a t", a=3)
                    pool.wait_ge(c_qk_sb, count(t * 2 + 2))
                    pool.wait_ge(c_qc_sb, count(t + 1))
                    pool.wait_ge(c_parts_out, count(t * 16))
                    settle(pool)
                    pool.tensor_copy(p3[:, :, 0, :], qkc32[:]).then_inc(c_split, 1)
                    pool.wait_ge(c_split, count(t * 4 + 1))
                    pool.tensor_tensor(res3[:], qkc32[:], p3[:, :, 0, :], ALU.subtract).then_inc(c_split, 1)
                    pool.wait_ge(c_split, count(t * 4 + 2))
                    settle(pool)
                    pool.tensor_copy(p3[:, :, 1, :], res3[:]).then_inc(c_split, 1)
                    pool.wait_ge(c_split, count(t * 4 + 3))
                    pool.tensor_tensor(p3[:, :, 2, :], res3[:], p3[:, :, 1, :], ALU.subtract).then_inc(c_split, 1)
                if isinstance(t, int) and t in (18, 19):
                    send(0, SENT0[2 * t - 35], SENT0[2 * t - 34])
                if "E" in on:
                    b = t - 4
                    pool.wait_ge(c_mv_sb, count(b * 2 + 2))
                    pool.wait_ge(c_rstd_sb, count(b))
                    settle(pool)
                    pool.tensor_scalar(ve[:], mv[:, :, 1], EPS, None, ALU.add).then_inc(c_ve_sb, 1)
                    pool.wait_ge(c_ve_sb, count(b + 1))
                    pool.wait_ge(x2_sb, count(b * 2))
                    pool.tensor_tensor(rstd[:], ve[:], half[:], ALU.pow).then_inc(c_rstd_sb, 1)
                if isinstance(t, int) and t in (17, 18, 19):
                    if t == 17:
                        pool.wait_ge(r_slots, 1)
                        pool.wait_ge(zeroed, 16 * 5)
                    send(0, SENT0[(t - 17) * 2], SENT0[(t - 17) * 2 + 1]) if t < 19 else None
            pool.wait_ge(x1_sb, 2 * B)
            pool.wait_ge(cx_in, 144)
            pool.wait_ge(v_out, 32 * B)
            run(pool, step2, B + 5)
            send(0, SENT0[-1], TOP * WAVES[0])
            pool.wait_ge(r_slots, 2)
            send(1, 0, TOP * WAVES[1])
            def norm(k):
                pool.wait_ge(g_mv, 4 * k + 4)
                if k:
                    pool.wait_ge(g_rs, k)
                pool.tensor_scalar(ve4[:], mv4[:, :, 1], EPS, None, ALU.add).then_inc(g_ve, 1)
                pool.wait_ge(g_ve, k + 1)
                if k:
                    pool.wait_ge(g_yo, 4 * k)
                pool.tensor_tensor(rs4[:], ve4[:], half4[:], ALU.pow).then_inc(g_rs, 1)
            done = 0
            for k in range(NTT // 4):
                q = k % NRG
                w = int(4 * k >= T0[1])
                last = BLOCKS[0] // 4 if w == 0 else NG
                pool.wait_ge(b_y_out[0], 16 * ((last + 1) // 2))
                pool.wait_ge(b_y_out[1], 16 * (last // 2))
                if k >= NRG:
                    pool.wait_ge(g_acc, k - NRG + 1)
                for t in range(4):
                    for r_ in range(TOP):
                        pool.indirect_dma_start(gat[q][:, r_, t, :], None, ys[w], bass.IndirectOffsetOnAxis(ap=slot_u[:, r_, 4 * k + t:4 * k + t + 1], axis=0)).then_inc(g_in[q], 16)
                if k > 0:
                    norm(k - 1)
            norm(NTT // 4 - 1)

        @block.sync
        def _(sp):
            xv = x.rearrange("b (c p) f -> p (b c) f", p=128)
            sp.dma_start(WnatA[:, 0:3, :], aW.rearrange("(c p) e -> p c e", p=128)).then_inc(wA_in, 16)
            sp.dma_start(WnatA[:, 3, :], aWo).then_inc(wA_in, 16)
            for i in range(4):
                n = B * NT // 4
                sp.dma_start(X[:, n * i:n * i + n, :], xv[:, n * i:n * i + n, :]).then_inc(x_in[i], 16)
            bx = ab.rearrange("(j x) -> x j", x=24)
            for a in range(2):
                sp.dma_start(bqkA[:, a:a + 1], bx[8 * a:8 * a + 8, :], allow_slow_non_contiguous=True).then_inc(cA_in, 16)
            sp.dma_start(bvA[:].rearrange("p (j d) -> p j d", d=8), ab.rearrange("(j x) -> j x", x=24)[:, 16:24].unsqueeze(0).to_broadcast((128, 16, 8))).then_inc(cA_in, 16)
            sp.dma_start(boA[:], abo.unsqueeze(0).to_broadcast((128, C))).then_inc(cA_in, 16)
            for n, name in enumerate(("Wq", "Wk", "Wcq", "Wv", "Wp")):
                sp.dma_start(Wx[:, n, :], W[name]).then_inc(wx_in, 16)
            sp.dma_start(cin, ctx_in.rearrange("(n u) t c -> (u t) n c", u=2)).then_inc(cin_in, 16)
            sp.dma_start(Wckr[:, 0, :], W["Wck"]).then_inc(cx_in, 16)
            sp.dma_start(Wckr[:, 1, :], W["Wcv"]).then_inc(cx_in, 16)
            for n, name in enumerate(("bq", "bk", "bcq", "bck")):
                sp.dma_start(bx3[:, n:n + 1], W[name].rearrange("(h d) -> d h", d=D), allow_slow_non_contiguous=True).then_inc(cx_in, 16)
            for tile, name in ((bvx, "bv"), (bcvx, "bcv"), (bpx, "bp")):
                sp.dma_start(tile[:], W[name].unsqueeze(0).to_broadcast((128, C))).then_inc(cx_in, 16)
            sp.wait_ge(kc_split, 5)
            for a in range(3):
                sp.dma_start(scr_kc[a].rearrange("b p t -> p b t"), kcp[:, a, :].rearrange("p (b t) -> p b t", t=TK)).then_inc(kc_out, 16)
            sp.wait_ge(vc_sb, 1)
            sp.dma_start(scr_vc.rearrange("(n p) c -> p n c", p=128), vc32.rearrange("p (n c) -> p n c", c=C)).then_inc(vc_out, 16)
            sp.wait_ge(zero_ok, 6 * NBUF)
            sp.wait_ge(vp_ok, 5 * NBUF + 2 * NBUF)
            sp.wait_ge(ident_ok, 2)
            rows1 = scr_qk.rearrange("a (d j) t -> (a d) (j t)", d=8)
            sp.dma_start(wrr[:], rwqkv).then_inc(f_wr_in, 16)

            def step(t, u, on):
                if "P" in on:
                    sp.wait_ge(xT_ps, count(t - 2))
                    settle(sp)
                    sp.wait_ge(xin_in, count(t * 16))
                    settle(sp)
                    settle(sp)
                    sp.dma_start(xin[u][:], (x[t] if isinstance(t, int) else x[bass.ds(t, 1)].rearrange("o n f -> (o n) f")).rearrange("(c p) f -> p c f", p=128)).then_inc(xin_in, 16)
                if "L" in on:
                    b = t - 1
                    k = (u - 1) % 3
                    sp.wait_ge(parts_out, count(b * 16 + 16))
                    settle(sp)
                    sp.wait_ge(v_out, count(b * 32 + 32))
                    settle(sp)
                    sp.wait_ge(stacks_in, count(b * 96))
                    settle(sp)
                    sp.wait_ge(v_in, count(b * 64))
                    settle(sp)
                    sp.wait_ge(st_ps, count(b * 8 - 16))
                    settle(sp)
                    for n, o in ((3, 0), (2, 24), (1, 40)):
                        sp.dma_start(Qs[k][o:o + 8 * n, :], rows1[0:8 * n, :]).then_inc(stacks_in, 16)
                        a = (3 - n) * 8 + 24
                        sp.dma_start(Ks[k][o:o + 8 * n, :], rows1[a:a + 8, :].unsqueeze(0).to_broadcast((n, 8, H * T))).then_inc(stacks_in, 16)
                    sp.wait_ge(pv_ps, count(b * 4 - 8))
                    settle(sp)
                    vr = scr_v.rearrange("(kt j) (i m g) d -> kt g (j i) m d", kt=2, i=16, g=2)
                    for kt in range(2):
                        for g in range(2):
                            dst = Vp[k][:, kt, :, :].rearrange("p (m g) x -> p m g x", g=2)[:, :, g, 8 * g:8 * g + 8]
                            sp.dma_start(dst, vr[kt, g]).then_inc(v_in, 16)
                if "P" in on:
                    sp.wait_ge(v_sb, count(t + 1))
                    settle(sp)
                    sp.wait_ge(v_in, count(t * 64))
                    settle(sp)
                    for c in range(2):
                        sp.dma_start(scr_v[:, 128 * c:128 * c + 128, :].rearrange("j p d -> p j d"),
                                     vsb[:, c, :].rearrange("p (j d) -> p j d", d=8)).then_inc(v_out, 16)
                if "SB" in on:
                    b = t - 2
                    k = (u - 2) % 3
                    sp.wait_ge(mb_sb, count(b * 2 + 2))
                    settle(sp)
                    sp.wait_ge(m_in, count(b * 64))
                    settle(sp)
                    for c in range(2):
                        for f in range(2):
                            sp.dma_start(Qs[k][MROW + c:MROW + c + 1, 2048 * f:2048 * f + 2048].rearrange("o (q h) -> o q h", h=H),
                                         Mb[:, c, 16 * f:16 * f + 16]).then_inc(m_in, 16)
                if "P" in on:
                    sp.wait_ge(split, count(t * 4 + 4))
                    settle(sp)
                    sp.wait_ge(stacks_in, count(t * 96))
                    settle(sp)
                    sp.dma_start(scr_qk.rearrange("a p t -> p a t"), parts[:]).then_inc(parts_out, 16)
                if isinstance(t, int) and t >= B - 1:
                    sp.wait_ge(f_zero, 1)
                    n = (t - (B - 1)) * 16
                    for w in range(2):
                        lo, hi = max(n, B0[w]), min(n + 16, B0[w] + BLOCKS[w])
                        if lo < hi:
                            sp.dma_start(xs[w].rearrange("(b p) f -> p b f", p=128)[:, lo - B0[w]:hi - B0[w], :],
                                         zrow[:].unsqueeze(1).to_broadcast((128, hi - lo, C))).then_inc(zeroed, 16)
            run(sp, step, B + 4)
            for i in range(2):
                sp.dma_start(w2r[:, 4 * i:4 * i + 4, :], w2[4 * i:4 * i + 4].rearrange("e c f -> c e f")).then_inc(f_w2_in, 16)
            sp.wait_ge(kc_out, 48)
            sp.wait_ge(vc_out, 16)
            rows2 = scr_qkc.rearrange("a (d h) t -> (a d) (h t)", d=D)

            def step2(t, u, on):
                if "L" in on:
                    b = t - 1
                    k = (u - 1) % 3
                    sp.wait_ge(c_parts_out, count(b * 16 + 16))
                    settle(sp)
                    sp.wait_ge(c_stacks_in, count(b * 224))
                    settle(sp)
                    sp.wait_ge(c_st_ps, count(b * 10 - 20))
                    settle(sp)
                    for n, o in ((3, 0), (2, 24), (1, 40)):
                        sp.dma_start(Qs[k][o:o + 8 * n, :], rows2[0:8 * n, :]).then_inc(c_stacks_in, 16)
                        sp.dma_start(Qcs[k][o:o + 8 * n, :], rows2[48:48 + 8 * n, :]).then_inc(c_stacks_in, 16)
                        a = (3 - n) * 8 + 24
                        sp.dma_start(Ks[k][o:o + 8 * n, :], rows2[a:a + 8, :].unsqueeze(0).to_broadcast((n, 8, H * T))).then_inc(c_stacks_in, 16)
                        kb = (scr_kc[3 - n][b] if isinstance(b, int) else scr_kc[3 - n][bass.ds(b, 1)].rearrange("o p t -> (o p) t")).rearrange("(d h) t -> d (h t)", d=D)
                        sp.dma_start(Kcs[k][o:o + 8 * n, :], kb.unsqueeze(0).to_broadcast((n, 8, H * TK))).then_inc(c_stacks_in, 16)
                    sp.wait_ge(c_pv_ps, count(b * 6 - 12))
                    settle(sp)
                    vb = scr_vc[bass.ds(b * TK, TK)] if not isinstance(b, int) else scr_vc[b * TK:b * TK + TK]
                    vb = vb.rearrange("t (m g d) -> g t m d", g=2, d=D)
                    for g in range(2):
                        sp.dma_start(VCp[k][64 * g:64 * g + 64, :, 8 * g:8 * g + 8], vb[g]).then_inc(c_stacks_in, 16)
                if "SB" in on:
                    b = t - 2
                    k = (u - 2) % 3
                    sp.wait_ge(c_mT_sb, count(b * 2 + 2))
                    settle(sp)
                    sp.wait_ge(c_m_in, count(b * 64))
                    settle(sp)
                    for c in range(2):
                        for stack, o in ((Qs, 0), (Qcs, 2 * H)):
                            sp.dma_start(stack[k][MROW + c:MROW + c + 1, :].rearrange("o (r q) -> o r q", q=128),
                                         mT[o:o + 2 * H, c, :]).then_inc(c_m_in, 16)
                if "P" in on:
                    sp.wait_ge(c_split, count(t * 4 + 4))
                    settle(sp)
                    sp.wait_ge(c_stacks_in, count(t * 224))
                    settle(sp)
                    sp.dma_start(scr_qkc.rearrange("a p t -> p a t"), parts3[:]).then_inc(c_parts_out, 16)
                if isinstance(t, int) and t in (17, 18):
                    sp.wait_ge(c_st_ps, 10 * (B - 2) if t == 17 else 10 * (B - 1))
                    for n, e0, ne in (((1, 3, 2), (2, 5, 2)) if t == 17 else ((3, 7, 1), (4, 2, 1), (5, 0, 2))):
                        st_, o = W1R[e0]
                        sp.dma_start(f32(st_[:])[0:W1ROWS, o:o + 1024 * ne].rearrange("p (e x) -> p e x", e=ne),
                                     w1[e0:e0 + ne].rearrange("e (p k) c -> p e (k c)", k=8)).then_inc(f_w1_in[n - 1], 16)
            sp.wait_ge(st_ps, 8 * B)
            sp.wait_ge(pv_ps, 4 * B)
            run(sp, step2, B + 5)
            def rows(t, g):
                a = t.rearrange("(g b p) f -> g p b f", b=4, p=128)
                return a[g] if isinstance(g, int) else a[bass.ds(g, 1)].rearrange("o p b f -> (o p) b f")

            def load(g, p, w):
                sp.wait_ge(b_xT_ps, count(g - 1)) if not isinstance(g, int) or g >= 2 else None
                settle(sp)
                sp.dma_start(xblk[p][:], rows(xs[w], g - w * GW0)).then_inc(b_x_in[p], 16)

            def store(g, p, w):
                sp.wait_ge(b_y_sb, count(g * 4 + 4))
                settle(sp)
                sp.dma_start(rows(ys[w], g - w * GW0), ysb[p][:]).then_inc(b_y_out[p], 16)
            sp.wait_ge(x_sent[0], 16 * TOP * WAVES[0])
            sp.wait_ge(c_pv_ps, 6 * B)
            load(0, 0, 0)
            load(1, 1, 0)

            def step(lw, sw):
                def _(g, h, p):
                    if lw is not None:
                        load(g + 2, p, lw)
                    store(g, p, sw)
                return _
            span(sp, 0, GW0 - 2, step(0, 0))
            sp.wait_ge(x_sent[1], 16 * TOP * WAVES[1])
            span(sp, GW0 - 2, GW0, step(1, 0))
            span(sp, GW0, NG - 2, step(1, 1))
            span(sp, NG - 2, NG, step(None, 1))
            ov = out.rearrange("(k b) (c p) f -> k p (b c) f", b=2, p=128)
            for k in range(NTT // 4):
                sp.wait_ge(g_yo, 4 * k + 4)
                sp.dma_start(ov[k], yo[:]).then_inc(g_out, 16)
            sp.wait_ge(g_out, 16 * (NTT // 4))



def kernel(**inputs):
    import concourse.bacc as bacc
    from concourse.bass_utils import run_bass_kernel_spmd
    nc = bacc.Bacc("TRN2", target_bir_lowering=False, num_devices=1)
    arrays, a = {}, {}
    for name, value in inputs.items():
        arrays[name] = np.ascontiguousarray(value)
        a[name] = nc.dram_tensor(name, arrays[name].shape, mybir.dt.from_np(arrays[name].dtype), kind="ExternalInput").ap()
    out = nc.dram_tensor("out", arrays["x"].shape, F32, kind="ExternalOutput").ap()
    cross = {k.removeprefix("L0_xattn_"): v for k, v in a.items() if k.startswith("L0_xattn_")}
    decoder_layer(nc, a["x"], a["ctx_512"], a["L0_attn_W_qkv"], a["L0_attn_b_qkv"], a["L0_attn_W_out"], a["L0_attn_b_out"],
                  cross, None, a["L0_ffn_wqkv"], a["L0_ffn_w1"], a["L0_ffn_w2"], out)
    return run_bass_kernel_spmd(nc, [arrays], core_ids=[0]).results[0]["out"]
```

```python
from contextlib import ExitStack
import numpy as np
import concourse.bass as bass
from concourse import mybir

F32, BF16, I32, U32 = mybir.dt.float32, mybir.dt.bfloat16, mybir.dt.int32, mybir.dt.uint32
ALU = mybir.AluOpType
ACT = mybir.ActivationFunctionType
AX = mybir.AxisListType


def decoder_layer(nc, x, ctx_in, aW, ab, aWo, abo, W, rwqkv, w1, w2, out):
    B, T, C = x.shape
    H, D = 16, C // 16
    NT = T // 128
    SCALE = float(1.0 / np.sqrt(np.float32(D)))
    EPS = 1e-5
    KS, MROW = 96, 96
    NBUF = 3

    es = ExitStack()
    with es:
        def sb(name, shape, dt=F32):
            return es.enter_context(nc.sbuf_tensor(name, shape, dt))

        def sem(name):
            return es.enter_context(nc.semaphore(name))

        X = sb("X", [128, B * NT, C])
        ident = sb("ident", [128, 128])
        half = sb("half", [128, NT])
        arena1 = sb("arena1", [128, 4160])
        taken = [0]

        def part(arena, cols, dt=F32, size=None):
            a = arena[:, taken[0]:taken[0] + cols]
            taken[0] += cols
            assert taken[0] <= arena.shape[1], (taken[0], arena.shape)
            return a if dt == F32 else a.bitcast(dt)
        WnatA = part(arena1, 512).rearrange("p (a b) -> p a b", b=128)
        WTA = part(arena1, 512)
        bvA = part(arena1, C)
        boA = part(arena1, C)
        WqkA = part(arena1, 2 * C).rearrange("p (a b) -> p a b", b=C)
        xin = [part(arena1, NT * C).rearrange("p (a b) -> p a b", b=C) for i in range(3)]
        qk32 = part(arena1, 2 * T).rearrange("p (a b) -> p a b", b=T)
        res = part(arena1, 2 * T).rearrange("p (a b) -> p a b", b=T)
        parts = part(arena1, 3 * T, BF16).rearrange("p (a b) -> p a b", b=T)
        M = part(arena1, NT * H).rearrange("p (a b) -> p a b", b=H)
        Mb = part(arena1, NT * H, BF16).rearrange("p (a b) -> p a b", b=NT * H)
        bqkA = sb("bqkA", [128, 2])
        stackQ = sb("stackQ", [128, NBUF * H * T], BF16)
        stackK = sb("stackK", [128, NBUF * H * T], BF16)
        Qs = [stackQ[:, H * T * i:H * T * (i + 1)] for i in range(NBUF)]
        Ks = [stackK[:, H * T * i:H * T * (i + 1)] for i in range(NBUF)]
        Vp = [sb(f"Vp{i}", [128, 2, H, 32]) for i in range(NBUF)]
        xT = sb("xT", [128, T])
        vsb = sb("vsb", [128, NT, C])
        arenaP = sb("arenaP", [128, 5 * 4 * T])
        P = [arenaP[:, 4 * T * i:4 * T * (i + 1)].rearrange("p (a b c) -> p a b c", a=2, b=2) for i in range(5)]
        TK = ctx_in.shape[1]
        CK = ctx_in.shape[2]
        stackQc = sb("stackQc", [128, NBUF * H * T], BF16)
        stackKc = sb("stackKc", [128, NBUF * H * TK], BF16)
        Qcs = [stackQc[:, H * T * i:H * T * (i + 1)] for i in range(NBUF)]
        Kcs = [stackKc[:, H * TK * i:H * TK * (i + 1)] for i in range(NBUF)]
        VCp = [sb(f"VCp{i}", [128, H // 2, 32]) for i in range(NBUF)]
        identb = sb("identb", [128, 128], BF16)
        maskq = sb("maskq", [128, 128], BF16)
        maskk = sb("maskk", [128, 128], BF16)
        Wx = sb("Wx", [128, 5, C])
        Wqkc = sb("Wqkc", [128, 3, C])
        Wckr = sb("Wckr", [CK, 2, C])
        Wckp = sb("Wckp", [CK, C])
        bx3 = sb("bx3", [128, 4])
        bvx = sb("bvx", [128, C])
        bcvx = sb("bcvx", [128, C])
        bpx = sb("bpx", [128, C])
        arena2 = sb("arena2", [128, 8 * 3 * C])
        taken[0] = 0
        x2in = part(arena2, NT * C).rearrange("p (a b) -> p a b", b=C)
        qkc32 = part(arena2, 3 * T).rearrange("p (a b) -> p a b", b=T)
        res3 = part(arena2, 3 * T).rearrange("p (a b) -> p a b", b=T)
        parts3 = part(arena2, 9 * T // 2, BF16).rearrange("p (a b) -> p a b", b=T)
        M2 = sb("M2", [128, 4 * H])
        mT = sb("mT", [4 * H, 2, 128], BF16)
        OTx = sb("OTx", [128, 2, T])
        linx = sb("linx", [128, 4, 4, 2])
        ctx2 = sb("ctx2", [128, NT, C])
        cin = P[0][:].rearrange("p a b c -> p (a b c)")[:, 0:512].rearrange("p (n c) -> p n c", n=8)
        cT = P[1][:].rearrange("p a b c -> p (a b c)")[0:CK, :]
        kc32 = P[2][:].rearrange("p a b c -> p (a b c)")
        rc32 = P[3][:].rearrange("p a b c -> p (a b c)")
        vc32 = P[4][:].rearrange("p a b c -> p (a b c)")
        kcp = sb("kcp", [128, 3, B * TK], BF16)
        E_, F2 = w1.shape[0], w1.shape[1]
        FF = F2 // 2
        KF = (128, 128, FF - 256)
        NC = 8
        WAVES = (18, 14)
        TOP = 2
        G4 = 4
        BLOCKS = [-(-(TOP * n + E_ - 1) // G4) * G4 for n in WAVES]
        NTT = B * NT
        NBK = sum(BLOCKS)
        NG, GW0 = NBK // G4, BLOCKS[0] // G4
        T0 = (0, WAVES[0])
        B0 = (0, BLOCKS[0])
        NW = max(WAVES)
        NK = NTT // 2
        NCH = 24
        f32 = lambda t: t.bitcast(F32)
        W1R = {6: (stackQ, 4096), 7: (stackQ, 5120), 0: (stackQc, 4096), 1: (stackQc, 5120),
               2: (stackQ, 0), 3: (stackQ, 1024), 4: (stackQc, 0), 5: (stackQc, 1024)}
        W1ROWS = F2 // 8
        w1r = {e: f32(t[:])[0:W1ROWS, o:o + 8 * C].rearrange("p (k c) -> p k c", c=C) for e, (t, o) in W1R.items()}
        w1T = f32(stackK[:])[:, 0:E_ * F2].rearrange("p (e f) -> p e f", e=E_)
        w2T = arena2[:].rearrange("p (e f) -> p e f", e=E_)
        w2r = sb("w2r", [128, E_, FF])
        taken[0] = 0
        A = part(arena1, NW * 64).rearrange("p (t a b) -> p t a b", a=8, b=8)
        G = part(arena1, NW * 32, BF16).rearrange("p (t a b) -> p t a b", a=8, b=8)
        EQ = part(arena1, NW * 32, BF16).rearrange("p (t a b) -> p t a b", a=8, b=8)
        mx = part(arena1, NTT * 24).rearrange("p (t c) -> p t c", c=24)
        rxin = part(arena1, NT * C).rearrange("p (a b) -> p a b", b=C)
        rxT = part(arena1, NT * C)
        taken[0] = 0
        xblk = [part(arenaP, 512).rearrange("p (a b) -> p a b", b=C) for i in range(2)]
        xbT = [part(arenaP, 512).rearrange("p (a b) -> p a b", b=C) for i in range(2)]
        ysb = [part(arenaP, 512).rearrange("p (a b) -> p a b", b=C) for i in range(2)]
        sa = [part(arenaP, FF) for i in range(2)]
        he = [part(arenaP, FF) for i in range(2)]
        heT = [f32(stackKc[:])[:, 384 * i:384 * i + 384].rearrange("p (a b) -> p a b", b=128) for i in range(2)]
        gat = [f32((stackQ, stackQc)[i // 12][:])[:, 512 * (i % 12):512 * (i % 12) + 512].rearrange("p (a b c) -> p a b c", a=2, b=2)
               for i in range(NK)]
        acc = [f32(stackQc[:])[:, 3072 + 256 * i:3328 + 256 * i].rearrange("p (a b) -> p a b", b=C) for i in range(2)]
        yo = [f32(stackQc[:])[:, 3584 + 256 * i:3840 + 256 * i].rearrange("p (a b) -> p a b", b=C) for i in range(2)]
        ZEROS = [(w, lo, min(lo + 16, BLOCKS[w])) for w in range(2) for lo in range(0, BLOCKS[w], 16)]
        wrr = sb("wrr", [24, C])
        wrT = sb("wrT", [C, 24])
        LT = sb("LT", [128, 8, 8])
        mr = sb("mr", [128, NW, 8])
        den = sb("den", [128, NW, 8])
        num = sb("num", [128, NW, 8])
        lg = sb("lg", [128, NW, 8])
        rank = sb("rank", [128, NW, 8])
        m0 = sb("m0", [128, NW])
        pick = sb("pick", [128, 2, NTT, 8])
        both = sb("both", [128, NTT, 8], BF16)
        cw = sb("cw", [128, 2, NTT])
        iota_i = sb("iota_i", [128, 64], I32)
        iota = sb("iota", [128, 64])
        iota128 = sb("iota128", [128, 32])
        trib = sb("trib", [128, 128], BF16)
        onesb = sb("onesb", [128, 128], BF16)
        nb3 = sb("nb3", [128, 8, NW])
        nblk = sb("nblk", [128, 8])
        ex3 = sb("ex3", [128, 8, 8])
        exb = sb("exb", [128, 8])
        eb3 = sb("eb3", [128, 64, 7], BF16)
        ebf = sb("ebf", [128, 64])
        eid = sb("eid", [128, NBK], I32)
        place = sb("place", [128, NW, 8])
        sl3 = sb("sl3", [128, NW, 8])
        slf = sb("slf", [128, NW])
        slot_u = sb("slot_u", [128, 2, NTT], U32)
        zrow = sb("zrow", [128, C])
        st4 = sb("st4", [128, 2, 6])
        mv4 = [sb(f"mv4{i}", [128, 2, 2]) for i in range(2)]
        ve4 = sb("ve4", [128, 2])
        rs4 = [sb(f"rs4{i}", [128, 2]) for i in range(2)]
        xs = [nc.dram_tensor(f"xs{w}", (128 * BLOCKS[w], C), F32, kind="Internal").ap() for w in range(2)]
        ys = [nc.dram_tensor(f"ys{w}", (128 * BLOCKS[w], C), F32, kind="Internal").ap() for w in range(2)]
        scr_qkc = nc.dram_tensor("scr_qkc", (9, 128, T), BF16, kind="Internal").ap()
        scr_kc = nc.dram_tensor("scr_kc", (3, B, 128, TK), BF16, kind="Internal").ap()
        scr_vc = nc.dram_tensor("scr_vc", (B * TK, C), F32, kind="Internal").ap()
        OTs = sb("OTs", [128, 2, T])
        linv = sb("linv", [128, 4, 4, 2])
        ctx = sb("ctx", [128, NT, C])
        ctxT = sb("ctxT", [128, T])
        r = sb("r", [128, NT, C])
        xb = sb("xb", [128, NT, C])
        st = sb("st", [128, NT, 6])
        mv = sb("mv", [128, NT, 2])
        ve = sb("ve", [128, NT])
        rstd = sb("rstd", [128, NT])

        scr_qk = nc.dram_tensor("scr_qk", (6, 128, T), BF16, kind="Internal").ap()
        scr_v = nc.dram_tensor("scr_v", (16, T, D), F32, kind="Internal").ap()

        PS = es.enter_context(nc.psum_tensor("PS", [128, 8 * 512], F32))
        Sps = [PS[:, 512 * i:512 * (i + 1)] for i in range(2)]
        STps = [PS[:, 1024 * (i + 1):1024 * (i + 2)] for i in range(2)]
        OTps = PS[:, 512 * 6:512 * 7]
        AUX = PS[:, 512 * 7:512 * 8]
        BK = [PS[:, 512 * i:512 * i + 512] for i in range(8)]

        turns = sem("turns")
        xin_in = sem("xin_in")
        wA_in = sem("wA_in")
        cA_in = sem("cA_in")
        ident_ok = sem("ident_ok")
        zero_ok = [sem(f"zero_ok{i}") for i in range(NBUF)]
        zeroc_ok = sem("zeroc_ok")
        wTA_ps = sem("wTA_ps")
        wTA_sb = sem("wTA_sb")
        xT_ps = sem("xT_ps")
        xT_sb = sem("xT_sb")
        qk_ps = sem("qk_ps")
        qk_sb = sem("qk_sb")
        v_ps = sem("v_ps")
        v_sb = sem("v_sb")
        split = sem("split")
        parts_out = sem("parts_out")
        v_out = sem("v_out")
        stacks_in = sem("stacks_in")
        v_in = sem("v_in")
        s_ps = sem("s_ps")
        max_sb = sem("max_sb")
        mb_sb = sem("mb_sb")
        m_in = sem("m_in")
        st_ps = sem("st_ps")
        p_sb = sem("p_sb")
        pv_ps = sem("pv_ps")
        ot_sb = sem("ot_sb")
        oT_ps = sem("oT_ps")
        linv_sb = sem("linv_sb")
        ctx_sb = sem("ctx_sb")
        ctxT_ps = sem("ctxT_ps")
        ctxT_sb = sem("ctxT_sb")
        y_ps = sem("y_ps")
        xb_sb = sem("xb_sb")
        r_sb = sem("r_sb")
        st_sb = sem("st_sb")
        mv_sb = sem("mv_sb")
        ve_sb = sem("ve_sb")
        rstd_sb = sem("rstd_sb")
        x1_sb = sem("x1_sb")
        vp_ok = [sem(f"vp_ok{i}") for i in range(NBUF)]
        vcp_ok = sem("vcp_ok")
        mask_ok = sem("mask_ok")
        wx_in = sem("wx_in")
        cx_in = sem("cx_in")
        cin_in = sem("cin_in")
        wx_sb = sem("wx_sb")
        cT_ps = sem("cT_ps")
        cT_sb = sem("cT_sb")
        kc_ps = sem("kc_ps")
        kc_split = sem("kc_split")
        vc_ps = sem("vc_ps")
        vc_sb = sem("vc_sb")
        kc_out = sem("kc_out")
        vc_out = sem("vc_out")
        c_x2in = sem("c_x2in")
        c_xT_ps = sem("c_xT_ps")
        c_xT_sb = sem("c_xT_sb")
        c_qk_ps = sem("c_qk_ps")
        c_qk_sb = sem("c_qk_sb")
        c_qv_ps = sem("c_qv_ps")
        c_qc_sb = sem("c_qc_sb")
        c_v_sb = sem("c_v_sb")
        c_split = sem("c_split")
        c_vp_sb = sem("c_vp_sb")
        c_parts_out = sem("c_parts_out")
        c_stacks_in = sem("c_stacks_in")
        c_s_ps = sem("c_s_ps")
        c_max_sb = sem("c_max_sb")
        c_mT_ps = sem("c_mT_ps")
        c_mT_sb = sem("c_mT_sb")
        c_m_in = sem("c_m_in")
        c_st_ps = sem("c_st_ps")
        c_p_sb = sem("c_p_sb")
        c_pv_ps = sem("c_pv_ps")
        c_ot_sb = sem("c_ot_sb")
        c_oTs_ps = sem("c_oTs_ps")
        c_oTx_ps = sem("c_oTx_ps")
        c_lin_sb = sem("c_lin_sb")
        c_ctx_sb = sem("c_ctx_sb")
        c_ctx2_sb = sem("c_ctx2_sb")
        c_ctxT_ps = sem("c_ctxT_ps")
        c_ctxT_sb = sem("c_ctxT_sb")
        c_y_ps = sem("c_y_ps")
        c_xb_sb = sem("c_xb_sb")
        c_r_sb = sem("c_r_sb")
        c_st_sb = sem("c_st_sb")
        c_mv_sb = sem("c_mv_sb")
        c_ve_sb = sem("c_ve_sb")
        c_rstd_sb = sem("c_rstd_sb")
        x2_sb = sem("x2_sb")
        f_w1_in = [sem(f"f_w1_in{i}") for i in range(4)]
        f_w2_in = sem("f_w2_in")
        f_wr_in = sem("f_wr_in")
        f_w_ps = sem("f_w_ps")
        f_w_sb = sem("f_w_sb")
        f_const = sem("f_const")
        f_zero = sem("f_zero")
        r_chain = sem("r_chain")
        r_exp = sem("r_exp")
        r_place_ps = sem("r_place_ps")
        r_slots = sem("r_slots")
        x_sent = [sem(f"x_sent{w}") for w in range(2)]
        s_chain = sem("s_chain")
        g_half = sem("g_half")
        zeroed = sem("zeroed")
        b_x_in = [sem(f"b_x_in{i}") for i in range(2)]
        b_xT_ps = sem("b_xT_ps")
        b_xT_sb = sem("b_xT_sb")
        b_h_ps = sem("b_h_ps")
        b_sa = sem("b_sa")
        b_he = sem("b_he")
        b_heT_ps = sem("b_heT_ps")
        b_heT_sb = sem("b_heT_sb")
        b_y_ps = sem("b_y_ps")
        b_y_sb = sem("b_y_sb")
        b_y_out = [sem(f"b_y_out{i}") for i in range(2)]
        g_in = [sem(f"g_in{i}") for i in range(8)]
        g_acc = sem("g_acc")
        g_st = sem("g_st")
        g_mv = sem("g_mv")
        g_ve = sem("g_ve")
        g_rs = sem("g_rs")
        g_yo = sem("g_yo")
        g_out = [sem(f"g_out{i}") for i in range(2)]
        rx_sb = sem("rx_sb")
        rxT_ps = sem("rxT_ps")
        rxT_sb = sem("rxT_sb")
        mx_ps = sem("mx_ps")
        mx_sb = sem("mx_sb")
        wr_ps = sem("wr_ps")
        wr_sb = sem("wr_sb")
        x_in = [sem(f"x_in{i}") for i in range(4)]

        def count(value):
            return max(value, 0) if isinstance(value, int) else value

        def settle(eng):
            eng.sem_inc(turns, 1)

        def span(eng, lo, hi, step):
            if (hi - lo) % 2:
                step(lo, lo // 2, lo % 2)
                lo += 1
            if hi > lo:
                with eng.Fori(0, (hi - lo) // 2, 1) as i:
                    for u in (lo, lo + 1):
                        step(i * 2 + u, i + u // 2, u % 2)
        ranges = [("P", 0), ("L", 1), ("SA", 1), ("SB", 2), ("T", 3), ("E", 4), ("R", 5)]

        def active(t):
            return {k for k, lag in ranges if 0 <= t - lag < B}

        def run(eng, step, step2, between):
            def both(t):
                between(t)
                step2(t, (t + 1) % 3, active(t))
            for t in range(5):
                step(t, t % 3, active(t))
            with eng.Fori(5, B - 4, 3) as it:
                for u in range(3):
                    step(it + u, (5 + u) % 3, {k for k, _ in ranges})
            for t in range(B - 2, B + 4):
                step(t, t % 3, active(t))
                if t >= B:
                    both(t - B)
            for t in range(4, 8):
                both(t)
            with eng.Fori(8, B - 4, 3) as it:
                for u in range(3):
                    step2(it + u, (9 + u) % 3, {k for k, _ in ranges})
            for t in range(B - 2, B + 4):
                step2(t, (t + 1) % 3, active(t))

        S_SLOTS = {4: ("SA", 0, 2), 5: ("SA", 2, 4), 6: ("SA", 4, 6), 7: ("SA", 6, 8),
                   0: ("SB", 8, 10), 1: ("SB", 10, 12), 2: ("SB", 12, 14), 3: ("SB", 14, 16)}
        S2_SLOTS = {5: ("SA", 0, 2), 6: ("SA", 2, 4), 7: ("SA", 4, 6), 8: ("SA", 6, 8), 9: ("SA", 8, 10),
                    0: ("SB", 10, 12), 1: ("SB", 12, 14), 2: ("SB", 14, 16), 3: ("SB", 16, 18), 4: ("SB", 18, 20)}
        LAG = dict(ranges)
        UNITS = ([((17, 5 + e // 2), "w2", e, 0) for e in range(8)]
                 + [((18, i), "w1", (6, 7, 0, 1)[i // 2], i % 2) for i in range(8)]
                 + [((19, i), "w1", 2 + i // 2, i % 2) for i in range(8)])
        ROUTE = ((14, 0), (14, 1), (14, 3), (14, 4), (14, 6), (14, 7), (14, 8), (14, 9), (15, 0), (15, 2), (15, 5))
        ROUTE1 = {(1, 0): (0,), (1, 1): (1,), (1, 3): (2,), (2, 0): (3,), (2, 1): (4,), (2, 2): (5,), (2, 3): (6,),
                  (3, 0): (7, 8), (3, 1): (9,), (3, 3): (10,)}
        W1LOAD = {6: 1, 7: 1, 0: 2, 1: 2, 2: 3, 3: 3, 4: 4, 5: 4}

        block = es.enter_context(nc.Block())

        @block.tensor
        def _(pe):
            pe.wait_ge(ident_ok, 2)
            pe.wait_ge(wA_in, 32)
            for c in range(4):
                i = pe.transpose(AUX[:, 128 * c:128 * c + 128], WnatA[:, c, :], ident[:])
            i.then_inc(wTA_ps, 1)
            pe.wait_ge(wTA_sb, 3)
            WV = WTA[:, 0:384].rearrange("p (j x) -> p j x", x=24)[:, :, 16:24]
            def cross_context():
                pe.wait_ge(f_wr_in, 16)
                pe.transpose(OTps[:, 0:24], wrr[:], ident[0:24, 0:24]).then_inc(wr_ps, 1)
                pe.wait_ge(cin_in, 16)
                for n in range(8):
                    i = pe.transpose(PS[0:CK, 1024 + 128 * n:1152 + 128 * n], cin[:, n, :], ident[:])
                i.then_inc(cT_ps, 1)
                pe.wait_ge(cT_sb, 1)
                pe.wait_ge(wx_sb, 4)
                for n in range(2):
                    i = pe.matmul(PS[:, 2048 + 512 * n:2560 + 512 * n], Wckp[:], cT[:, 512 * n:512 * n + 512], start=True, stop=True)
                i.then_inc(kc_ps, 1)
                for n in range(8):
                    i = pe.matmul(PS[:, 1024 + 128 * n:1152 + 128 * n], cT[:, 128 * n:128 * n + 128], Wckr[:, 1, :], start=True, stop=True)
                i.then_inc(vc_ps, 1)
                pe.wait_ge(vc_sb, 1)

            def step(t, u, on):
                def S(slot):
                    if slot not in S_SLOTS:
                        return
                    stage, h0, h1 = S_SLOTS[slot]
                    if stage not in on:
                        return
                    b = t - LAG[stage]
                    k = (u - LAG[stage]) % 3
                    if h0 == 0:
                        pe.wait_ge(stacks_in, count(b * 96 + 96))
                    Q4 = Qs[k][0:KS, :].rearrange("p (q h) -> p q h", h=H)
                    K4 = Ks[k][0:KS, :].rearrange("p (q h) -> p q h", h=H)
                    for h in range(h0, h1):
                        pe.wait_ge(max_sb, count(b * 16 + (h - 1)))
                        for q in range(2):
                            i = pe.matmul(Sps[h % 2][:, 256 * q:256 * q + 256], Q4[:, 128 * q:128 * q + 128, h], K4[:, :, h],
                                          start=True, stop=True)
                        i.then_inc(s_ps, 1)

                def ST(slot):
                    if "T" not in on:
                        return
                    b = t - 3
                    k = u % 3
                    if slot == 0:
                        pe.wait_ge(m_in, count(b * 64 + 64))
                    pe.wait_ge(p_sb, count(b * 8 + (slot - 1)))
                    Q4 = Qs[k][0:MROW + 2, :].rearrange("p (q h) -> p q h", h=H)
                    K4 = Ks[k][0:MROW + 2, :].rearrange("p (q h) -> p q h", h=H)
                    for n in range(2):
                        h = slot // 2 + 4 * (2 * (slot % 2) + n)
                        for kt in range(2):
                            o = 512 * n + 256 * kt
                            i = pe.matmul(STps[slot % 2][:, o:o + 256], K4[:, 128 * kt:128 * kt + 128, h], Q4[:, :, h],
                                          start=True, stop=True)
                    i.then_inc(st_ps, 1)

                def PV(g, b, k):
                    pe.wait_ge(p_sb, count(b * 8 + (2 * g + 2)))
                    if g == 0:
                        pe.wait_ge(ot_sb, count(b))
                        pe.wait_ge(v_in, count(b * 64 + 64))
                    hf, gg = g // 2, g % 2
                    for kt in range(2):
                        for c in range(4):
                            h = 4 * c + g
                            i = pe.matmul(OTps[32 * c:32 * c + 32, 256 * hf:256 * hf + 256], Vp[k][:, kt, h, :],
                                          P[(2 * g + c // 2) % 4][:, c % 2, kt, :],
                                          start=(gg == 0 and kt == 0), stop=(gg == 1 and kt == 1))
                    i.then_inc(pv_ps, 1)

                for slot in range(8):
                    S(slot)
                    ST(slot)
                    if slot == 0 and "P" in on:
                        b = t
                        pe.wait_ge(v_sb, count(t))
                        pe.wait_ge(xin_in, count(t * 16 + 16))
                        pe.wait_ge(r_sb, count(t - 4))
                        for c in range(NT):
                            i = pe.transpose(AUX[:, 128 * c:128 * c + 128], xin[u][:, c, :], ident[:])
                        i.then_inc(xT_ps, 1)
                    if slot == 1 and "P" in on:
                        pe.wait_ge(xT_sb, count(t + 1))
                        for a in range(2):
                            i = pe.matmul(AUX[:, 256 * a:256 * a + 256], WqkA[:, a, :], xT[:], start=True, stop=True)
                        i.then_inc(qk_ps, 1)
                    if slot == 2 and "P" in on:
                        pe.wait_ge(qk_sb, count(t * 2 + 2))
                        for c in range(2):
                            i = pe.matmul(AUX[:, 128 * c:128 * c + 128], xT[:, 128 * c:128 * c + 128], WV, start=True, stop=True)
                        i.then_inc(v_ps, 1)
                    if slot == 4 and "E" in on:
                        b = t - 4
                        pe.wait_ge(ot_sb, count(b + 1))
                        if "P" in on:
                            pe.wait_ge(v_sb, count(t + 1))
                        else:
                            pe.wait_ge(r_sb, count(t - 4))
                            pe.wait_ge(c_v_sb, count(t - B))
                            pe.wait_ge(c_qc_sb, count(t - B))
                        for c in range(2):
                            for hf in range(2):
                                o = 256 * c + 128 * hf
                                i = pe.transpose(AUX[:, o:o + 128], OTs[:, hf, 128 * c:128 * c + 128], ident[:])
                        i.then_inc(oT_ps, 1)
                    if slot == 5 and "E" in on:
                        pe.wait_ge(ctx_sb, count(t - 3))
                        for c in range(NT):
                            i = pe.transpose(AUX[:, 128 * c:128 * c + 128], ctx[:, c, :], ident[:])
                        i.then_inc(ctxT_ps, 1)
                    if slot == 6 and "E" in on:
                        pe.wait_ge(ctxT_sb, count(t - 3))
                        for c in range(NT):
                            i = pe.matmul(AUX[:, 128 * c:128 * c + 128], ctxT[:, 128 * c:128 * c + 128], WTA[:, 384:512], start=True, stop=True)
                        i.then_inc(y_ps, 1)
                    if slot == 0 and "E" in on:
                        PV(3, t - 4, (u - 1) % 3)
                    if slot in (2, 4, 6) and "T" in on:
                        PV(slot // 2 - 1, t - 3, u % 3)
                if isinstance(t, int) and t == 2:
                    cross_context()


            def placement(w, bank):
                n = WAVES[w]
                pe.wait_ge(r_chain, NCH * w + 15)
                m = both[:, T0[w]:T0[w] + n, :]
                pe.matmul(bank[:, 0:8 * n], trib[:], m, start=True, stop=False)
                for i in range(n - 1):
                    pe.matmul(bank[:, 8 * i + 8:8 * n], onesb[:], m[:, i:i + 1, :].to_broadcast((128, n - 1 - i, 8)), start=False, stop=(i == n - 2))
                for i in range(n):
                    j = pe.matmul(bank[:, 8 * n:8 * n + 8], onesb[:], m[:, i, :], start=(i == 0), stop=(i == n - 1))
                j.then_inc(r_place_ps, 1)

            def turn_weights(n, kind, e, part_):
                bank = BK[n % 2]
                if n >= 2:
                    pe.wait_ge(f_w_sb, n - 1)
                else:
                    pe.wait_ge(c_max_sb, 20 * B)
                if kind == "w2":
                    pe.wait_ge(f_w2_in, 32)
                    for k in range(3):
                        i = pe.transpose(bank[0:KF[k], 128 * k:128 * k + 128], w2r[:, e, 128 * k:128 * k + KF[k]], ident[:])
                else:
                    pe.wait_ge(f_w1_in[W1LOAD[e] - 1], 16)
                    for k in range(4):
                        i = pe.transpose(bank[:, W1ROWS * k:W1ROWS * k + W1ROWS], w1r[e][:, 4 * part_ + k, :], ident[0:W1ROWS, 0:W1ROWS])
                i.then_inc(f_w_ps, 1)

            def step2(t, u, on):
                def S(slot):
                    if slot not in S2_SLOTS or S2_SLOTS[slot][0] not in on:
                        return
                    stage, n0, n1 = S2_SLOTS[slot]
                    b = t - LAG[stage]
                    k = (u - LAG[stage]) % 3
                    if n0 == 0:
                        pe.wait_ge(c_stacks_in, count(b * 224 + 224))
                    for n in range(n0, n1):
                        pe.wait_ge(c_max_sb, count(b * 20 + (n - 1)))
                        o = Sps[n % 2]
                        if n < 16:
                            q, kk = Qs[k][0:KS, T * n:T * n + T], Ks[k][0:KS, T * n:T * n + T]
                            pe.matmul(o[:, 0:128], q[:, 0:128], kk[:, 0:128], start=True, stop=False)
                            pe.matmul(o[:, 0:128], identb[:], maskq[:], start=False, stop=True)
                            pe.matmul(o[:, 128:384], q[:, 128:256], kk, start=True, stop=False)
                            i = pe.matmul(o[:, 256:384], identb[:], maskq[:], start=False, stop=True)
                        else:
                            for h in range(4 * (n - 16), 4 * (n - 15)):
                                for qt in range(2):
                                    c = (h % 4) * 128 + 64 * qt
                                    i = pe.matmul(o[:, c:c + 64], Qcs[k][0:KS, T * h + 128 * qt:T * h + 128 * qt + 128],
                                                  Kcs[k][0:KS, TK * h:TK * h + TK], start=True, stop=True)
                        i.then_inc(c_s_ps, 1)

                def ST(slot):
                    if "T" not in on:
                        return
                    b = t - 3
                    k = u % 3
                    if slot == 0:
                        pe.wait_ge(c_m_in, count(b * 64 + 64))
                    pe.wait_ge(c_p_sb, count(b * 10 + (slot - 1)))
                    o = STps[slot % 2]
                    if slot < 8:
                        for n in range(2):
                            h = slot // 2 + 4 * (2 * (slot % 2) + n)
                            q, kk = Qs[k][0:MROW + 2, T * h:T * h + T], Ks[k][0:MROW + 2, T * h:T * h + T]
                            c = 512 * n
                            pe.matmul(o[:, c:c + 256], kk[:, 0:128], q, start=True, stop=False)
                            pe.matmul(o[:, c:c + 128], identb[:], maskk[:], start=False, stop=True)
                            pe.matmul(o[:, c + 256:c + 384], kk[:, 128:256], q[:, 128:256], start=True, stop=False)
                            i = pe.matmul(o[:, c + 256:c + 384], identb[:], maskk[:], start=False, stop=True)
                    else:
                        for c in range(4):
                            for n in range(2):
                                h = 4 * c + 2 * (slot - 8) + n
                                i = pe.matmul(o[64 * n:64 * n + 64, 256 * c:256 * c + 256], Kcs[k][0:MROW + 2, TK * h:TK * h + TK],
                                              Qcs[k][0:MROW + 2, T * h:T * h + T], start=True, stop=True)
                    i.then_inc(c_st_ps, 1)

                def PV(g, b, k):
                    pe.wait_ge(c_p_sb, count(b * 10 + (2 * g + 2)))
                    if g == 0:
                        pe.wait_ge(c_ot_sb, count(b * 2))
                        pe.wait_ge(c_vp_sb, count(b * 2 + 2))
                    hf, gg = g // 2, g % 2
                    for kt in range(2):
                        for c in range(4):
                            h = 4 * c + g
                            tile = P[(2 * g + c // 2) % 5][:, c % 2].rearrange("p a b -> p (a b)")
                            i = pe.matmul(OTps[32 * c:32 * c + 32, 256 * hf + 128 * kt:256 * hf + 256], Vp[k][:, kt, h, :],
                                          tile[:, 256 * kt:256 + 128 * kt],
                                          start=(gg == 0 and kt == 0), stop=(gg == 1 and kt == 1))
                    i.then_inc(c_pv_ps, 1)

                def PVX(hf, b, k):
                    pe.wait_ge(c_p_sb, count(b * 10 + 9 + hf))
                    if hf == 0:
                        pe.wait_ge(c_ot_sb, count(b * 2 + 1))
                    tile = P[(8 + hf) % 5][:].rearrange("p a b c -> p (a b c)")
                    for c in range(4):
                        i = pe.matmul(OTps[32 * c:32 * c + 32, 256 * hf:256 * hf + 256], VCp[k][:, 2 * c + hf, :],
                                      tile[:, 256 * c:256 * c + 256], start=True, stop=True)
                    i.then_inc(c_pv_ps, 1)

                for slot in range(10):
                    if slot == 5 and "SB" in on:
                        b = t - 2
                        if "P" in on:
                            pe.wait_ge(c_qc_sb, count(t + 1))
                            pe.wait_ge(c_v_sb, count(t + 1))
                        else:
                            pe.wait_ge(c_r_sb, count(t - 4))
                            pe.wait_ge(mx_sb, count(t - 5))
                        if isinstance(t, int) and t == 15:
                            pe.wait_ge(r_slots, 1)
                        pe.wait_ge(c_max_sb, count(b * 20 + 20))
                        settle(pe)
                        pe.transpose(AUX[0:4 * H, 0:128], M2[:], ident[:]).then_inc(c_mT_ps, 1)
                    S(slot)
                    ST(slot)
                    if slot == 0 and "P" in on:
                        pe.wait_ge(c_v_sb, count(t))
                        pe.wait_ge(mx_sb, count(t - 5))
                        pe.wait_ge(c_x2in, count(t + 1))
                        pe.wait_ge(c_r_sb, count(t - 4))
                        for c in range(NT):
                            i = pe.transpose(AUX[:, 128 * c:128 * c + 128], x2in[:, c, :], ident[:])
                        i.then_inc(c_xT_ps, 1)
                    if slot == 1 and "P" in on:
                        pe.wait_ge(c_xT_sb, count(t + 1))
                        for a in range(2):
                            i = pe.matmul(AUX[:, 256 * a:256 * a + 256], Wqkc[:, a, :], xT[:], start=True, stop=True)
                        i.then_inc(c_qk_ps, 1)
                    if slot == 2 and "P" in on:
                        pe.wait_ge(c_qk_sb, count(t * 2 + 2))
                        pe.matmul(AUX[:, 0:256], Wqkc[:, 2, :], xT[:], start=True, stop=True)
                        for c in range(2):
                            i = pe.matmul(AUX[:, 256 + 128 * c:384 + 128 * c], xT[:, 128 * c:128 * c + 128], Wx[:, 3, :], start=True, stop=True)
                        i.then_inc(c_qv_ps, 1)
                    if slot == 5 and "E" in on:
                        if "SB" in on:
                            pe.wait_ge(c_mT_sb, count(t * 2 - 2))
                        else:
                            pe.wait_ge(c_r_sb, count(t - 4))
                            pe.wait_ge(mx_sb, count(t - 5))
                        for c in range(2):
                            for hf in range(2):
                                o = 256 * c + 128 * hf
                                i = pe.transpose(AUX[:, o:o + 128], OTs[:, hf, 128 * c:128 * c + 128], ident[:])
                        i.then_inc(c_oTs_ps, 1)
                    if slot == 6 and "E" in on:
                        pe.wait_ge(c_ot_sb, count(t * 2 - 6))
                        pe.wait_ge(c_ctx_sb, count(t - 3))
                        for c in range(2):
                            for hf in range(2):
                                o = 256 * c + 128 * hf
                                i = pe.transpose(AUX[:, o:o + 128], OTx[:, hf, 128 * c:128 * c + 128], ident[:])
                        i.then_inc(c_oTx_ps, 1)
                    if slot == 7 and "E" in on:
                        pe.wait_ge(c_ctx2_sb, count(t * 2 - 6))
                        for c in range(NT):
                            i = pe.transpose(AUX[:, 128 * c:128 * c + 128], ctx[:, c, :], ident[:])
                        i.then_inc(c_ctxT_ps, 1)
                    if slot == 8 and "E" in on:
                        pe.wait_ge(c_ctxT_sb, count(t - 3))
                        for c in range(NT):
                            i = pe.matmul(AUX[:, 128 * c:128 * c + 128], ctxT[:, 128 * c:128 * c + 128], Wx[:, 4, :], start=True, stop=True)
                        i.then_inc(c_y_ps, 1)
                    if slot == 8 and "R" in on:
                        pe.wait_ge(rx_sb, count(t - 4))
                        if "E" not in on:
                            pe.wait_ge(mx_sb, count(t - 5))
                            pe.wait_ge(c_r_sb, B)
                        for c in range(NT):
                            i = pe.transpose(AUX[:, 256 + 128 * c:384 + 128 * c], rxin[:, c, :], ident[:])
                        i.then_inc(rxT_ps, 1)
                    if slot == 0 and "E" in on:
                        PVX(1, t - 4, (u - 1) % 3)
                    if slot in (2, 4, 6, 8) and "T" in on:
                        PV(slot // 2 - 1, t - 3, u % 3)
                    if slot == 9 and "T" in on:
                        PVX(0, t - 3, u % 3)
                    if slot == 9 and "R" in on:
                        pe.wait_ge(rxT_sb, count(t - 4))
                        pe.wait_ge(c_r_sb, count(t - 3)) if "E" in on else None
                        for c in range(NT):
                            i = pe.matmul(AUX[:, 24 * c:24 * c + 24], rxT[:, 128 * c:128 * c + 128], wrT[:], start=True, stop=True)
                        i.then_inc(mx_ps, 1)
                    if isinstance(t, int):
                        if t == 15 and slot == 4:
                            pe.wait_ge(mx_sb, t - 5)
                            pe.wait_ge(c_qc_sb, t + 1)
                            pe.wait_ge(c_v_sb, t + 1)
                            placement(0, BK[7])
                        for n, unit in enumerate(UNITS):
                            if unit[0] == (t, slot):
                                turn_weights(n, *unit[1:])
                if isinstance(t, int) and t == 3:
                    pe.wait_ge(c_mT_sb, 4)
                    pe.wait_ge(c_qc_sb, 4)
                    pe.wait_ge(c_v_sb, 4)

            def between(t):
                if t < 4:
                    pe.wait_ge(r_sb, B - 3 + t)
                if t == 1:
                    pe.wait_ge(max_sb, 16 * B)
                    pe.wait_ge(mask_ok, 6)
                    pe.wait_ge(zeroc_ok, 3 * NBUF)
            run(pe, step, step2, between)
            pe.wait_ge(c_ot_sb, 2 * B)
            pe.wait_ge(f_w_sb, len(UNITS))
            pe.wait_ge(c_p_sb, 10 * B)
            pe.wait_ge(mx_sb, B - 1)

            def turn_x(g, h, p):
                pe.wait_ge(b_x_in[p], h * 16 + 16)
                pe.wait_ge(b_xT_sb, count(g))
                for i in range(4):
                    j = pe.transpose(BK[7][:, 128 * i:128 * i + 128], xblk[p][:, i, :], ident[:])
                j.then_inc(b_xT_ps, 1)

            def expert(j):
                return pe.value_load(eid[0:1, j:j + 1] if isinstance(j, int) else eid[0:1, bass.ds(j, 1)], min_val=0, max_val=E_ - 1)

            def hidden(j, u, p):
                e = expert(j)
                pe.wait_ge(b_he, count(j - 1))
                for f in range(2):
                    i = pe.matmul(BK[2 * f + u % 2][:, 0:FF], xbT[p][:, u, :], w1T[:, bass.ds(e, 1), FF * f:FF * f + FF].rearrange("p a b -> p (a b)"), start=True, stop=True)
                i.then_inc(b_h_ps, 1)

            def turn_hidden(j, u):
                pe.wait_ge(b_he, count(j + 1))
                pe.wait_ge(b_heT_sb, count(j - 1))
                for k in range(3):
                    i = pe.transpose(BK[4 + u % 2][0:KF[k], 128 * k:128 * k + 128], he[u % 2][:, 128 * k:128 * k + KF[k]], ident[:])
                i.then_inc(b_heT_ps, 1)

            def result(j, u):
                e = expert(j)
                pe.wait_ge(b_heT_sb, count(j + 1))
                pe.wait_ge(b_y_sb, count(j))
                for k in range(3):
                    i = pe.matmul(BK[6][:, 0:128], heT[u % 2][0:KF[k], k, :], w2T[0:KF[k], bass.ds(e, 1), 128 * k:128 * k + 128].rearrange("p a b -> p (a b)"), start=(k == 0), stop=(k == 2))
                i.then_inc(b_y_ps, 1)

            def step(g, h, p, more=True):
                for u in range(4):
                    j = g * 4 + u
                    if u == 0:
                        pe.wait_ge(b_xT_sb, count(g + 1))
                    if isinstance(g, int) and (g, u) == (1, 1):
                        pe.wait_ge(mx_sb, B)
                    if isinstance(g, int) and (g, u) == (4, 1):
                        pe.wait_ge(r_slots, 2)
                    hidden(j, u, p)
                    if not (isinstance(j, int) and j < 1):
                        turn_hidden(j - 1, u + 1)
                    if not (isinstance(j, int) and j < 2):
                        result(j - 2, u)
                    if u == 1 and more:
                        turn_x(g + 1, h + p, 1 - p)
                    if isinstance(g, int) and (g, u) == (0, 2):
                        pe.wait_ge(rx_sb, B)
                        pe.wait_ge(b_xT_sb, g + 2)
                        for c in range(NT):
                            i = pe.transpose(AUX[:, 256 + 128 * c:384 + 128 * c], rxin[:, c, :], ident[:])
                        i.then_inc(rxT_ps, 1)
                    if isinstance(g, int) and (g, u) == (0, 3):
                        pe.wait_ge(rxT_sb, B)
                        for c in range(NT):
                            i = pe.matmul(AUX[:, 24 * c:24 * c + 24], rxT[:, 128 * c:128 * c + 128], wrT[:], start=True, stop=True)
                        i.then_inc(mx_ps, 1)
                    if isinstance(g, int) and (g, u) == (3, 2):
                        pe.wait_ge(b_xT_sb, g + 2)
                        placement(1, BK[7])
            turn_x(0, 0, 0)
            for g in range(5):
                step(g, g // 2, g % 2)
            span(pe, 5, NG - 2, step)
            step(NG - 2, NG // 2 - 1, 0)
            step(NG - 1, NG // 2 - 1, 1, more=False)
            turn_hidden(NBK - 1, 1)
            result(NBK - 2, 0)
            result(NBK - 1, 1)

        @block.scalar
        def _(act):
            def step(t, u, on):
                for slot in range(8):
                    if "T" in on:
                        b = t - 3
                        act.wait_ge(st_ps, count(b * 8 + (slot + 1)))
                        act.wait_ge(pv_ps, count(b * 4 + (slot // 2 - 1)))
                        act.activation(P[slot % 4][:].rearrange("p a b c -> p (a b c)"), STps[slot % 2], ACT.Exp, scale=SCALE).then_inc(p_sb, 1)
                    if slot == 1 and "P" in on:
                        act.wait_ge(qk_ps, count(t + 1))
                        act.wait_ge(split, count(t * 4))
                        for a in range(2):
                            act.activation(qk32[:, a, :], AUX[:, 256 * a:256 * a + 256], ACT.Identity, bias=bqkA[:, a:a + 1]).then_inc(qk_sb, 1)
                    if slot == 5 and "E" in on:
                        act.wait_ge(ctxT_ps, count(t - 3))
                        act.wait_ge(y_ps, count(t - 4))
                        act.activation(ctxT[:], AUX[:, 0:256], ACT.Copy).then_inc(ctxT_sb, 1)
                    if slot == 0 and "E" in on:
                        act.wait_ge(pv_ps, count(t * 4 - 12))
                        act.wait_ge(oT_ps, count(t - 4))
                        act.activation(OTs[:].rearrange("p f (i j) -> p f j i", j=16), OTps.rearrange("p (f j i) -> p f j i", f=2, i=16), ACT.Copy).then_inc(ot_sb, 1)
            act.wait_ge(cA_in, 64)

            def step2(t, u, on):
                for slot in range(10):
                    if "T" in on:
                        b = t - 3
                        act.wait_ge(c_st_ps, count(b * 10 + (slot + 1)))
                        if slot < 5:
                            if not (isinstance(b, int) and b == 0):
                                act.wait_ge(c_pv_ps, count(b * 6 - 6 + (3, 4, 4, 5, 6)[slot]))
                        else:
                            act.wait_ge(c_pv_ps, count(b * 6 + ((slot - 5) // 2 + 1)))
                        src, dst = STps[slot % 2], P[slot % 5][:].rearrange("p a b c -> p (a b c)")
                        if slot < 8:
                            src = src.rearrange("p (n k) -> p n k", n=2)[:, :, 0:384]
                            dst = dst.rearrange("p (n k) -> p n k", n=2)[:, :, 0:384]
                        act.activation(dst, src, ACT.Exp, scale=SCALE).then_inc(c_p_sb, 1)
                    if slot == 1 and "P" in on:
                        act.wait_ge(c_qk_ps, count(t + 1))
                        act.wait_ge(c_split, count(t * 4))
                        for a in range(2):
                            act.activation(qkc32[:, a, :], AUX[:, 256 * a:256 * a + 256], ACT.Identity, bias=bx3[:, a:a + 1]).then_inc(c_qk_sb, 1)
                    if slot == 2 and "P" in on:
                        act.wait_ge(c_qv_ps, count(t + 1))
                        act.activation(qkc32[:, 2, :], AUX[:, 0:256], ACT.Identity, bias=bx3[:, 2:3]).then_inc(c_qc_sb, 1)
                    if slot == 7 and "E" in on:
                        act.wait_ge(c_ctxT_ps, count(t - 3))
                        act.wait_ge(c_y_ps, count(t - 4))
                        act.activation(ctxT[:], AUX[:, 0:256], ACT.Copy).then_inc(c_ctxT_sb, 1)
                    if slot == 8 and "T" in on:
                        b = t - 3
                        act.wait_ge(c_pv_ps, count(b * 6 + 4))
                        act.wait_ge(c_oTs_ps, count(b))
                        act.activation(OTs[:].rearrange("p a b -> p (a b)"), OTps, ACT.Copy).then_inc(c_ot_sb, 1)
                    if slot == 5 and "R" in on:
                        b = t - 5
                        act.wait_ge(x2_sb, count(b * 2 + 2))
                        act.wait_ge(rxT_ps, count(b))
                        act.activation(rxin, X[:, 2 * b:2 * b + 2, :] if isinstance(b, int) else X[:, bass.ds(b * 2, 2), :], ACT.Copy).then_inc(rx_sb, 1)
                    if slot == 9 and "R" in on:
                        act.wait_ge(mx_ps, count(t - 4))
                        b = t - 5
                        act.activation(mx[:, 2 * b:2 * b + 2, :] if isinstance(b, int) else mx[:, bass.ds(b * 2, 2), :],
                                       AUX[:, 0:48].rearrange("p (a b) -> p a b", b=24), ACT.Copy).then_inc(mx_sb, 1)
                    if isinstance(t, int) and (t, slot) == (14, 2):
                        act.wait_ge(r_chain, 3)
                        act.activation(A[:, 0:WAVES[0]], A[:, 0:WAVES[0]], ACT.Exp).then_inc(r_exp, 1)
                    if isinstance(t, int) and (t, slot) == (15, 3):
                        act.wait_ge(r_chain, 21)
                        act.activation(m0[:, 0:WAVES[0]], m0[:, 0:WAVES[0]], ACT.Exp).then_inc(r_exp, 1)
                    if slot == 0 and "E" in on:
                        b = t - 4
                        act.wait_ge(c_pv_ps, count(b * 6 + 6))
                        act.wait_ge(c_oTx_ps, count(b))
                        act.activation(OTx[:].rearrange("p a b -> p (a b)"), OTps, ACT.Copy).then_inc(c_ot_sb, 1)

            def between(t):
                if t == 0:
                    act.wait_ge(cx_in, 144)

            run(act, step, step2, between)
            act.wait_ge(x2_sb, 2 * B)
            act.wait_ge(rxT_ps, B - 1)
            act.activation(rxin, X[:, NTT - 2:NTT, :], ACT.Copy).then_inc(rx_sb, 1)

            def step(g, h, p):
                for u in range(4):
                    j = g * 4 + u
                    act.wait_ge(b_h_ps, count(j + 1))
                    act.wait_ge(b_he, count(j - 1))
                    act.activation(sa[u % 2][:], BK[u % 2][:, 0:FF], ACT.Silu).then_inc(b_sa, 1)
                    if not (isinstance(j, int) and j < 1):
                        copy_heT(j - 1, u + 1)
                    if isinstance(g, int) and (g, u) == (0, 3):
                        act.wait_ge(mx_ps, B)
                        act.activation(mx[:, NTT - 2:NTT, :], AUX[:, 0:48].rearrange("p (a b) -> p a b", b=24), ACT.Copy).then_inc(mx_sb, 1)
                    if isinstance(g, int) and (g, u) == (1, 2):
                        act.wait_ge(r_chain, NCH + 3)
                        act.activation(A[:, 0:WAVES[1]], A[:, 0:WAVES[1]], ACT.Exp).then_inc(r_exp, 1)
                    if isinstance(g, int) and (g, u) == (3, 2):
                        act.wait_ge(r_chain, NCH + 21)
                        act.activation(m0[:, 0:WAVES[1]], m0[:, 0:WAVES[1]], ACT.Exp).then_inc(r_exp, 1)

            def copy_heT(j, u):
                act.wait_ge(b_heT_ps, count(j + 1))
                act.wait_ge(b_y_ps, count(j - 1))
                act.activation(heT[u % 2][:, 0:2, :].rearrange("p a b -> p (a b)"), BK[4 + u % 2][:, 0:256], ACT.Copy)
                act.activation(heT[u % 2][0:KF[2], 2, :], BK[4 + u % 2][0:KF[2], 256:384], ACT.Copy).then_inc(b_heT_sb, 1)
            for g in range(4):
                step(g, g // 2, g % 2)
            span(act, 4, NG, step)
            copy_heT(NBK - 1, 1)

        @block.vector
        def _(dve):
            dve.memset(zrow[:], 0.0).then_inc(f_zero, 1)
            dve.wait_ge(wTA_ps, 1)
            dve.tensor_copy(WTA[:], AUX).then_inc(wTA_sb, 1)
            for a in range(2):
                dve.tensor_copy(WqkA[:, a, :].rearrange("p (d j) -> p d j", j=16),
                                AUX[:, 0:384].rearrange("p (j x) -> p x j", x=24)[:, 8 * a:8 * a + 8, :]).then_inc(wTA_sb, 1)
            ONES = float(np.frombuffer(bytes((0x80, 0x3F)) * 2, np.float32)[0])

            def clear_K(k):
                dve.memset(Ks[k][32:64, :].bitcast(F32), 0.0).then_inc(zero_ok[k], 1)
                dve.memset(Ks[k][64:96, :].bitcast(F32), 0.0).then_inc(zero_ok[k], 1)
                dve.memset(Ks[k][96:98, :].bitcast(F32), ONES).then_inc(zero_ok[k], 1)

            def clear_cross():
                for k in range(NBUF):
                    dve.memset(Kcs[k][96:98, :], 1.0).then_inc(zeroc_ok, 1)
                dve.wait_ge(vcp_ok, NBUF)
                for k in range(NBUF):
                    dve.memset(VCp[k][0:64, :, 16:17], 1.0).then_inc(vcp_ok, 1)
                    dve.memset(VCp[k][64:128, :, 17:18], 1.0).then_inc(vcp_ok, 1)

            def cross_context():
                dve.wait_ge(wr_ps, 1)
                dve.tensor_copy(wrT[:], OTps[:, 0:24]).then_inc(wr_sb, 1)
                dve.wait_ge(wx_in, 80)
                for a in range(3):
                    dve.tensor_copy(Wqkc[:, a, :].rearrange("p (d h) -> p d h", d=D), Wx[:, a, :].rearrange("p (h d) -> p d h", d=D)).then_inc(wx_sb, 1)
                dve.wait_ge(cx_in, 144)
                dve.tensor_copy(Wckp[:].rearrange("p (d h) -> p d h", d=D), Wckr[:, 0, :].rearrange("p (h d) -> p d h", d=D)).then_inc(wx_sb, 1)
                dve.wait_ge(cT_ps, 1)
                dve.tensor_copy(cT, PS[0:CK, 1024:2048]).then_inc(cT_sb, 1)
                dve.wait_ge(kc_ps, 1)
                dve.tensor_scalar(kc32, PS[:, 2048:3072], bx3[:, 3:4], None, ALU.add).then_inc(kc_split, 1)
                dve.wait_ge(kc_split, 1)
                kv = kcp[:]
                dve.tensor_copy(kv[:, 0, :], kc32).then_inc(kc_split, 1)
                dve.wait_ge(kc_split, 2)
                dve.tensor_tensor(rc32, kc32, kv[:, 0, :], ALU.subtract).then_inc(kc_split, 1)
                dve.wait_ge(kc_split, 3)
                dve.tensor_copy(kv[:, 1, :], rc32).then_inc(kc_split, 1)
                dve.wait_ge(kc_split, 4)
                dve.tensor_tensor(kv[:, 2, :], rc32, kv[:, 1, :], ALU.subtract).then_inc(kc_split, 1)
                dve.wait_ge(vc_ps, 1)
                dve.tensor_tensor(vc32.rearrange("p (n c) -> p n c", c=C), PS[:, 1024:2048].rearrange("p (n c) -> p n c", c=C),
                                  bcvx[:].unsqueeze(1).to_broadcast((128, 8, C)), ALU.add).then_inc(vc_sb, 1)

            clear_K(0)
            dve.wait_ge(cA_in, 64)

            def step(t, u, on):
                for slot in range(8):
                    if slot == 4 and "SB" in on:
                        b = t - 2
                        dve.wait_ge(m_in, count(b * 64))
                        dve.wait_ge(max_sb, count(b * 16 + 16))
                        dve.tensor_scalar(Mb[:, 0, :], M[:].rearrange("p q h -> p (q h)"), -1.0, None, ALU.mult).then_inc(mb_sb, 1)
                        dve.wait_ge(mb_sb, count(b * 2 + 1))
                        dve.scalar_tensor_tensor(out=Mb[:, 1, :], in0=M[:].rearrange("p q h -> p (q h)"), scalar=-1.0, in1=Mb[:, 0, :],
                                                 op0=ALU.mult, op1=ALU.subtract).then_inc(mb_sb, 1)
                    if slot in S_SLOTS and S_SLOTS[slot][0] in on:
                        stage, h0, h1 = S_SLOTS[slot]
                        b = t - LAG[stage]
                        if h0 == 0:
                            dve.wait_ge(mb_sb, count(b * 2))
                        for h in range(h0, h1):
                            dve.wait_ge(s_ps, count(b * 16 + (h + 1)))
                            dve.tensor_reduce(out=M[:, :, h], in_=Sps[h % 2].rearrange("p (q k) -> p q k", q=2), op=ALU.max,
                                              axis=AX.X).then_inc(max_sb, 1)
                    if slot == 0 and "P" in on:
                        dve.wait_ge(xT_ps, count(t + 1))
                        dve.wait_ge(v_ps, count(t))
                        dve.tensor_copy(xT[:].rearrange("p (i h) -> p h i", h=H), AUX[:, 0:256].rearrange("p (h i) -> p h i", i=16)).then_inc(xT_sb, 1)
                    if slot == 2 and "P" in on:
                        dve.wait_ge(v_ps, count(t + 1))
                        dve.wait_ge(v_out, count(t * 32))
                        dve.tensor_tensor(vsb[:], AUX[:, 0:256].rearrange("p (c f) -> p c f", c=2),
                                          bvA[:].unsqueeze(1).to_broadcast((128, 2, C)), ALU.add).then_inc(v_sb, 1)
                    if slot == 4 and "E" in on:
                        b = t - 4
                        dve.wait_ge(oT_ps, count(b + 1))
                        o5 = AUX.rearrange("p (t c x) -> p t c x", t=4, c=4)
                        dve.wait_ge(ctx_sb, count(b))
                        dve.reciprocal(linv[:], o5[:, :, :, 16:18]).then_inc(linv_sb, 1)
                        dve.wait_ge(linv_sb, count(b + 1))
                        dve.wait_ge(ctxT_ps, count(b))
                        for c in range(2):
                            for hf in range(2):
                                th = 2 * c + hf
                                i = dve.tensor_tensor(ctx[:, c, :].rearrange("p (q f g d) -> p q f g d", q=4, f=2, g=2)[:, :, hf],
                                                      o5[:, th, :, 0:16].rearrange("p q (g d) -> p q g d", g=2),
                                                      linv[:, th, :, :].unsqueeze(3).to_broadcast((128, 4, 2, D)), ALU.mult)
                        i.then_inc(ctx_sb, 1)
                    if slot == 6 and "E" in on:
                        b = t - 4
                        dve.wait_ge(y_ps, count(b + 1))
                        dve.wait_ge(xb_sb, count(b + 1))
                        dve.wait_ge(x1_sb, count(b * 2))
                        dve.tensor_tensor(r[:], AUX[:, 0:256].rearrange("p (c f) -> p c f", c=2), xb[:], ALU.add).then_inc(r_sb, 1)
                        dve.wait_ge(r_sb, count(b + 1))
                        dve.wait_ge(mv_sb, count(b * 2))
                        for c in range(2):
                            dve.bn_stats(st[:, c, :], r[:, c, :]).then_inc(st_sb, 1)
                        dve.wait_ge(st_sb, count(b * 2 + 2))
                        settle(dve)
                        for c in range(2):
                            dve.bn_aggr(mv[:, c, :], st[:, c, :]).then_inc(mv_sb, 1)
                    if slot == 7 and "E" in on:
                        b = t - 4
                        dve.wait_ge(rstd_sb, count(b + 1))
                        for c in range(2):
                            dve.tensor_scalar(X[:, b * 2 + c, :], r[:, c, :], mv[:, c, 0:1], rstd[:, c:c + 1],
                                              ALU.subtract, ALU.mult).then_inc(x1_sb, 1)
                if isinstance(t, int) and t in (0, 1):
                    clear_K(t + 1)
                if isinstance(t, int) and t == 2:
                    cross_context()
                if isinstance(t, int) and t == 4:
                    clear_cross()

            def between(t):
                if t == 0:
                    dve.wait_ge(v_out, 32 * B)
                    dve.wait_ge(f_const, 8)



            turn, slots = [0], [0]

            def link(ins):
                turn[0] += 1
                ins.then_inc(r_chain, 1)
                dve.wait_ge(r_chain, turn[0])

            def hop(ins):
                slots[0] += 1
                ins.then_inc(s_chain, 1)
                dve.wait_ge(s_chain, slots[0])

            def route(w, piece):
                n, t0 = WAVES[w], T0[w]
                a, g, eq = A[:, 0:n], G[:, 0:n], EQ[:, 0:n]
                m, r_, d_, n_, l_, k_ = mx[:, t0:t0 + n], mr[:, 0:n], den[:, 0:n], num[:, 0:n], lg[:, 0:n], rank[:, 0:n]
                p0, p1 = pick[:, 0, t0:t0 + n], pick[:, 1, t0:t0 + n]
                c0, c1 = cw[:, 0, t0:t0 + n], cw[:, 1, t0:t0 + n]
                bj = lambda t: t.unsqueeze(2).to_broadcast((128, n, 8, 8))
                be = lambda t: t.unsqueeze(3).to_broadcast((128, n, 8, 8))
                if piece == 0:
                    dve.wait_ge(mx_sb, (t0 + n) // 2)
                    link(dve.tensor_tensor(a, be(m[:, :, 0:8]), bj(m[:, :, 8:16]), ALU.mult))
                    link(dve.tensor_reduce(out=r_, in_=a, op=ALU.max, axis=AX.X))
                if piece == 1:
                    link(dve.tensor_tensor(a, a, be(r_), ALU.subtract))
                if piece == 2:
                    dve.wait_ge(r_exp, 2 * w + 1)
                    link(dve.tensor_reduce(out=d_, in_=a, op=ALU.add, axis=AX.X))
                    link(dve.tensor_tensor(a, a, bj(m[:, :, 16:24]), ALU.mult))
                if piece == 3:
                    link(dve.tensor_reduce(out=n_, in_=a, op=ALU.add, axis=AX.X))
                    link(dve.reciprocal(d_, d_))
                    link(dve.tensor_tensor(l_, n_, d_, ALU.mult))
                if piece == 4:
                    link(dve.tensor_tensor(g, bj(l_), be(l_), ALU.is_gt))
                if piece == 5:
                    link(dve.tensor_tensor(eq, bj(l_), be(l_), ALU.is_equal))
                if piece == 6:
                    link(dve.tensor_tensor(eq, eq, LT[:].unsqueeze(1).to_broadcast((128, n, 8, 8)), ALU.mult))
                if piece == 7:
                    link(dve.tensor_tensor(g, g, eq, ALU.add))
                if piece == 8:
                    link(dve.tensor_reduce(out=k_, in_=g, op=ALU.add, axis=AX.X))
                if piece == 9:
                    link(dve.tensor_scalar(p0, k_, 0.5, None, ALU.is_lt))
                    link(dve.tensor_scalar(both[:, t0:t0 + n, :], k_, 1.5, None, ALU.is_lt))
                    link(dve.tensor_scalar(p1, k_, 1.0, None, ALU.is_equal))
                    link(dve.tensor_tensor(n_, p0, l_, ALU.mult))
                    link(dve.tensor_tensor(d_, p1, l_, ALU.mult))
                    link(dve.tensor_reduce(out=c0, in_=n_, op=ALU.add, axis=AX.X))
                    link(dve.tensor_reduce(out=c1, in_=d_, op=ALU.add, axis=AX.X))
                    if w:
                        dve.wait_ge(r_exp, 2)
                    link(dve.tensor_tensor(m0[:, 0:n], c1, c0, ALU.subtract))
                if piece == 10:
                    dve.wait_ge(r_exp, 2 * w + 2)
                    link(dve.tensor_scalar(c0, m0[:, 0:n], 1.0, None, ALU.add))
                    link(dve.reciprocal(c0, c0))
                    link(dve.tensor_tensor(c1, m0[:, 0:n], c0, ALU.mult))
                    assert turn[0] == NCH * (w + 1)

            def place_rows(w):
                n, t0, b0, nb = WAVES[w], T0[w], B0[w], BLOCKS[w]
                dve.wait_ge(r_place_ps, w + 1)
                bank = BK[7]
                tot = bank[:, 8 * n:8 * n + 8]
                hop(dve.tensor_tensor(nb3[:, :, 0:n], tot.unsqueeze(2).to_broadcast((128, 8, n)),
                                      iota128[:, 0:n].unsqueeze(1).to_broadcast((128, 8, n)), ALU.is_gt))
                hop(dve.tensor_reduce(out=nblk[:], in_=nb3[:, :, 0:n], op=ALU.add, axis=AX.X))
                hop(dve.tensor_tensor(ex3[:], LT[:], nblk[:].unsqueeze(1).to_broadcast((128, 8, 8)), ALU.mult))
                hop(dve.tensor_reduce(out=exb[:], in_=ex3[:], op=ALU.add, axis=AX.X))
                hop(dve.tensor_tensor(eb3[:, 0:nb, :], iota[:, 0:nb].unsqueeze(2).to_broadcast((128, nb, 7)),
                                      exb[:, 1:8].unsqueeze(1).to_broadcast((128, nb, 7)), ALU.is_ge))
                hop(dve.tensor_reduce(out=ebf[:, 0:nb], in_=eb3[:, 0:nb, :], op=ALU.add, axis=AX.X))
                hop(dve.tensor_copy(eid[:, b0:b0 + nb], ebf[:, 0:nb]))
                hop(dve.scalar_tensor_tensor(out=place[:, 0:n], in0=exb[:].unsqueeze(1).to_broadcast((128, n, 8)), scalar=128.0,
                                             in1=bank[:, 0:8 * n].rearrange("p (t e) -> p t e", e=8), op0=ALU.mult, op1=ALU.add))
                for k in range(TOP):
                    hop(dve.tensor_tensor(sl3[:, 0:n], place[:, 0:n], pick[:, k, t0:t0 + n], ALU.mult))
                    hop(dve.tensor_reduce(out=slf[:, 0:n], in_=sl3[:, 0:n], op=ALU.add, axis=AX.X))
                    i = dve.tensor_copy(slot_u[:, k, t0:t0 + n], slf[:, 0:n])
                    if k == 0:
                        hop(i)
                i.then_inc(r_slots, 1)

            def take_weights(n, kind, e, part_):
                dve.wait_ge(f_w_ps, n + 1)
                bank = BK[n % 2]
                if kind == "w2":
                    dve.tensor_copy(w2T[:, e, 0:256], bank[:, 0:256])
                    dve.tensor_copy(w2T[0:KF[2], e, 256:384], bank[0:KF[2], 256:384]).then_inc(f_w_sb, 1)
                else:
                    dve.tensor_copy(w1T[:, e, :].rearrange("p (q k) -> p k q", k=8)[:, 4 * part_:4 * part_ + 4, :],
                                    bank[:, 0:4 * W1ROWS].rearrange("p (k q) -> p k q", k=4)).then_inc(f_w_sb, 1)

            def router_x(t):
                dve.wait_ge(rxT_ps, count(t - 4))
                dve.wait_ge(mx_ps, count(t - 5))
                dve.tensor_copy(rxT, AUX[:, 256:512]).then_inc(rxT_sb, 1)

            def step2(t, u, on):
                def normalise(lin, dst):
                    o5 = AUX.rearrange("p (t c x) -> p t c x", t=4, c=4)
                    for c in range(2):
                        for hf in range(2):
                            th = 2 * c + hf
                            i = dve.tensor_tensor(dst[:, c, :].rearrange("p (q f g d) -> p q f g d", q=4, f=2, g=2)[:, :, hf],
                                                  o5[:, th, :, 0:16].rearrange("p q (g d) -> p q g d", g=2),
                                                  lin[:, th, :, :].unsqueeze(3).to_broadcast((128, 4, 2, D)), ALU.mult)
                    return i
                for slot in range(10):
                    if slot == 5 and "SB" in on:
                        b = t - 2
                        dve.wait_ge(c_mT_ps, count(b + 1))
                        dve.wait_ge(c_m_in, count(b * 64))
                        dve.tensor_scalar(mT[:, 0, :], AUX[0:4 * H, 0:128], -1.0, None, ALU.mult).then_inc(c_mT_sb, 1)
                        dve.wait_ge(c_mT_sb, count(b * 2 + 1))
                        dve.scalar_tensor_tensor(out=mT[:, 1, :], in0=AUX[0:4 * H, 0:128], scalar=-1.0, in1=mT[:, 0, :],
                                                 op0=ALU.mult, op1=ALU.subtract).then_inc(c_mT_sb, 1)
                    if slot in S2_SLOTS and S2_SLOTS[slot][0] in on:
                        stage, n0, n1 = S2_SLOTS[slot]
                        b = t - LAG[stage]
                        if n0 == 0:
                            dve.wait_ge(c_mT_ps, count(b))
                        for n in range(n0, n1):
                            dve.wait_ge(c_s_ps, count(b * 20 + (n + 1)))
                            if n < 16:
                                dve.tensor_reduce(out=M2[:, 2 * n:2 * n + 1], in_=Sps[n % 2][:, 0:128], op=ALU.max, axis=AX.X)
                                i = dve.tensor_reduce(out=M2[:, 2 * n + 1:2 * n + 2], in_=Sps[n % 2][:, 128:384], op=ALU.max, axis=AX.X)
                            else:
                                c = 32 + 8 * (n - 16)
                                i = dve.tensor_reduce(out=M2[:, c:c + 8], in_=Sps[n % 2].rearrange("p (g k) -> p g k", k=TK), op=ALU.max, axis=AX.X)
                            i.then_inc(c_max_sb, 1)
                    if slot == 0 and "P" in on:
                        dve.wait_ge(c_xT_ps, count(t + 1))
                        dve.wait_ge(c_qv_ps, count(t))
                        dve.tensor_copy(xT[:], AUX[:, 0:256]).then_inc(c_xT_sb, 1)
                    if slot == 3 and "P" in on:
                        dve.wait_ge(c_qv_ps, count(t + 1))
                        dve.wait_ge(c_vp_sb, count(t * 2))
                        dve.wait_ge(c_qc_sb, count(t + 1))
                        dve.tensor_tensor(vsb[:], AUX[:, 256:512].rearrange("p (c f) -> p c f", c=2),
                                          bvx[:].unsqueeze(1).to_broadcast((128, 2, C)), ALU.add).then_inc(c_v_sb, 1)
                    if slot == 5 and "E" in on:
                        b = t - 4
                        dve.wait_ge(c_oTs_ps, count(b + 1))
                        dve.reciprocal(linv[:], AUX.rearrange("p (t c x) -> p t c x", t=4, c=4)[:, :, :, 16:18]).then_inc(c_lin_sb, 1)
                        dve.wait_ge(c_lin_sb, count(b * 2 + 1))
                        dve.wait_ge(c_ctxT_ps, count(b))
                        normalise(linv, ctx).then_inc(c_ctx_sb, 1)
                    if slot == 6 and "E" in on:
                        b = t - 4
                        dve.wait_ge(c_oTx_ps, count(b + 1))
                        dve.reciprocal(linx[:], AUX.rearrange("p (t c x) -> p t c x", t=4, c=4)[:, :, :, 16:18]).then_inc(c_lin_sb, 1)
                        dve.wait_ge(c_lin_sb, count(b * 2 + 2))
                        normalise(linx, ctx2).then_inc(c_ctx2_sb, 1)
                        dve.wait_ge(c_ctx2_sb, count(b * 2 + 1))
                        dve.tensor_tensor(ctx[:], ctx[:], ctx2[:], ALU.add).then_inc(c_ctx2_sb, 1)
                    if slot == 8 and "E" in on:
                        b = t - 4
                        dve.wait_ge(c_y_ps, count(b + 1))
                        if "R" in on:
                            dve.wait_ge(rxT_ps, count(t - 4))
                        dve.wait_ge(c_xb_sb, count(b + 1))
                        dve.wait_ge(x2_sb, count(b * 2))
                        dve.tensor_tensor(r[:], AUX[:, 0:256].rearrange("p (c f) -> p c f", c=2), xb[:], ALU.add).then_inc(c_r_sb, 1)
                        dve.wait_ge(c_r_sb, count(b + 1))
                        if "R" in on:
                            router_x(t)
                        dve.wait_ge(c_mv_sb, count(b * 2))
                        for c in range(2):
                            dve.bn_stats(st[:, c, :], r[:, c, :]).then_inc(c_st_sb, 1)
                        dve.wait_ge(c_st_sb, count(b * 2 + 2))
                        settle(dve)
                        for c in range(2):
                            dve.bn_aggr(mv[:, c, :], st[:, c, :]).then_inc(c_mv_sb, 1)
                    if slot == 8 and "R" in on and "E" not in on:
                        router_x(t)
                    if slot == 9 and "E" in on:
                        b = t - 4
                        dve.wait_ge(c_rstd_sb, count(b + 1))
                        for c in range(2):
                            dve.tensor_scalar(X[:, b * 2 + c, :], r[:, c, :], mv[:, c, 0:1], rstd[:, c:c + 1],
                                              ALU.subtract, ALU.mult).then_inc(x2_sb, 1)
                    if isinstance(t, int):
                        if (t, slot) in ROUTE:
                            route(0, ROUTE.index((t, slot)))
                        if (t, slot) == (15, 4):
                            place_rows(0)
                        for n, unit in enumerate(UNITS):
                            if unit[0] == (t, slot):
                                if n == 0:
                                    dve.wait_ge(c_parts_out, 16 * B)
                                    dve.wait_ge(c_split, 4 * B)
                                if n == 8:
                                    dve.wait_ge(c_st_ps, 10 * (B - 1))
                                if n == 16:
                                    dve.wait_ge(c_st_ps, 10 * B)
                                take_weights(n, *unit[1:])
            run(dve, step, step2, between)
            dve.wait_ge(r_slots, 1)
            def combine(k):
                dve.wait_ge(g_in[k % 8], 64 * (k // 8 + 1))
                if k >= 2:
                    dve.wait_ge(g_yo, 2 * k - 2)
                    dve.wait_ge(g_mv, 2 * k)
                a = acc[k % 2]
                for t in range(2):
                    dve.scalar_tensor_tensor(out=a[:, t, :], in0=gat[k][:, 0, t, :], scalar=cw[:, 0, 2 * k + t:2 * k + t + 1],
                                             in1=X[:, 2 * k + t, :], op0=ALU.mult, op1=ALU.add).then_inc(g_half, 1)
                dve.wait_ge(g_half, 2 * k + 2)
                for t in range(2):
                    dve.scalar_tensor_tensor(out=a[:, t, :], in0=gat[k][:, 1, t, :], scalar=cw[:, 1, 2 * k + t:2 * k + t + 1],
                                             in1=a[:, t, :], op0=ALU.mult, op1=ALU.add).then_inc(g_acc, 1)
                dve.wait_ge(g_acc, 2 * k + 2)
                for t in range(2):
                    dve.bn_stats(st4[:, t, :], a[:, t, :]).then_inc(g_st, 1)
                dve.wait_ge(g_st, 2 * k + 2)
                for t in range(2):
                    dve.bn_aggr(mv4[k % 2][:, t, :], st4[:, t, :]).then_inc(g_mv, 1)

            def finish(k):
                dve.wait_ge(g_rs, k + 1)
                if k >= 2:
                    dve.wait_ge(g_out[k % 2], 16 * (k // 2))
                for t in range(2):
                    dve.tensor_scalar(yo[k % 2][:, t, :], acc[k % 2][:, t, :], mv4[k % 2][:, t, 0:1], rs4[k % 2][:, t:t + 1],
                                      ALU.subtract, ALU.mult).then_inc(g_yo, 1)

            def copy_xT(g, p):
                dve.wait_ge(b_xT_ps, count(g + 1))
                dve.wait_ge(b_h_ps, count(g * 4 - 4))
                dve.tensor_copy(xbT[p][:].rearrange("p a b -> p (a b)"), BK[7]).then_inc(b_xT_sb, 1)

            def copy_y(j, u, h, p):
                dve.wait_ge(b_y_ps, count(j + 1))
                if u == 0:
                    dve.wait_ge(b_y_out[p], count(h * 16))
                dve.tensor_copy(ysb[p][:, u, :], BK[6][:, 0:128]).then_inc(b_y_sb, 1)

            def step(g, h, p, more=True):
                for u in range(4):
                    j = g * 4 + u
                    dve.wait_ge(b_sa, count(j + 1))
                    dve.wait_ge(b_heT_ps, count(j - 1))
                    dve.tensor_tensor(he[u % 2][:], sa[u % 2][:], BK[2 + u % 2][:, 0:FF], ALU.mult).then_inc(b_he, 1)
                    if u >= 2:
                        copy_y(j - 2, u - 2, h, p)
                    elif not (isinstance(j, int) and j < 2):
                        copy_y(j - 2, u + 2, h, 1 - p)
                    if u == 1 and more:
                        copy_xT(g + 1, 1 - p)
                    if isinstance(g, int) and (g, u) == (0, 2):
                        dve.wait_ge(rxT_ps, B)
                        dve.wait_ge(mx_ps, B - 1)
                        dve.tensor_copy(rxT, AUX[:, 256:512]).then_inc(rxT_sb, 1)
                    if isinstance(g, int) and g < 4:
                        for piece in ROUTE1.get((g, u), ()):
                            route(1, piece)
                        if (g, u) == (3, 3):
                            place_rows(1)
                    if isinstance(g, int) and g >= NG - 5:
                        k = 2 * (g - (NG - 5)) + u // 2
                        if u % 2 == 0 and k < WAVES[0] // 2:
                            combine(k)
                        if u % 2 == 1 and 0 < k <= WAVES[0] // 2:
                            finish(k - 1)
            copy_xT(0, 0)
            for g in range(4):
                step(g, g // 2, g % 2)
            span(dve, 4, NG - 5, step)
            for g in range(NG - 5, NG - 1):
                step(g, g // 2, g % 2)
            step(NG - 1, NG // 2 - 1, 1, more=False)
            copy_y(NBK - 2, 2, 0, 1)
            copy_y(NBK - 1, 3, 0, 1)

            for k in range(WAVES[0] // 2, NK):
                combine(k)
                if k > WAVES[0] // 2:
                    finish(k - 1)
            finish(NK - 1)

        @block.gpsimd
        def _(pool):
            pool.memset(ident[:], 0.0).then_inc(ident_ok, 1)
            pool.wait_ge(ident_ok, 1)
            pool.affine_select(out=ident[:], in_=ident[:], compare_op=ALU.not_equal, fill=1.0, base=0, pattern=[[-1, 128]],
                               channel_multiplier=1).then_inc(ident_ok, 1)

            def clear(k):
                pool.memset(Qs[k][0:96, :].bitcast(F32), 0.0).then_inc(zero_ok[k], 1)
                pool.memset(Vp[k][:], 0.0).then_inc(vp_ok[k], 1)
                pool.wait_ge(vp_ok[k], 1)
                v = Vp[k][:].rearrange("p t (m g) x -> p (t m) g x", g=2)
                for g in range(2):
                    pool.memset(v[:, :, g, 16 + g:17 + g], 1.0).then_inc(vp_ok[k], 1)

            def clear_cross():
                for k in range(NBUF):
                    pool.memset(Qcs[k][0:96, :].bitcast(F32), 0.0).then_inc(zeroc_ok, 1)
                    pool.memset(Kcs[k][0:96, :], 0.0).then_inc(zeroc_ok, 1)
                    pool.memset(VCp[k][:], 0.0).then_inc(vcp_ok, 1)

            def masks():
                pool.wait_ge(ident_ok, 2)
                pool.memset(maskq[:], 0.0).then_inc(mask_ok, 1)
                pool.memset(maskk[:], 0.0).then_inc(mask_ok, 1)
                pool.wait_ge(mask_ok, 2)
                for m, sign in ((maskq, 1), (maskk, -1)):
                    pool.affine_select(out=m[:], in_=m[:], compare_op=ALU.is_ge, fill=-1e38, base=0, pattern=[[-sign, 128]],
                                       channel_multiplier=sign).then_inc(mask_ok, 1)
                pool.tensor_copy(identb[:], ident[:]).then_inc(mask_ok, 1)
                pool.memset(half[:], -0.5).then_inc(mask_ok, 1)

            def constants():
                pool.memset(onesb[:], 1.0).then_inc(f_const, 1)
                pool.memset(trib[:], 1.0).then_inc(f_const, 1)
                pool.memset(LT[:], 1.0).then_inc(f_const, 1)
                pool.iota(iota_i[:], [[1, 64]], base=0, channel_multiplier=0).then_inc(f_const, 1)
                pool.wait_ge(f_const, 4)
                pool.affine_select(out=trib[:], in_=trib[:], compare_op=ALU.is_ge, fill=0.0, base=-1, pattern=[[1, 128]],
                                   channel_multiplier=-1).then_inc(f_const, 1)
                pool.affine_select(out=LT[:], in_=LT[:], compare_op=ALU.is_ge, fill=0.0, base=-1, pattern=[[1, 8], [-1, 8]],
                                   channel_multiplier=0).then_inc(f_const, 1)
                pool.tensor_copy(iota[:], iota_i[:]).then_inc(f_const, 1)
                pool.wait_ge(f_const, 7)
                pool.tensor_scalar(iota128[:], iota[:, 0:32], 128.0, None, ALU.mult).then_inc(f_const, 1)
            clear(0)
            pool.wait_ge(cA_in, 64)

            def step(t, u, on):
                if "E" in on:
                    b = t - 4
                    pool.wait_ge(r_sb, count(b))
                    pool.tensor_tensor(xb[:], X[:, bass.ds(b * 2, 2), :] if not isinstance(b, int) else X[:, 2 * b:2 * b + 2, :],
                                       boA[:].unsqueeze(1).to_broadcast((128, 2, C)), ALU.add).then_inc(xb_sb, 1)
                if "P" in on:
                    pool.wait_ge(qk_sb, count(t * 2 + 2))
                    pool.wait_ge(parts_out, count(t * 16))
                    settle(pool)
                    pool.tensor_copy(parts[:, 0:6:3, :], qk32[:]).then_inc(split, 1)
                    pool.wait_ge(split, count(t * 4 + 1))
                    pool.tensor_tensor(res[:], qk32[:], parts[:, 0:6:3, :], ALU.subtract).then_inc(split, 1)
                    pool.wait_ge(split, count(t * 4 + 2))
                    settle(pool)
                    pool.tensor_copy(parts[:, 1:6:3, :], res[:]).then_inc(split, 1)
                    pool.wait_ge(split, count(t * 4 + 3))
                    pool.tensor_tensor(parts[:, 2:6:3, :], res[:], parts[:, 1:6:3, :], ALU.subtract).then_inc(split, 1)
                if "E" in on:
                    b = t - 4
                    pool.wait_ge(mv_sb, count(b * 2 + 2))
                    pool.wait_ge(rstd_sb, count(b))
                    settle(pool)
                    pool.tensor_scalar(ve[:], mv[:, :, 1], EPS, None, ALU.add).then_inc(ve_sb, 1)
                    pool.wait_ge(ve_sb, count(b + 1))
                    pool.wait_ge(x1_sb, count(b * 2))
                    pool.tensor_tensor(rstd[:], ve[:], half[:], ALU.pow).then_inc(rstd_sb, 1)
                if isinstance(t, int) and t in (1, 2):
                    clear(t)
                if isinstance(t, int) and t == 2:
                    masks()
                if isinstance(t, int) and t == 3:
                    clear_cross()
                if isinstance(t, int) and t == B - 2:
                    constants()
                if isinstance(t, int) and t == 3:
                    for i in range(4):
                        pool.wait_ge(x_in[i], 16)

            SENT0 = {(15, 1): (0, 5), (16, 0): (5, 9), (16, 1): (9, 16), (17, 0): (16, 21), (17, 1): (21, 26), (18, 0): (26, 31), (18, 1): (31, 36)}

            def send(w, lo, hi):
                for n in range(lo, hi):
                    t, k = T0[w] + n // TOP, n % TOP
                    pool.indirect_dma_start(xs[w], bass.IndirectOffsetOnAxis(ap=slot_u[:, k, t:t + 1], axis=0), X[:, t, :], None).then_inc(x_sent[w], 16)

            def step2(t, u, on):
                if "P" in on:
                    pool.wait_ge(x1_sb, count(t * 2 + 2)) if isinstance(t, int) else None
                    pool.wait_ge(c_xT_ps, count(t))
                    settle(pool)
                    src = X[:, 2 * t:2 * t + 2, :] if isinstance(t, int) else X[:, bass.ds(t * 2, 2), :]
                    pool.tensor_copy(x2in[:], src).then_inc(c_x2in, 1)
                if "E" in on:
                    b = t - 4
                    pool.wait_ge(c_r_sb, count(b))
                    pool.tensor_tensor(xb[:], X[:, bass.ds(b * 2, 2), :] if not isinstance(b, int) else X[:, 2 * b:2 * b + 2, :],
                                       bpx[:].unsqueeze(1).to_broadcast((128, 2, C)), ALU.add).then_inc(c_xb_sb, 1)
                if "L" in on:
                    b = t - 1
                    pool.wait_ge(c_v_sb, count(b + 1))
                    pool.wait_ge(c_pv_ps, count(b * 6 - 12))
                    settle(pool)
                    vd = Vp[(u - 1) % 3][:].rearrange("p t (m g) x -> p (t m) g x", g=2)
                    vs = vsb[:].rearrange("p t (m g d) -> p (t m) g d", g=2, d=D)
                    for g in range(2):
                        pool.tensor_copy(vd[:, :, g, 8 * g:8 * g + 8], vs[:, :, g, :]).then_inc(c_vp_sb, 1)
                if "P" in on:
                    p3 = parts3[:].rearrange("p (g a) t -> p g a t", a=3)
                    pool.wait_ge(c_qk_sb, count(t * 2 + 2))
                    pool.wait_ge(c_qc_sb, count(t + 1))
                    pool.wait_ge(c_parts_out, count(t * 16))
                    settle(pool)
                    pool.tensor_copy(p3[:, :, 0, :], qkc32[:]).then_inc(c_split, 1)
                    pool.wait_ge(c_split, count(t * 4 + 1))
                    pool.tensor_tensor(res3[:], qkc32[:], p3[:, :, 0, :], ALU.subtract).then_inc(c_split, 1)
                    pool.wait_ge(c_split, count(t * 4 + 2))
                    settle(pool)
                    pool.tensor_copy(p3[:, :, 1, :], res3[:]).then_inc(c_split, 1)
                    pool.wait_ge(c_split, count(t * 4 + 3))
                    pool.tensor_tensor(p3[:, :, 2, :], res3[:], p3[:, :, 1, :], ALU.subtract).then_inc(c_split, 1)
                if isinstance(t, int) and (t, 0) in SENT0:
                    send(0, *SENT0[t, 0])
                if "E" in on:
                    b = t - 4
                    pool.wait_ge(c_mv_sb, count(b * 2 + 2))
                    pool.wait_ge(c_rstd_sb, count(b))
                    settle(pool)
                    pool.tensor_scalar(ve[:], mv[:, :, 1], EPS, None, ALU.add).then_inc(c_ve_sb, 1)
                    pool.wait_ge(c_ve_sb, count(b + 1))
                    pool.wait_ge(x2_sb, count(b * 2))
                    pool.tensor_tensor(rstd[:], ve[:], half[:], ALU.pow).then_inc(c_rstd_sb, 1)
                if isinstance(t, int) and (t, 1) in SENT0:
                    if t == 15:
                        pool.wait_ge(r_slots, 1)
                        pool.wait_ge(zeroed, 16 * len(ZEROS))
                    send(0, *SENT0[t, 1])

            def between(t):
                if t == 0:
                    pool.wait_ge(cx_in, 144)
                if 1 <= t <= 3:
                    pool.wait_ge(pv_ps, 4 * (B - 3 + t))
                if t == 3:
                    pool.wait_ge(x1_sb, 2 * B)
            run(pool, step, step2, between)
            pool.wait_ge(r_slots, 2)
            send(1, 0, TOP * WAVES[1])
            def norm(k):
                pool.wait_ge(g_mv, 2 * k + 2)
                if k:
                    pool.wait_ge(g_rs, k)
                pool.tensor_scalar(ve4[:], mv4[k % 2][:, :, 1], EPS, None, ALU.add).then_inc(g_ve, 1)
                pool.wait_ge(g_ve, k + 1)
                if k >= 2:
                    pool.wait_ge(g_yo, 2 * k - 2)
                pool.tensor_tensor(rs4[k % 2][:], ve4[:], half[:], ALU.pow).then_inc(g_rs, 1)

            def gather(k):
                w = int(2 * k >= T0[1])
                last = GW0 if w == 0 else NG
                pool.wait_ge(b_y_out[0], 16 * ((last + 1) // 2))
                pool.wait_ge(b_y_out[1], 16 * (last // 2))
                if k >= 8:
                    pool.wait_ge(g_acc, 2 * (k - 8) + 2)
                for t in range(2):
                    for r_ in range(TOP):
                        pool.indirect_dma_start(gat[k][:, r_, t, :], None, ys[w],
                                                bass.IndirectOffsetOnAxis(ap=slot_u[:, r_, 2 * k + t:2 * k + t + 1], axis=0)).then_inc(g_in[k % 8], 16)
            NK0 = WAVES[0] // 2
            for k in range(NK0):
                gather(k)
            for k in range(NK0):
                norm(k)
            for k in range(NK0, NK):
                gather(k)
                if k >= NK0 + 2:
                    norm(k - 2)
            norm(NK - 2)
            norm(NK - 1)

        @block.sync
        def _(sp):
            xv = x.rearrange("b (c p) f -> p (b c) f", p=128)
            sp.dma_start(WnatA[:, 0:3, :], aW.rearrange("(c p) e -> p c e", p=128)).then_inc(wA_in, 16)
            sp.dma_start(WnatA[:, 3, :], aWo).then_inc(wA_in, 16)
            bx = ab.rearrange("(j x) -> x j", x=24)
            for a in range(2):
                sp.dma_start(bqkA[:, a:a + 1], bx[8 * a:8 * a + 8, :], allow_slow_non_contiguous=True).then_inc(cA_in, 16)
            sp.dma_start(bvA[:].rearrange("p (j d) -> p j d", d=8), ab.rearrange("(j x) -> j x", x=24)[:, 16:24].unsqueeze(0).to_broadcast((128, 16, 8))).then_inc(cA_in, 16)
            sp.dma_start(boA[:], abo.unsqueeze(0).to_broadcast((128, C))).then_inc(cA_in, 16)
            rows1 = scr_qk.rearrange("a (d j) t -> (a d) (j t)", d=8)

            def clear_rows(lo, hi):
                for w, b0, b1 in ZEROS[lo:hi]:
                    sp.dma_start(xs[w].rearrange("(b p) f -> p b f", p=128)[:, b0:b1, :],
                                 zrow[:].unsqueeze(1).to_broadcast((128, b1 - b0, C))).then_inc(zeroed, 16)

            def step(t, u, on):
                if "P" in on:
                    sp.wait_ge(xT_ps, count(t - 2))
                    settle(sp)
                    sp.wait_ge(xin_in, count(t * 16))
                    settle(sp)
                    settle(sp)
                    sp.dma_start(xin[u][:], (x[t] if isinstance(t, int) else x[bass.ds(t, 1)].rearrange("o n f -> (o n) f")).rearrange("(c p) f -> p c f", p=128)).then_inc(xin_in, 16)
                if isinstance(t, int) and t == 0:
                    for n, name in enumerate(("Wq", "Wk", "Wcq", "Wv", "Wp")):
                        sp.dma_start(Wx[:, n, :], W[name]).then_inc(wx_in, 16)
                    sp.dma_start(cin, ctx_in.rearrange("(n u) t c -> (u t) n c", u=2)).then_inc(cin_in, 16)
                    sp.dma_start(Wckr[:, 0, :], W["Wck"]).then_inc(cx_in, 16)
                    sp.dma_start(Wckr[:, 1, :], W["Wcv"]).then_inc(cx_in, 16)
                    for n, name in enumerate(("bq", "bk", "bcq", "bck")):
                        sp.dma_start(bx3[:, n:n + 1], W[name].rearrange("(h d) -> d h", d=D), allow_slow_non_contiguous=True).then_inc(cx_in, 16)
                    for tile, name in ((bvx, "bv"), (bcvx, "bcv"), (bpx, "bp")):
                        sp.dma_start(tile[:], W[name].unsqueeze(0).to_broadcast((128, C))).then_inc(cx_in, 16)
                    sp.dma_start(wrr[:], rwqkv).then_inc(f_wr_in, 16)
                if "L" in on:
                    b = t - 1
                    k = (u - 1) % 3
                    sp.wait_ge(parts_out, count(b * 16 + 16))
                    settle(sp)
                    sp.wait_ge(v_out, count(b * 32 + 32))
                    settle(sp)
                    sp.wait_ge(stacks_in, count(b * 96))
                    settle(sp)
                    sp.wait_ge(v_in, count(b * 64))
                    settle(sp)
                    sp.wait_ge(st_ps, count(b * 8 - 16))
                    settle(sp)
                    if isinstance(b, int) and b < NBUF:
                        sp.wait_ge(zero_ok[k], 4)
                    for n, o in ((3, 0), (2, 24), (1, 40)):
                        sp.dma_start(Qs[k][o:o + 8 * n, :], rows1[0:8 * n, :]).then_inc(stacks_in, 16)
                        a = (3 - n) * 8 + 24
                        sp.dma_start(Ks[k][o:o + 8 * n, :], rows1[a:a + 8, :].unsqueeze(0).to_broadcast((n, 8, H * T))).then_inc(stacks_in, 16)
                    sp.wait_ge(pv_ps, count(b * 4 - 8))
                    settle(sp)
                    if isinstance(b, int) and b < NBUF:
                        sp.wait_ge(vp_ok[k], 3)
                    vr = scr_v.rearrange("(kt j) (i m g) d -> kt g (j i) m d", kt=2, i=16, g=2)
                    for kt in range(2):
                        for g in range(2):
                            dst = Vp[k][:, kt, :, :].rearrange("p (m g) x -> p m g x", g=2)[:, :, g, 8 * g:8 * g + 8]
                            sp.dma_start(dst, vr[kt, g]).then_inc(v_in, 16)
                if "P" in on:
                    sp.wait_ge(v_sb, count(t + 1))
                    settle(sp)
                    sp.wait_ge(v_in, count(t * 64))
                    settle(sp)
                    for c in range(2):
                        sp.dma_start(scr_v[:, 128 * c:128 * c + 128, :].rearrange("j p d -> p j d"),
                                     vsb[:, c, :].rearrange("p (j d) -> p j d", d=8)).then_inc(v_out, 16)
                if "SB" in on:
                    b = t - 2
                    k = (u - 2) % 3
                    sp.wait_ge(mb_sb, count(b * 2 + 2))
                    settle(sp)
                    sp.wait_ge(m_in, count(b * 64))
                    settle(sp)
                    for c in range(2):
                        for f in range(2):
                            sp.dma_start(Qs[k][MROW + c:MROW + c + 1, 2048 * f:2048 * f + 2048].rearrange("o (q h) -> o q h", h=H),
                                         Mb[:, c, 16 * f:16 * f + 16]).then_inc(m_in, 16)
                if "P" in on:
                    sp.wait_ge(split, count(t * 4 + 4))
                    settle(sp)
                    sp.wait_ge(stacks_in, count(t * 96))
                    settle(sp)
                    sp.dma_start(scr_qk.rearrange("a p t -> p a t"), parts[:]).then_inc(parts_out, 16)
                if isinstance(t, int) and t == 1:
                    for i in range(4):
                        n = B * NT // 4
                        sp.dma_start(X[:, n * i:n * i + n, :], xv[:, n * i:n * i + n, :]).then_inc(x_in[i], 16)
                if isinstance(t, int) and t == 3:
                    sp.wait_ge(kc_split, 5)
                    for a in range(3):
                        sp.dma_start(scr_kc[a].rearrange("b p t -> p b t"), kcp[:, a, :].rearrange("p (b t) -> p b t", t=TK)).then_inc(kc_out, 16)
                    sp.wait_ge(vc_sb, 1)
                    sp.dma_start(scr_vc.rearrange("(n p) c -> p n c", p=128), vc32.rearrange("p (n c) -> p n c", c=C)).then_inc(vc_out, 16)
            rows2 = scr_qkc.rearrange("a (d h) t -> (a d) (h t)", d=D)

            def step2(t, u, on):
                if "L" in on:
                    b = t - 1
                    k = (u - 1) % 3
                    sp.wait_ge(c_parts_out, count(b * 16 + 16))
                    settle(sp)
                    sp.wait_ge(c_stacks_in, count(b * 224))
                    settle(sp)
                    sp.wait_ge(c_st_ps, count(b * 10 - 20))
                    settle(sp)
                    for n, o in ((3, 0), (2, 24), (1, 40)):
                        sp.dma_start(Qs[k][o:o + 8 * n, :], rows2[0:8 * n, :]).then_inc(c_stacks_in, 16)
                        sp.dma_start(Qcs[k][o:o + 8 * n, :], rows2[48:48 + 8 * n, :]).then_inc(c_stacks_in, 16)
                        a = (3 - n) * 8 + 24
                        sp.dma_start(Ks[k][o:o + 8 * n, :], rows2[a:a + 8, :].unsqueeze(0).to_broadcast((n, 8, H * T))).then_inc(c_stacks_in, 16)
                        kb = (scr_kc[3 - n][b] if isinstance(b, int) else scr_kc[3 - n][bass.ds(b, 1)].rearrange("o p t -> (o p) t")).rearrange("(d h) t -> d (h t)", d=D)
                        sp.dma_start(Kcs[k][o:o + 8 * n, :], kb.unsqueeze(0).to_broadcast((n, 8, H * TK))).then_inc(c_stacks_in, 16)
                    sp.wait_ge(c_pv_ps, count(b * 6 - 12))
                    settle(sp)
                    vb = scr_vc[bass.ds(b * TK, TK)] if not isinstance(b, int) else scr_vc[b * TK:b * TK + TK]
                    vb = vb.rearrange("t (m g d) -> g t m d", g=2, d=D)
                    for g in range(2):
                        sp.dma_start(VCp[k][64 * g:64 * g + 64, :, 8 * g:8 * g + 8], vb[g]).then_inc(c_stacks_in, 16)
                if "SB" in on:
                    b = t - 2
                    k = (u - 2) % 3
                    sp.wait_ge(c_mT_sb, count(b * 2 + 2))
                    settle(sp)
                    sp.wait_ge(c_m_in, count(b * 64))
                    settle(sp)
                    for c in range(2):
                        for stack, o in ((Qs, 0), (Qcs, 2 * H)):
                            sp.dma_start(stack[k][MROW + c:MROW + c + 1, :].rearrange("o (r q) -> o r q", q=128),
                                         mT[o:o + 2 * H, c, :]).then_inc(c_m_in, 16)
                if "P" in on:
                    sp.wait_ge(c_split, count(t * 4 + 4))
                    settle(sp)
                    sp.wait_ge(c_stacks_in, count(t * 224))
                    settle(sp)
                    sp.dma_start(scr_qkc.rearrange("a p t -> p a t"), parts3[:]).then_inc(c_parts_out, 16)
                if isinstance(t, int) and 4 <= t < 8:
                    sp.wait_ge(f_zero, 1)
                    clear_rows(t - 4, t - 3)
                if isinstance(t, int) and t == B - 2:
                    clear_rows(4, len(ZEROS))
                if isinstance(t, int) and t in (17, 18):
                    sp.wait_ge(c_st_ps, 10 * (B - 2) if t == 17 else 10 * (B - 1))
                    for n, e0, ne in (((1, 6, 2), (2, 0, 2)) if t == 17 else ((3, 2, 2), (4, 4, 2))):
                        st_, o = W1R[e0]
                        sp.dma_start(f32(st_[:])[0:W1ROWS, o:o + 1024 * ne].rearrange("p (e x) -> p e x", e=ne),
                                     w1[e0:e0 + ne].rearrange("e (p k) c -> p e (k c)", k=8)).then_inc(f_w1_in[n - 1], 16)

            def between(t):
                if t == 1:
                    sp.wait_ge(zeroc_ok, 3 * NBUF)
                    sp.wait_ge(vcp_ok, 3 * NBUF)
                    sp.wait_ge(kc_out, 48)
                    sp.wait_ge(vc_out, 16)
                if 1 <= t <= 3:
                    sp.wait_ge(st_ps, 8 * (B - 3 + t))
                    sp.wait_ge(pv_ps, 4 * (B - 3 + t))
                if t == 4:
                    for i in range(2):
                        sp.dma_start(w2r[:, 4 * i:4 * i + 4, :], w2[4 * i:4 * i + 4].rearrange("e c f -> c e f")).then_inc(f_w2_in, 16)
            run(sp, step, step2, between)
            def rows(t, g):
                a = t.rearrange("(g b p) f -> g p b f", b=4, p=128)
                return a[g] if isinstance(g, int) else a[bass.ds(g, 1)].rearrange("o p b f -> (o p) b f")

            def load(g, p, w):
                sp.wait_ge(b_xT_ps, count(g - 1)) if not isinstance(g, int) or g >= 2 else None
                settle(sp)
                sp.dma_start(xblk[p][:], rows(xs[w], g - w * GW0)).then_inc(b_x_in[p], 16)

            def store(g, p, w):
                sp.wait_ge(b_y_sb, count(g * 4 + 4))
                settle(sp)
                sp.dma_start(rows(ys[w], g - w * GW0), ysb[p][:]).then_inc(b_y_out[p], 16)
            sp.wait_ge(x_sent[0], 16 * TOP * WAVES[0])
            sp.wait_ge(c_pv_ps, 6 * B)
            load(0, 0, 0)
            load(1, 1, 0)

            def deliver(k):
                sp.wait_ge(g_yo, 2 * k + 2)
                sp.dma_start(out[k].rearrange("(c p) f -> p c f", p=128), yo[k % 2]).then_inc(g_out[k % 2], 16)

            def step(lw, sw):
                def _(g, h, p):
                    if lw is not None:
                        load(g + 2, p, lw)
                    if isinstance(g, int) and g >= NG - 5:
                        for k in (2 * (g - (NG - 5)) - 1, 2 * (g - (NG - 5))):
                            if 0 <= k < WAVES[0] // 2:
                                deliver(k)
                    store(g, p, sw)
                return _
            span(sp, 0, GW0 - 2, step(0, 0))
            sp.wait_ge(x_sent[1], 16 * TOP * WAVES[1])
            span(sp, GW0 - 2, GW0, step(1, 0))
            span(sp, GW0, NG - 5, step(1, 1))
            for g in range(NG - 5, NG):
                step(1 if g < NG - 2 else None, 1)(g, g // 2, g % 2)
            for k in range(WAVES[0] // 2, NK):
                deliver(k)
            for o in g_out:
                sp.wait_ge(o, 16 * (NK // 2))



def kernel(**inputs):
    import concourse.bacc as bacc
    from concourse.bass_utils import run_bass_kernel_spmd
    nc = bacc.Bacc("TRN2", target_bir_lowering=False, num_devices=1)
    arrays, a = {}, {}
    for name, value in inputs.items():
        arrays[name] = np.ascontiguousarray(value)
        a[name] = nc.dram_tensor(name, arrays[name].shape, mybir.dt.from_np(arrays[name].dtype), kind="ExternalInput").ap()
    out = nc.dram_tensor("out", arrays["x"].shape, F32, kind="ExternalOutput").ap()
    cross = {k.removeprefix("L0_xattn_"): v for k, v in a.items() if k.startswith("L0_xattn_")}
    decoder_layer(nc, a["x"], a["ctx_512"], a["L0_attn_W_qkv"], a["L0_attn_b_qkv"], a["L0_attn_W_out"], a["L0_attn_b_out"],
                  cross, a["L0_ffn_wqkv"], a["L0_ffn_w1"], a["L0_ffn_w2"], out)
    return run_bass_kernel_spmd(nc, [arrays], core_ids=[0]).results[0]["out"]
```
